# Optimizing a Trainium2 kernel written in Bass

```python
import numpy as np
import jax
import jax.numpy as jnp

def _softmax(x, axis=-1):
    return jax.nn.softmax(x, axis=axis)

def _gelu(x):
    return jax.nn.gelu(x, approximate=True)

def _silu(x):
    return jax.nn.silu(x)

def _sigmoid(x):
    return jax.nn.sigmoid(x)

def _layernorm(x, axis=-1, eps=1e-05):
    m = jnp.mean(x, axis=axis, keepdims=True)
    v = jnp.var(x, axis=axis, keepdims=True)
    return (x - m) / jnp.sqrt(v + eps)

def _scatter_add(tgt, idx, src, axis=0):
    return tgt.at[idx].add(src)

def _segment_sum(src, seg, n):
    return jax.ops.segment_sum(src, seg, n)
kernel_name = 'mk_flamingo_gated_d4_seqx_r8_d86fb1'

def setup_inputs(seed: int=0):
    np.random.seed(seed)
    _w = jnp.asarray

    def _rec_inputs():
        import jax
        import jax.numpy as jnp
        _rk = jax.random.key(seed)
        x = -0.0005857 + 0.9999 * jax.random.normal(jax.random.fold_in(_rk, 1), (1, 1024, 128), jnp.float32)
        _lenS = 1024 - jax.random.randint(jax.random.fold_in(_rk, 7), (1,), 0, max(1, 1024 // 4) + 1, jnp.int32)
        _lenS2 = 6404 - jax.random.randint(jax.random.fold_in(_rk, 8), (1,), 0, max(1, 6404 // 4) + 1, jnp.int32)
        _ctx_1024P = jax.random.normal(jax.random.fold_in(_rk, 11), (1, 16, 128), jnp.float32)
        _ctx_1024c = jax.random.dirichlet(jax.random.fold_in(_rk, 511), 0.3 * jnp.ones((16,), jnp.float32), (1, 6404))
        _ctx_1024t = jnp.einsum('bsk,bkd->bsd', _ctx_1024c, _ctx_1024P)
        _ctx_1024t = _ctx_1024t * jax.lax.rsqrt(jnp.mean(jnp.square(_ctx_1024t)) + 1e-12) * 0.953939
        ctx_1024 = -0.000264403 + 1.00002 * (_ctx_1024t + 0.3 * jax.random.normal(jax.random.fold_in(_rk, 611), (1, 6404, 128), jnp.float32))
        _validS = jnp.arange(1024)[None, :] < _lenS[:, None]
        _validS2 = jnp.arange(6404)[None, :] < _lenS2[:, None]
        _causal = jnp.tril(jnp.ones((1024, 1024), dtype=bool))
        mask_Bx1x1xS2_if1 = jnp.where(jnp.ones((1, 1, 1, 6404), dtype=bool), 1, 0).astype(jnp.int32)
        mask_Bx1x1xS2_ik0 = jnp.where(jnp.broadcast_to(_validS2[:, None, None, :], (1, 1, 1, 6404)), 0, 1).astype(jnp.int32)
        mask_BxS2_bf0 = jnp.logical_not(jnp.ones((1, 6404), dtype=bool))
        _g = jax.random.normal(jax.random.fold_in(_rk, 9001), (2, 4), jnp.float32)
        _g = jnp.sign(_g) * jnp.maximum(jnp.abs(_g), 1.0) + (_g == 0) * 1.0
        g_xattn = _g[0]
        g_ffn = _g[1]
        return (x, ctx_1024, mask_Bx1x1xS2_if1, mask_Bx1x1xS2_ik0, mask_BxS2_bf0, g_xattn, g_ffn)
    x, ctx_1024, mask_Bx1x1xS2_if1, mask_Bx1x1xS2_ik0, mask_BxS2_bf0, g_xattn, g_ffn = _rec_inputs()

    def _L0_xattn_setup():
        import jax, jax.numpy as jnp
        import numpy as np
        M, T, D, H = (2, 256, 128, 16)
        HD = D // H
        SCALE = 1.0 / np.sqrt(D).astype(np.float32)
        key = jax.random.key(seed)
        ks = jax.random.split(key, 8)

        def lin(k):
            kw, kb = jax.random.split(k)
            W = jax.random.normal(kw, (D, D), dtype=jnp.float32) * (1.0 / np.sqrt(D))
            b = jax.random.normal(kb, (D,), dtype=jnp.float32) * 0.01
            return (W, b)
        Wq, bq = lin(ks[0])
        Wk, bk = lin(ks[1])
        Wv, bv = lin(ks[2])
        Wo, bo = lin(ks[3])
        Q = jax.random.normal(ks[4], (M, T, D), dtype=jnp.float32)
        K = jax.random.normal(ks[5], (M, T, D), dtype=jnp.float32)
        V = jax.random.normal(ks[6], (M, T, D), dtype=jnp.float32)
        mask = jnp.ones((M, 1, 1, T), dtype=jnp.int32)
        return {'Q': Q, 'K': K, 'V': V, 'mask': mask, 'Wq': Wq, 'bq': bq, 'Wk': Wk, 'bk': bk, 'Wv': Wv, 'bv': bv, 'Wo': Wo, 'bo': bo}
    _L0_xattn_all = _L0_xattn_setup()
    _L0_xattn_in = {k: v for k, v in _L0_xattn_all.items() if k in ('Wq', 'bq', 'Wk', 'bk', 'Wv', 'bv', 'Wo', 'bo')}
    del _L0_xattn_all

    def _L0_ffn_setup():
        import jax, jax.numpy as jnp
        import numpy as np
        B, S, D = (2, 64, 128)
        E, K, I = (16, 8, 128)
        I_SH = 128
        ROUTE_SCALE = 2.826
        key = jax.random.key(seed)
        ks = jax.random.split(key, 8)
        s = 0.02
        return {'x': jax.random.normal(ks[0], (B, S, D), dtype=jnp.float32), 'gate_w': jax.random.normal(ks[1], (E, D), dtype=jnp.float32) * s, 'expert_bias': jnp.zeros((E,), dtype=jnp.float32), 'w_gate': jax.random.normal(ks[2], (E, I, D), dtype=jnp.float32) * s, 'w_up': jax.random.normal(ks[3], (E, I, D), dtype=jnp.float32) * s, 'w_down': jax.random.normal(ks[4], (E, D, I), dtype=jnp.float32) * s, 'shared_gate_w': jax.random.normal(ks[5], (I_SH, D), dtype=jnp.float32) * s, 'shared_up_w': jax.random.normal(ks[6], (I_SH, D), dtype=jnp.float32) * s, 'shared_down_w': jax.random.normal(ks[7], (D, I_SH), dtype=jnp.float32) * s}
    _L0_ffn_all = _L0_ffn_setup()
    _L0_ffn_in = {k: v for k, v in _L0_ffn_all.items() if k in ('gate_w', 'expert_bias', 'w_gate', 'w_up', 'w_down', 'shared_gate_w', 'shared_up_w', 'shared_down_w')}
    del _L0_ffn_all

    def _L1_xattn_setup():
        import jax, jax.numpy as jnp
        import numpy as np
        D_MODEL = 128
        NUM_HEADS = 16
        DEPTH = D_MODEL // NUM_HEADS
        NEG = -1e+30

        def _split_heads(x):
            B, S, _ = x.shape
            return x.reshape(B, S, NUM_HEADS, DEPTH).transpose(0, 2, 1, 3)
        key = jax.random.key(seed)
        ks = jax.random.split(key, 12)
        B, S = (4, 256)
        scale = 1.0 / np.sqrt(D_MODEL)
        inp = {'v': jax.random.normal(ks[0], (B, S, D_MODEL), dtype=jnp.float32), 'k': jax.random.normal(ks[1], (B, S, D_MODEL), dtype=jnp.float32), 'q': jax.random.normal(ks[2], (B, S, D_MODEL), dtype=jnp.float32), 'mask': jax.random.randint(ks[3], (B, 1, 1, S), 0, 2, dtype=jnp.int32), 'wq': jax.random.normal(ks[4], (D_MODEL, D_MODEL), dtype=jnp.float32) * scale, 'bq': jnp.zeros((D_MODEL,), dtype=jnp.float32), 'wk': jax.random.normal(ks[5], (D_MODEL, D_MODEL), dtype=jnp.float32) * scale, 'bk': jnp.zeros((D_MODEL,), dtype=jnp.float32), 'wv': jax.random.normal(ks[6], (D_MODEL, D_MODEL), dtype=jnp.float32) * scale, 'bv': jnp.zeros((D_MODEL,), dtype=jnp.float32), 'wo': jax.random.normal(ks[7], (D_MODEL, D_MODEL), dtype=jnp.float32) * scale, 'bo': jnp.zeros((D_MODEL,), dtype=jnp.float32)}
        return inp
    _L1_xattn_all = _L1_xattn_setup()
    _L1_xattn_in = {k: v for k, v in _L1_xattn_all.items() if k in ('wq', 'bq', 'wk', 'bk', 'wv', 'bv', 'wo', 'bo')}
    del _L1_xattn_all

    def _L1_ffn_setup():
        import jax, jax.numpy as jnp
        import numpy as np

        def _ste(w, w_q):
            return w + jax.lax.stop_gradient(w_q - w)

        def quantize_w8_per(w, axis):
            amax = jnp.clip(jnp.max(jnp.abs(w), axis=axis, keepdims=True), 1e-08, None)
            scale = 127.0 / amax
            w_q = jnp.clip(jnp.round(w * scale), -128.0, 127.0) / scale
            return _ste(w, w_q)

        def quantize_a16(x):
            amax = jnp.clip(jnp.max(jnp.abs(x)), 1e-08, None)
            scale = 32767.0 / amax
            x_q = jnp.clip(jnp.round(x * scale), -32768.0, 32767.0) / scale
            return _ste(x, x_q)
        key = jax.random.key(seed)
        k1, k2, k3 = jax.random.split(key, 3)
        d_model, d_ff = (128, 512)
        x = jax.random.normal(k1, (4, 256, d_model), dtype=jnp.float32)
        W_in = jax.random.normal(k2, (d_model, d_ff), dtype=jnp.float32) / np.sqrt(d_model)
        b_in = jnp.zeros((d_ff,), dtype=jnp.float32)
        W_out = jax.random.normal(k3, (d_ff, d_model), dtype=jnp.float32) / np.sqrt(d_ff)
        b_out = jnp.zeros((d_model,), dtype=jnp.float32)
        return {'x': x, 'W_in': W_in, 'b_in': b_in, 'W_out': W_out, 'b_out': b_out}
    _L1_ffn_all = _L1_ffn_setup()
    _L1_ffn_in = {k: v for k, v in _L1_ffn_all.items() if k in ('W_in', 'b_in', 'W_out', 'b_out')}
    del _L1_ffn_all

    def _L2_xattn_setup():
        import jax, jax.numpy as jnp
        import numpy as np
        import math
        D_MODEL = 128
        N_HEADS = 16
        HEAD_DIM = D_MODEL // N_HEADS
        TOP_K = 32
        SCALE = math.sqrt(HEAD_DIM)

        def _split_heads(t, n):
            B, L, _ = t.shape
            return t.reshape(B, L, N_HEADS, HEAD_DIM).transpose(0, 2, 1, 3)
        key = jax.random.key(seed)
        ks = jax.random.split(key, 12)
        B, S, N = (2, 256, 256)
        std = 1.0 / math.sqrt(D_MODEL)
        inp = {'x': jax.random.normal(ks[0], (B, S, D_MODEL), dtype=jnp.float32), 'knowledge_embeddings': jax.random.normal(ks[1], (B, N, D_MODEL), dtype=jnp.float32), 'Wq': jax.random.normal(ks[2], (D_MODEL, D_MODEL), dtype=jnp.float32) * std, 'bq': jnp.zeros((D_MODEL,), dtype=jnp.float32), 'Wk': jax.random.normal(ks[3], (D_MODEL, D_MODEL), dtype=jnp.float32) * std, 'bk': jnp.zeros((D_MODEL,), dtype=jnp.float32), 'Wv': jax.random.normal(ks[4], (D_MODEL, D_MODEL), dtype=jnp.float32) * std, 'bv': jnp.zeros((D_MODEL,), dtype=jnp.float32), 'Wo': jax.random.normal(ks[5], (D_MODEL, D_MODEL), dtype=jnp.float32) * std, 'bo': jnp.zeros((D_MODEL,), dtype=jnp.float32)}
        return inp
    _L2_xattn_all = _L2_xattn_setup()
    _L2_xattn_in = {k: v for k, v in _L2_xattn_all.items() if k in ('Wq', 'bq', 'Wk', 'bk', 'Wv', 'bv', 'Wo', 'bo')}
    del _L2_xattn_all

    def _L2_ffn_setup():
        import jax, jax.numpy as jnp
        import numpy as np
        DIM = 128
        DEPTH = 6
        HEADS = 16
        DIM_HEAD = 64
        WINDOW = 32
        INNER = HEADS * DIM_HEAD
        DIM_INNER = int(DIM * 4 * 2 / 3)
        QK_SCALE = 8.0

        def shift_tokens(t):
            a, s = jnp.split(t, 2, -1)
            s = jnp.pad(s, ((0, 0), (1, 0), (0, 0)))[:, :-1]
            return jnp.concatenate([a, s], -1)

        def l2norm(t):
            return t / jnp.maximum(jnp.linalg.norm(t, axis=-1, keepdims=True), 1e-12)

        def rotate_half(x):
            x1, x2 = jnp.split(x, 2, -1)
            return jnp.concatenate([-x2, x1], -1)

        def rotary_tables(n):
            half = jnp.arange(0, DIM_HEAD, 2, dtype=jnp.float32)
            inv_freq = 1.0 / 10000.0 ** (half / DIM_HEAD)
            t = jnp.arange(n, dtype=jnp.float32)
            freqs = t[:, None] * inv_freq[None, :]
            freqs = jnp.concatenate([freqs, freqs], -1)
            base_scale = (half + 0.4 * DIM_HEAD) / (1.4 * DIM_HEAD)
            power = (t - n // 2) / (WINDOW // 2)
            scale = base_scale[None, :] ** power[:, None]
            scale = jnp.concatenate([scale, scale], -1)
            return (freqs, scale)

        def local_attention(q, k, v):
            b, h, n, d = q.shape
            w = WINDOW
            nw = n // w
            bq = q.reshape(b, h, nw, w, d)
            bk = k.reshape(b, h, nw, w, d)
            bv = v.reshape(b, h, nw, w, d)

            def look(t):
                p = jnp.pad(t, ((0, 0), (0, 0), (1, 0), (0, 0), (0, 0)))
                return jnp.concatenate([p[:, :, :nw], p[:, :, 1:]], axis=3)
            bk2, bv2 = (look(bk), look(bv))
            seq = jnp.arange(n).reshape(nw, w)
            seq_p = jnp.pad(seq, ((1, 0), (0, 0)), constant_values=-1)
            jt = jnp.concatenate([seq_p[:nw], seq_p[1:]], axis=1)
            it = seq[:, :, None]
            jb = jt[:, None, :]
            mask = (it < jb) | (it > jb + w) | (jb == -1)
            sim = jnp.einsum('bhwie,bhwje->bhwij', bq, bk2) * QK_SCALE
            sim = jnp.where(mask, -jnp.finfo(sim.dtype).max, sim)
            attn = jax.nn.softmax(sim, -1)
            out = jnp.einsum('bhwij,bhwje->bhwie', attn, bv2)
            return out.reshape(b, h, n, d)

        def attn_layer(x, Wqkv, qs, ksc, Wo):
            b, n, _ = x.shape
            qkv = x @ Wqkv
            q, k, v = jnp.split(qkv, 3, -1)
            sh = lambda t: t.reshape(b, n, HEADS, DIM_HEAD).transpose(0, 2, 1, 3)
            q, k, v = (sh(q), sh(k), sh(v))
            q = l2norm(q) * qs
            k = l2norm(k) * ksc
            freqs, scale = rotary_tables(n)
            cos, sin = (jnp.cos(freqs), jnp.sin(freqs))
            q = q * cos * scale + rotate_half(q) * sin * scale
            inv = 1.0 / scale
            k = k * cos * inv + rotate_half(k) * sin * inv
            out = local_attention(q, k, v)
            out = out.transpose(0, 2, 1, 3).reshape(b, n, INNER)
            return out @ Wo

        def ffn_layer(x, g, bln, W1, b1, W2, b2):
            mu = x.mean(-1, keepdims=True)
            var = ((x - mu) ** 2).mean(-1, keepdims=True)
            xn = (x - mu) / jnp.sqrt(var + 1e-05) * g + bln
            hg = xn @ W1 + b1
            a, gate = jnp.split(hg, 2, -1)
            return a * jax.nn.gelu(gate, approximate=False) @ W2 + b2
        key = jax.random.key(seed)
        ks = jax.random.split(key, 8)
        B, N = (2, 256)
        init = lambda k, shape: jax.random.normal(k, shape, jnp.float32) * 0.02
        return {'x': jax.random.normal(ks[0], (B, N, DIM), jnp.float32), 'Wqkv': init(ks[1], (DEPTH, DIM, 3 * INNER)), 'q_scale': jnp.ones((DEPTH, DIM_HEAD), jnp.float32), 'k_scale': jnp.ones((DEPTH, DIM_HEAD), jnp.float32), 'Wo': init(ks[2], (DEPTH, INNER, DIM)), 'ln_g': jnp.ones((DEPTH, DIM), jnp.float32), 'ln_b': jnp.zeros((DEPTH, DIM), jnp.float32), 'W1': init(ks[3], (DEPTH, DIM, 2 * DIM_INNER)), 'b1': jnp.zeros((DEPTH, 2 * DIM_INNER), jnp.float32), 'W2': init(ks[4], (DEPTH, DIM_INNER, DIM)), 'b2': jnp.zeros((DEPTH, DIM), jnp.float32)}
    _L2_ffn_all = _L2_ffn_setup()
    _L2_ffn_in = {k: v for k, v in _L2_ffn_all.items() if k in ('Wqkv', 'q_scale', 'k_scale', 'Wo', 'ln_g', 'ln_b', 'W1', 'b1', 'W2', 'b2')}
    del _L2_ffn_all

    def _L3_xattn_setup():
        import jax, jax.numpy as jnp
        import numpy as np
        B, SQ, SKV, D, H = (2, 256, 256, 128, 16)
        HD = D // H

        def cross_attention(query, context, mask, Wq, bq, Wkv, bkv, Wout, bout, num_heads):
            b, sq, d = query.shape
            skv = context.shape[1]
            hd = d // num_heads
            scale = hd ** (-0.5)
            q = query @ Wq + bq
            kv = context @ Wkv + bkv
            kv = kv.reshape(b, skv, 2, num_heads, hd).transpose(2, 0, 3, 1, 4)
            k, v = (kv[0], kv[1])
            q = q.reshape(b, sq, num_heads, hd).transpose(0, 2, 1, 3)
            scores = jnp.einsum('bhid,bhjd->bhij', q, k) * scale
            scores = jnp.where(mask[:, None, None, :], -jnp.inf, scores)
            attn = jax.nn.softmax(scores, axis=-1)
            out = jnp.einsum('bhij,bhjd->bhid', attn, v)
            out = out.transpose(0, 2, 1, 3).reshape(b, sq, d)
            return out @ Wout + bout
        key = jax.random.key(seed)
        ks = jax.random.split(key, 6)
        scale = 1.0 / np.sqrt(D)
        return {'query': jax.random.normal(ks[0], (B, SQ, D), dtype=jnp.float32), 'context': jax.random.normal(ks[1], (B, SKV, D), dtype=jnp.float32), 'mask': jnp.zeros((B, SKV), dtype=bool), 'Wq': jax.random.normal(ks[2], (D, D), dtype=jnp.float32) * scale, 'bq': jnp.zeros((D,), dtype=jnp.float32), 'Wkv': jax.random.normal(ks[3], (D, 2 * D), dtype=jnp.float32) * scale, 'bkv': jnp.zeros((2 * D,), dtype=jnp.float32), 'Wout': jax.random.normal(ks[4], (D, D), dtype=jnp.float32) * scale, 'bout': jnp.zeros((D,), dtype=jnp.float32), 'num_heads': H}
    _L3_xattn_all = _L3_xattn_setup()
    _L3_xattn_in = {k: v for k, v in _L3_xattn_all.items() if k in ('Wq', 'bq', 'Wkv', 'bkv', 'Wout', 'bout')}
    del _L3_xattn_all

    def _L3_ffn_setup():
        import jax, jax.numpy as jnp
        import numpy as np
        D_MODEL = 128
        HIDDEN = 352
        N_EXPERTS = 8
        TOP_K = 2
        BSZ, SEQ = (4, 512)
        key = jax.random.key(seed)
        ks = jax.random.split(key, 5)
        x = jax.random.normal(ks[0], (BSZ, SEQ, D_MODEL), dtype=jnp.float32)
        router_w = jax.random.normal(ks[1], (D_MODEL, N_EXPERTS), dtype=jnp.float32) * 0.02
        w1 = jax.random.normal(ks[2], (N_EXPERTS, D_MODEL, HIDDEN), dtype=jnp.float32) * 0.02
        w3 = jax.random.normal(ks[3], (N_EXPERTS, D_MODEL, HIDDEN), dtype=jnp.float32) * 0.02
        w2 = jax.random.normal(ks[4], (N_EXPERTS, HIDDEN, D_MODEL), dtype=jnp.float32) * 0.02
        return {'x': x, 'router_w': router_w, 'w1': w1, 'w3': w3, 'w2': w2}
    _L3_ffn_all = _L3_ffn_setup()
    _L3_ffn_in = {k: v for k, v in _L3_ffn_all.items() if k in ('router_w', 'w1', 'w3', 'w2')}
    del _L3_ffn_all
    return {'x': x, 'ctx_1024': ctx_1024, 'mask_Bx1x1xS2_if1': mask_Bx1x1xS2_if1, 'mask_Bx1x1xS2_ik0': mask_Bx1x1xS2_ik0, 'mask_BxS2_bf0': mask_BxS2_bf0, 'g_xattn': g_xattn, 'g_ffn': g_ffn, 'L0_xattn_Wq': _L0_xattn_in['Wq'], 'L0_xattn_bq': _L0_xattn_in['bq'], 'L0_xattn_Wk': _L0_xattn_in['Wk'], 'L0_xattn_bk': _L0_xattn_in['bk'], 'L0_xattn_Wv': _L0_xattn_in['Wv'], 'L0_xattn_bv': _L0_xattn_in['bv'], 'L0_xattn_Wo': _L0_xattn_in['Wo'], 'L0_xattn_bo': _L0_xattn_in['bo'], 'L0_ffn_gate_w': _L0_ffn_in['gate_w'], 'L0_ffn_expert_bias': _L0_ffn_in['expert_bias'], 'L0_ffn_w_gate': _L0_ffn_in['w_gate'], 'L0_ffn_w_up': _L0_ffn_in['w_up'], 'L0_ffn_w_down': _L0_ffn_in['w_down'], 'L0_ffn_shared_gate_w': _L0_ffn_in['shared_gate_w'], 'L0_ffn_shared_up_w': _L0_ffn_in['shared_up_w'], 'L0_ffn_shared_down_w': _L0_ffn_in['shared_down_w'], 'L1_xattn_wq': _L1_xattn_in['wq'], 'L1_xattn_bq': _L1_xattn_in['bq'], 'L1_xattn_wk': _L1_xattn_in['wk'], 'L1_xattn_bk': _L1_xattn_in['bk'], 'L1_xattn_wv': _L1_xattn_in['wv'], 'L1_xattn_bv': _L1_xattn_in['bv'], 'L1_xattn_wo': _L1_xattn_in['wo'], 'L1_xattn_bo': _L1_xattn_in['bo'], 'L1_ffn_W_in': _L1_ffn_in['W_in'], 'L1_ffn_b_in': _L1_ffn_in['b_in'], 'L1_ffn_W_out': _L1_ffn_in['W_out'], 'L1_ffn_b_out': _L1_ffn_in['b_out'], 'L2_xattn_Wq': _L2_xattn_in['Wq'], 'L2_xattn_bq': _L2_xattn_in['bq'], 'L2_xattn_Wk': _L2_xattn_in['Wk'], 'L2_xattn_bk': _L2_xattn_in['bk'], 'L2_xattn_Wv': _L2_xattn_in['Wv'], 'L2_xattn_bv': _L2_xattn_in['bv'], 'L2_xattn_Wo': _L2_xattn_in['Wo'], 'L2_xattn_bo': _L2_xattn_in['bo'], 'L2_ffn_Wqkv': _L2_ffn_in['Wqkv'], 'L2_ffn_q_scale': _L2_ffn_in['q_scale'], 'L2_ffn_k_scale': _L2_ffn_in['k_scale'], 'L2_ffn_Wo': _L2_ffn_in['Wo'], 'L2_ffn_ln_g': _L2_ffn_in['ln_g'], 'L2_ffn_ln_b': _L2_ffn_in['ln_b'], 'L2_ffn_W1': _L2_ffn_in['W1'], 'L2_ffn_b1': _L2_ffn_in['b1'], 'L2_ffn_W2': _L2_ffn_in['W2'], 'L2_ffn_b2': _L2_ffn_in['b2'], 'L3_xattn_Wq': _L3_xattn_in['Wq'], 'L3_xattn_bq': _L3_xattn_in['bq'], 'L3_xattn_Wkv': _L3_xattn_in['Wkv'], 'L3_xattn_bkv': _L3_xattn_in['bkv'], 'L3_xattn_Wout': _L3_xattn_in['Wout'], 'L3_xattn_bout': _L3_xattn_in['bout'], 'L3_ffn_router_w': _L3_ffn_in['router_w'], 'L3_ffn_w1': _L3_ffn_in['w1'], 'L3_ffn_w3': _L3_ffn_in['w3'], 'L3_ffn_w2': _L3_ffn_in['w2']}

def reference(x, ctx_1024, mask_Bx1x1xS2_if1, mask_Bx1x1xS2_ik0, mask_BxS2_bf0, g_xattn, g_ffn, L0_xattn_Wq, L0_xattn_bq, L0_xattn_Wk, L0_xattn_bk, L0_xattn_Wv, L0_xattn_bv, L0_xattn_Wo, L0_xattn_bo, L0_ffn_gate_w, L0_ffn_expert_bias, L0_ffn_w_gate, L0_ffn_w_up, L0_ffn_w_down, L0_ffn_shared_gate_w, L0_ffn_shared_up_w, L0_ffn_shared_down_w, L1_xattn_wq, L1_xattn_bq, L1_xattn_wk, L1_xattn_bk, L1_xattn_wv, L1_xattn_bv, L1_xattn_wo, L1_xattn_bo, L1_ffn_W_in, L1_ffn_b_in, L1_ffn_W_out, L1_ffn_b_out, L2_xattn_Wq, L2_xattn_bq, L2_xattn_Wk, L2_xattn_bk, L2_xattn_Wv, L2_xattn_bv, L2_xattn_Wo, L2_xattn_bo, L2_ffn_Wqkv, L2_ffn_q_scale, L2_ffn_k_scale, L2_ffn_Wo, L2_ffn_ln_g, L2_ffn_ln_b, L2_ffn_W1, L2_ffn_b1, L2_ffn_W2, L2_ffn_b2, L3_xattn_Wq, L3_xattn_bq, L3_xattn_Wkv, L3_xattn_bkv, L3_xattn_Wout, L3_xattn_bout, L3_ffn_router_w, L3_ffn_w1, L3_ffn_w3, L3_ffn_w2):
    import jax
    import jax.numpy as jnp

    def _L0_xattn_ref(Q, K, V, mask, Wq, bq, Wk, bk, Wv, bv, Wo, bo):
        import jax, jax.numpy as jnp
        import numpy as np
        M, T, D, H = (2, 256, 128, 16)
        HD = D // H
        SCALE = 1.0 / np.sqrt(D).astype(np.float32)
        m = Q.shape[0]
        q = (Q @ Wq.T + bq).reshape(m, -1, H, HD)
        k = (K @ Wk.T + bk).reshape(m, -1, H, HD)
        v = (V @ Wv.T + bv).reshape(m, -1, H, HD)
        energy = jnp.einsum('mqhd,mkhd->mhqk', q, k) * SCALE
        if mask is not None:
            energy = jnp.where(mask == 0, jnp.float32(-1e+20), energy)
        attn = jax.nn.softmax(energy, axis=3)
        out = jnp.einsum('mhqk,mkhd->mqhd', attn, v)
        concat = out.reshape(m, -1, H * HD)
        return concat @ Wo.T + bo

    def _L0_ffn_ref(x, gate_w, expert_bias, w_gate, w_up, w_down, shared_gate_w, shared_up_w, shared_down_w):
        import jax, jax.numpy as jnp
        import numpy as np
        B, S, D = (2, 64, 128)
        E, K, I = (16, 8, 128)
        I_SH = 128
        ROUTE_SCALE = 2.826
        gates = jnp.einsum('bsd,ed->bse', x, gate_w)
        scores = jax.nn.sigmoid(gates.astype(jnp.float32))
        sel_scores = scores + expert_bias
        _, inds = jax.lax.top_k(sel_scores, K)
        selected = jnp.take_along_axis(scores, inds, axis=-1)
        selected = selected / selected.sum(axis=-1, keepdims=True)
        selected = selected * ROUTE_SCALE
        onehot = jax.nn.one_hot(inds, E, dtype=selected.dtype)
        combine = jnp.einsum('bske,bsk->bse', onehot, selected)
        hg = jnp.einsum('bsd,eid->bsei', x, w_gate)
        hu = jnp.einsum('bsd,eid->bsei', x, w_up)
        h = jax.nn.silu(hg) * hu
        ye = jnp.einsum('bsei,edi->bsed', h, w_down)
        y = jnp.einsum('bsed,bse->bsd', ye, combine).astype(x.dtype)
        g = jnp.einsum('bsd,id->bsi', x, shared_gate_w)
        u = jnp.einsum('bsd,id->bsi', x, shared_up_w)
        y = y + jnp.einsum('bsi,di->bsd', jax.nn.silu(g) * u, shared_down_w)
        return y

    def _L1_xattn_ref(v, k, q, mask, wq, bq, wk, bk, wv, bv, wo, bo):
        import jax, jax.numpy as jnp
        import numpy as np
        D_MODEL = 128
        NUM_HEADS = 16
        DEPTH = D_MODEL // NUM_HEADS
        NEG = -1e+30

        def _split_heads(x):
            B, S, _ = x.shape
            return x.reshape(B, S, NUM_HEADS, DEPTH).transpose(0, 2, 1, 3)
        B, Sq, _ = q.shape
        qh = _split_heads(q @ wq + bq)
        kh = _split_heads(k @ wk + bk)
        vh = _split_heads(v @ wv + bv)
        scale = 1.0 / jnp.sqrt(jnp.float32(DEPTH))
        scores = scale * jnp.einsum('bhqd,bhkd->bhqk', qh, kh)
        scores = scores + mask.astype(scores.dtype) * NEG
        attn = jax.nn.softmax(scores, axis=-1)
        out = jnp.einsum('bhqk,bhkd->bhqd', attn, vh)
        out = out.transpose(0, 2, 1, 3).reshape(B, Sq, D_MODEL)
        return out @ wo + bo

    def _L1_ffn_ref(x, W_in, b_in, W_out, b_out):
        import jax, jax.numpy as jnp
        import numpy as np

        def _ste(w, w_q):
            return w + jax.lax.stop_gradient(w_q - w)

        def quantize_w8_per(w, axis):
            amax = jnp.clip(jnp.max(jnp.abs(w), axis=axis, keepdims=True), 1e-08, None)
            scale = 127.0 / amax
            w_q = jnp.clip(jnp.round(w * scale), -128.0, 127.0) / scale
            return _ste(w, w_q)

        def quantize_a16(x):
            amax = jnp.clip(jnp.max(jnp.abs(x)), 1e-08, None)
            scale = 32767.0 / amax
            x_q = jnp.clip(jnp.round(x * scale), -32768.0, 32767.0) / scale
            return _ste(x, x_q)
        W_in_sim = quantize_w8_per(W_in, axis=0)
        W_out_sim = quantize_w8_per(W_out, axis=1)
        x_sim = quantize_a16(x)
        hidden = jax.nn.gelu(x_sim @ W_in_sim + b_in, approximate=False)
        hidden_sim = quantize_a16(hidden)
        out = hidden_sim @ W_out_sim + b_out
        return out

    def _L2_xattn_ref(x, knowledge_embeddings, Wq, bq, Wk, bk, Wv, bv, Wo, bo):
        import jax, jax.numpy as jnp
        import numpy as np
        import math
        D_MODEL = 128
        N_HEADS = 16
        HEAD_DIM = D_MODEL // N_HEADS
        TOP_K = 32
        SCALE = math.sqrt(HEAD_DIM)

        def _split_heads(t, n):
            B, L, _ = t.shape
            return t.reshape(B, L, N_HEADS, HEAD_DIM).transpose(0, 2, 1, 3)
        B, S, _ = x.shape
        N = knowledge_embeddings.shape[1]
        Q = _split_heads(x @ Wq.T + bq, N_HEADS)
        K = _split_heads(knowledge_embeddings @ Wk.T + bk, N_HEADS)
        V = _split_heads(knowledge_embeddings @ Wv.T + bv, N_HEADS)
        scores = jnp.einsum('bhsd,bhnd->bhsn', Q, K) / SCALE
        k = min(TOP_K, N)
        topk_scores, topk_indices = jax.lax.top_k(scores, k)
        sparse_weights = jax.nn.softmax(topk_scores, axis=-1)
        sel_V = jnp.take_along_axis(V[:, :, None, :, :], topk_indices[..., None], axis=3)
        context = jnp.einsum('bhsk,bhskd->bhsd', sparse_weights, sel_V)
        context = context.transpose(0, 2, 1, 3).reshape(B, S, D_MODEL)
        return context @ Wo.T + bo

    def _L2_ffn_ref(x, Wqkv, q_scale, k_scale, Wo, ln_g, ln_b, W1, b1, W2, b2):
        import jax, jax.numpy as jnp
        import numpy as np
        DIM = 128
        DEPTH = 6
        HEADS = 16
        DIM_HEAD = 64
        WINDOW = 32
        INNER = HEADS * DIM_HEAD
        DIM_INNER = int(DIM * 4 * 2 / 3)
        QK_SCALE = 8.0

        def shift_tokens(t):
            a, s = jnp.split(t, 2, -1)
            s = jnp.pad(s, ((0, 0), (1, 0), (0, 0)))[:, :-1]
            return jnp.concatenate([a, s], -1)

        def l2norm(t):
            return t / jnp.maximum(jnp.linalg.norm(t, axis=-1, keepdims=True), 1e-12)

        def rotate_half(x):
            x1, x2 = jnp.split(x, 2, -1)
            return jnp.concatenate([-x2, x1], -1)

        def rotary_tables(n):
            half = jnp.arange(0, DIM_HEAD, 2, dtype=jnp.float32)
            inv_freq = 1.0 / 10000.0 ** (half / DIM_HEAD)
            t = jnp.arange(n, dtype=jnp.float32)
            freqs = t[:, None] * inv_freq[None, :]
            freqs = jnp.concatenate([freqs, freqs], -1)
            base_scale = (half + 0.4 * DIM_HEAD) / (1.4 * DIM_HEAD)
            power = (t - n // 2) / (WINDOW // 2)
            scale = base_scale[None, :] ** power[:, None]
            scale = jnp.concatenate([scale, scale], -1)
            return (freqs, scale)

        def local_attention(q, k, v):
            b, h, n, d = q.shape
            w = WINDOW
            nw = n // w
            bq = q.reshape(b, h, nw, w, d)
            bk = k.reshape(b, h, nw, w, d)
            bv = v.reshape(b, h, nw, w, d)

            def look(t):
                p = jnp.pad(t, ((0, 0), (0, 0), (1, 0), (0, 0), (0, 0)))
                return jnp.concatenate([p[:, :, :nw], p[:, :, 1:]], axis=3)
            bk2, bv2 = (look(bk), look(bv))
            seq = jnp.arange(n).reshape(nw, w)
            seq_p = jnp.pad(seq, ((1, 0), (0, 0)), constant_values=-1)
            jt = jnp.concatenate([seq_p[:nw], seq_p[1:]], axis=1)
            it = seq[:, :, None]
            jb = jt[:, None, :]
            mask = (it < jb) | (it > jb + w) | (jb == -1)
            sim = jnp.einsum('bhwie,bhwje->bhwij', bq, bk2) * QK_SCALE
            sim = jnp.where(mask, -jnp.finfo(sim.dtype).max, sim)
            attn = jax.nn.softmax(sim, -1)
            out = jnp.einsum('bhwij,bhwje->bhwie', attn, bv2)
            return out.reshape(b, h, n, d)

        def attn_layer(x, Wqkv, qs, ksc, Wo):
            b, n, _ = x.shape
            qkv = x @ Wqkv
            q, k, v = jnp.split(qkv, 3, -1)
            sh = lambda t: t.reshape(b, n, HEADS, DIM_HEAD).transpose(0, 2, 1, 3)
            q, k, v = (sh(q), sh(k), sh(v))
            q = l2norm(q) * qs
            k = l2norm(k) * ksc
            freqs, scale = rotary_tables(n)
            cos, sin = (jnp.cos(freqs), jnp.sin(freqs))
            q = q * cos * scale + rotate_half(q) * sin * scale
            inv = 1.0 / scale
            k = k * cos * inv + rotate_half(k) * sin * inv
            out = local_attention(q, k, v)
            out = out.transpose(0, 2, 1, 3).reshape(b, n, INNER)
            return out @ Wo

        def ffn_layer(x, g, bln, W1, b1, W2, b2):
            mu = x.mean(-1, keepdims=True)
            var = ((x - mu) ** 2).mean(-1, keepdims=True)
            xn = (x - mu) / jnp.sqrt(var + 1e-05) * g + bln
            hg = xn @ W1 + b1
            a, gate = jnp.split(hg, 2, -1)
            return a * jax.nn.gelu(gate, approximate=False) @ W2 + b2
        for i in range(DEPTH):
            x = attn_layer(shift_tokens(x), Wqkv[i], q_scale[i], k_scale[i], Wo[i]) + x
            x = ffn_layer(shift_tokens(x), ln_g[i], ln_b[i], W1[i], b1[i], W2[i], b2[i]) + x
        return x

    def _L3_xattn_ref(query, context, mask, Wq, bq, Wkv, bkv, Wout, bout, num_heads):
        import jax, jax.numpy as jnp
        import numpy as np
        B, SQ, SKV, D, H = (2, 256, 256, 128, 16)
        HD = D // H

        def cross_attention(query, context, mask, Wq, bq, Wkv, bkv, Wout, bout, num_heads):
            b, sq, d = query.shape
            skv = context.shape[1]
            hd = d // num_heads
            scale = hd ** (-0.5)
            q = query @ Wq + bq
            kv = context @ Wkv + bkv
            kv = kv.reshape(b, skv, 2, num_heads, hd).transpose(2, 0, 3, 1, 4)
            k, v = (kv[0], kv[1])
            q = q.reshape(b, sq, num_heads, hd).transpose(0, 2, 1, 3)
            scores = jnp.einsum('bhid,bhjd->bhij', q, k) * scale
            scores = jnp.where(mask[:, None, None, :], -jnp.inf, scores)
            attn = jax.nn.softmax(scores, axis=-1)
            out = jnp.einsum('bhij,bhjd->bhid', attn, v)
            out = out.transpose(0, 2, 1, 3).reshape(b, sq, d)
            return out @ Wout + bout
        return cross_attention(query, context, mask, Wq, bq, Wkv, bkv, Wout, bout, num_heads)

    def _L3_ffn_ref(x, router_w, w1, w3, w2):
        import jax, jax.numpy as jnp
        import numpy as np
        D_MODEL = 128
        HIDDEN = 352
        N_EXPERTS = 8
        TOP_K = 2
        BSZ, SEQ = (4, 512)
        bsz, seq_len, d_model = x.shape
        n_experts, top_k = (w1.shape[0], TOP_K)
        flat = x.reshape(-1, d_model)
        s = flat.shape[0]
        logits = flat @ router_w
        topk_vals, topk_idx = jax.lax.top_k(logits, top_k)
        topk_w = jax.nn.softmax(topk_vals, axis=-1)
        gates = jnp.zeros((s, n_experts), dtype=flat.dtype)
        gates = gates.at[jnp.arange(s)[:, None], topk_idx].set(topk_w)
        out = jnp.zeros_like(flat)
        for e in range(n_experts):
            h = jax.nn.silu(flat @ w1[e]) * (flat @ w3[e])
            out = out + h @ w2[e] * gates[:, e:e + 1]
        return out.reshape(bsz, seq_len, d_model)
    x = x + jnp.tanh(g_xattn[0]) * _L0_xattn_ref(_layernorm(x, axis=-1), ctx_1024, ctx_1024, mask_Bx1x1xS2_if1, L0_xattn_Wq, L0_xattn_bq, L0_xattn_Wk, L0_xattn_bk, L0_xattn_Wv, L0_xattn_bv, L0_xattn_Wo, L0_xattn_bo)
    x = x + jnp.tanh(g_ffn[0]) * _L0_ffn_ref(_layernorm(x, axis=-1), L0_ffn_gate_w, L0_ffn_expert_bias, L0_ffn_w_gate, L0_ffn_w_up, L0_ffn_w_down, L0_ffn_shared_gate_w, L0_ffn_shared_up_w, L0_ffn_shared_down_w)
    x = x + jnp.tanh(g_xattn[1]) * _L1_xattn_ref(ctx_1024, ctx_1024, _layernorm(x, axis=-1), mask_Bx1x1xS2_ik0, L1_xattn_wq, L1_xattn_bq, L1_xattn_wk, L1_xattn_bk, L1_xattn_wv, L1_xattn_bv, L1_xattn_wo, L1_xattn_bo)
    x = x + jnp.tanh(g_ffn[1]) * _L1_ffn_ref(_layernorm(x, axis=-1), L1_ffn_W_in, L1_ffn_b_in, L1_ffn_W_out, L1_ffn_b_out)
    x = x + jnp.tanh(g_xattn[2]) * _L2_xattn_ref(_layernorm(x, axis=-1), ctx_1024, L2_xattn_Wq, L2_xattn_bq, L2_xattn_Wk, L2_xattn_bk, L2_xattn_Wv, L2_xattn_bv, L2_xattn_Wo, L2_xattn_bo)
    x = x + jnp.tanh(g_ffn[2]) * _L2_ffn_ref(_layernorm(x, axis=-1), L2_ffn_Wqkv, L2_ffn_q_scale, L2_ffn_k_scale, L2_ffn_Wo, L2_ffn_ln_g, L2_ffn_ln_b, L2_ffn_W1, L2_ffn_b1, L2_ffn_W2, L2_ffn_b2)
    x = x + jnp.tanh(g_xattn[3]) * _L3_xattn_ref(_layernorm(x, axis=-1), ctx_1024, mask_BxS2_bf0, L3_xattn_Wq, L3_xattn_bq, L3_xattn_Wkv, L3_xattn_bkv, L3_xattn_Wout, L3_xattn_bout, 16)
    x = x + jnp.tanh(g_ffn[3]) * _L3_ffn_ref(_layernorm(x, axis=-1), L3_ffn_router_w, L3_ffn_w1, L3_ffn_w3, L3_ffn_w2)
    return x

_drawn_inputs = setup_inputs


def setup_inputs(seed=0):
    import zlib

    import numpy as np

    out = dict(_drawn_inputs(seed))
    spreads = {'L0_ffn_expert_bias': (0.0, 0.8),
     'L1_xattn_bq': (0.0, 0.401),
     'L1_xattn_bk': (0.0, 0.8),
     'L1_xattn_bv': (0.0, 0.1),
     'L1_xattn_bo': (0.0, 0.1),
     'L1_ffn_b_in': (0.0, 0.1),
     'L1_ffn_b_out': (0.0, 0.1),
     'L2_xattn_bq': (0.0, 0.1),
     'L2_xattn_bk': (0.0, 0.8),
     'L2_xattn_bv': (0.0, 0.1),
     'L2_xattn_bo': (0.0, 0.1),
     'L2_ffn_q_scale': (1.0, 0.6),
     'L2_ffn_k_scale': (1.0, 0.6),
     'L2_ffn_ln_g': (1.0, 0.6),
     'L2_ffn_ln_b': (0.0, 0.8),
     'L2_ffn_b1': (0.0, 0.615),
     'L2_ffn_b2': (0.0, 0.1),
     'L3_xattn_bq': (0.0, 0.473),
     'L3_xattn_bkv': (0.0, 0.1),
     'L3_xattn_bout': (0.0, 0.1)}
    factors = {'L0_xattn_bq': 8.0,
     'L0_xattn_bk': 8.0,
     'L0_xattn_bv': 6.56,
     'L0_xattn_bo': 5.95,
     'L0_ffn_gate_w': 8.0,
     'L0_ffn_w_gate': 8.0,
     'L0_ffn_w_up': 8.0,
     'L0_ffn_w_down': 8.0,
     'L0_ffn_shared_gate_w': 8.0,
     'L0_ffn_shared_up_w': 8.0,
     'L0_ffn_shared_down_w': 8.0,
     'L3_ffn_router_w': 8.0,
     'L3_ffn_w1': 8.0,
     'L3_ffn_w3': 8.0,
     'L3_ffn_w2': 8.0}
    for name, (base, spread) in spreads.items():
        noise = np.random.default_rng([zlib.crc32(name.encode()), seed]).standard_normal(out[name].shape)
        drawn = base * np.exp(spread * noise) if base else spread * noise
        out[name] = jnp.asarray(drawn.astype(out[name].dtype))
    for name, factor in factors.items():
        out[name] = (out[name] * factor).astype(out[name].dtype)
    return out
```

```python
from contextlib import ExitStack

import numpy as np

import concourse.bass as bass
from concourse import mybir

ALU = mybir.AluOpType
ACT = mybir.ActivationFunctionType
AX = mybir.AxisListType.X
F32 = mybir.dt.float32
BF16 = mybir.dt.bfloat16
I32 = mybir.dt.int32
U8 = mybir.dt.uint8
ds = bass.ds

P = 128
D = 128
N = 1024
NT = N // P
H = 16
HD = D // H
S2 = 6404
KT = -(-S2 // P)
KPAD = KT * P
TB = 3
NB = KT // TB
BK = TB * P
assert NB * TB == KT
LAYERS = 4
K_PARTS = (0, 1, 2, 0, 1, 0)
Q_PARTS = (0, 0, 0, 1, 1, 2)
NPROD = len(K_PARTS)
AUX = NPROD * HD
ROWS = AUX + 6
HROWS = 64
NEG0 = -1e20
NEG1 = -1e30
EPS = 1e-5
QC = 512
NQC = N // QC
G = 4
NG = H // G
L0_E = 16
L3_E = 8
L3_C = 3
LOWER = 50.0
VW = HD + 1


class Memory:

    def __init__(self, nc, ctx, tag):
        self.nc, self.ctx, self.tag, self.sems = nc, ctx, tag, []
        ctx.callback(self.clear)

    def sb(self, name, shape, dt=F32):
        return self.ctx.enter_context(self.nc.sbuf_tensor(f"{self.tag}_{name}", shape, dt))

    def ps(self, name, shape, dt=F32):
        return self.ctx.enter_context(self.nc.psum_tensor(f"{self.tag}_{name}", shape, dt))

    def sem(self, name):
        self.sems.append(self.nc.alloc_semaphore(f"{self.tag}_{name}"))
        return self.sems[-1]

    def clear(self):
        if self.sems:
            self.nc.clear_and_free_semaphores(self.sems)
            self.nc.all_engine_barrier()


def chain(eng, sem):
    count = [0]

    def link(ins):
        count[0] += 1
        ins.then_inc(sem, 1)
        eng.wait_ge(sem, count[0])

    return link


def settle(eng, sem):
    eng.sem_inc(sem, 1)


def make_identity(nc, ident):
    with ExitStack() as ctx:
        m = Memory(nc, ctx, "ident")
        zeroed = m.sem("zeroed")
        block = ctx.enter_context(nc.Block())

        @block.gpsimd
        def _(pool):
            pool.memset(ident[:, :], 0.0).then_inc(zeroed, 1)
            pool.wait_ge(zeroed, 1)
            pool.affine_select(out=ident[:, :], in_=ident[:, :], compare_op=ALU.not_equal, fill=1.0,
                               base=0, pattern=[[-1, P]], channel_multiplier=1)


def load_rows(nc, x, xs):
    with ExitStack() as ctx:
        m = Memory(nc, ctx, "loadx")
        loaded = m.sem("loaded")
        block = ctx.enter_context(nc.Block())

        @block.sync
        def _(sp):
            sp.dma_start(xs[:, :, :], x[0].rearrange("(t p) d -> p t d", p=P)).then_inc(loaded, 16)
            sp.wait_ge(loaded, 16)


def store_rows(nc, xs, out):
    with ExitStack() as ctx:
        m = Memory(nc, ctx, "storex")
        stored = m.sem("stored")
        block = ctx.enter_context(nc.Block())

        @block.sync
        def _(sp):
            sp.dma_start(out[0].rearrange("(t p) d -> p t d", p=P), xs[:, :, :]).then_inc(stored, 16)
            sp.wait_ge(stored, 16)


def mask_rows(nc, mask0, mask1, mask3, padneg, kmask, kst):
    with ExitStack() as ctx:
        m = Memory(nc, ctx, "mask")
        m0, m1 = m.sb("m0", [KT, P], I32), m.sb("m1", [KT, P], I32)
        m3 = m.sb("m3", [KT, P], I32)
        add = m.sb("add", [KT, LAYERS, P])
        mid, low = m.sb("mid", [KT, LAYERS, P]), m.sb("low", [KT, LAYERS, P])
        rows = m.sb("rows", [KT, LAYERS, 6, P], BF16)
        loaded, step, rows_ready = m.sem("loaded"), m.sem("step"), m.sem("rows_ready")
        rows_stored, copied = m.sem("rows_stored"), m.sem("copied")
        block = ctx.enter_context(nc.Block())

        @block.sync
        def _(sp):
            sp.dma_start(m0[:, :], mask0.rearrange("(t p) -> t p", p=P)).then_inc(loaded, 16)
            sp.dma_start(m1[:, :], mask1.rearrange("(t p) -> t p", p=P)).then_inc(loaded, 16)
            sp.dma_start(m3[:, :], mask3.rearrange("(t p) -> t p", p=P)).then_inc(loaded, 16)
            sp.dma_start(add[:, 2, :], padneg.rearrange("(t p) -> t p", p=P)).then_inc(loaded, 16)
            sp.wait_ge(rows_ready, 1)
            for layer in range(LAYERS):
                sp.dma_start(kmask[layer].rearrange("r (t c) -> t r c", c=P),
                             rows[:, layer, :, :]).then_inc(rows_stored, 16)
            sp.wait_ge(rows_stored, 16 * LAYERS)
            with sp.Fori(0, H) as h:
                for layer in range(LAYERS):
                    sp.dma_start(kst[layer, :, ds(h, 1), AUX:ROWS, :].rearrange("b o r c -> (b o) r c"),
                                 kmask[layer].rearrange("r (b c) -> b r c", c=BK)).then_inc(copied, 16)
            sp.wait_ge(copied, 16 * H * LAYERS)

        @block.vector
        def _(dve):
            link = chain(dve, step)
            link(dve.memset(rows[:, :, :, :], 1.0))
            dve.wait_ge(loaded, 64)
            link(dve.tensor_scalar(add[:, 0, :], m0[:, :], 0.0, NEG0, ALU.is_equal, ALU.mult))
            link(dve.tensor_scalar(add[:, 1, :], m1[:, :], NEG1, None, ALU.mult))
            link(dve.tensor_scalar(add[:, 3, :], m3[:, :], NEG1, None, ALU.mult))
            link(dve.tensor_copy(rows[:, :, 0, :], add[:, :, :]))
            link(dve.tensor_tensor(mid[:, :, :], add[:, :, :], rows[:, :, 0, :], ALU.subtract))
            link(dve.tensor_copy(rows[:, :, 2, :], mid[:, :, :]))
            link(dve.tensor_tensor(low[:, :, :], mid[:, :, :], rows[:, :, 2, :], ALU.subtract))
            dve.tensor_copy(rows[:, :, 4, :], low[:, :, :]).then_inc(rows_ready, 1)


def context_keys_values(nc, ctxT, wk, bk, wv, bv, valid, mask3t, kst, vst):
    with ExitStack() as ctx:
        m = Memory(nc, ctx, "kv")
        c_all = m.sb("c_all", [P, KPAD])
        cur = m.sb("cur", [P, BK])
        wk_sb, wv_sb = m.sb("wk", [P, LAYERS, D]), m.sb("wv", [P, LAYERS * D])
        bk_sb, bv_sb = m.sb("bk", [P, LAYERS]), m.sb("bv", [P, LAYERS * D])
        valid_sb, valid3, m3, keep3 = (m.sb("valid", [P, KT]), m.sb("valid3", [P, KT]),
                                       m.sb("m3", [P, KT], I32), m.sb("keep3", [P, KT]))
        ones = m.sb("ones", [P, TB, H])
        kf, rest = m.sb("kf", [P, LAYERS, BK]), m.sb("rest", [P, LAYERS, BK])
        parts = m.sb("parts", [P, LAYERS, NPROD, BK], BF16)
        va = m.sb("va", [P, LAYERS, TB, H, VW])
        kps, vps = m.ps("kps", [P, LAYERS, 512]), m.ps("vps", [P, TB, 512])
        loaded, setup, pool_settled = m.sem("loaded"), m.sem("setup"), m.sem("pool_settled")
        cur_ready, keys_done, values_done = m.sem("cur_ready"), m.sem("keys_done"), m.sem("values_done")
        keys_out, rest_ready, mid_ready, low_ready = (m.sem("keys_out"), m.sem("rest_ready"),
                                                      m.sem("mid_ready"), m.sem("low_ready"))
        va_ready, keys_stored, values_stored = m.sem("va_ready"), m.sem("keys_stored"), m.sem("values_stored")
        parts_free, va_free = m.sem("parts_free"), m.sem("va_free")
        KEY_STORES = 16 * LAYERS
        VALUE_STORES = 16 * LAYERS
        LOADS = 16 * (4 * LAYERS + 3)
        block = ctx.enter_context(nc.Block())

        @block.sync
        def _(sp):
            sp.dma_start(c_all[:, :], ctxT).then_inc(loaded, 16)
            for layer in range(LAYERS):
                sp.dma_start(wk_sb[:, layer, :], wk[layer]).then_inc(loaded, 16)
                sp.dma_start(wv_sb[:, layer * D:(layer + 1) * D], wv[layer]).then_inc(loaded, 16)
                sp.dma_start(bk_sb[:, layer:layer + 1], bk[layer].unsqueeze(1)).then_inc(loaded, 16)
                sp.dma_start(bv_sb[:, layer * D:(layer + 1) * D],
                             bv[layer].partition_broadcast(P)).then_inc(loaded, 16)
            sp.dma_start(valid_sb[:, :], valid).then_inc(loaded, 16)
            sp.dma_start(m3[:, :], mask3t).then_inc(loaded, 16)
            sp.sem_inc(parts_free, 1)
            sp.sem_inc(va_free, 1)
            with sp.Fori(0, NB) as b:
                sp.wait_ge(low_ready, b + 1)
                for layer in range(LAYERS):
                    dst = kst[layer, ds(b, 1), :, 0:AUX, :].rearrange("o h (d s) c -> (o h) d (s c)", s=NPROD)
                    sp.dma_start(dst, parts[:, layer, :, :].rearrange("p s c -> p (s c)")).then_inc(keys_stored, 16)
                sp.wait_ge(va_ready, b + 1)
                for layer in range(LAYERS):
                    dst = vst[layer, :, ds(b * TB, TB), :, :].rearrange("p t h w -> p (t h w)")
                    sp.dma_start(dst, va[:, layer, :, :, :].rearrange("p t h w -> p (t h w)")).then_inc(
                        values_stored, 16)
                sp.wait_ge(keys_stored, KEY_STORES * (b + 1))
                sp.sem_inc(parts_free, 1)
                sp.wait_ge(values_stored, VALUE_STORES * (b + 1))
                sp.sem_inc(va_free, 1)

        @block.tensor
        def _(pe):
            pe.wait_ge(loaded, LOADS)
            with pe.Fori(0, NB) as b:
                pe.wait_ge(cur_ready, b + 1)
                pe.wait_ge(keys_out, b + 1)
                for layer in range(LAYERS):
                    last = pe.matmul(kps[:, layer, 0:BK], wk_sb[:, layer, :], cur[:, :], start=True, stop=True)
                last.then_inc(keys_done, 1)
                for t in range(TB):
                    last = pe.matmul(vps[:, t, :], cur[:, t * P:(t + 1) * P], wv_sb[:, :], start=True, stop=True)
                last.then_inc(values_done, 1)

        @block.scalar
        def _(act):
            act.wait_ge(loaded, LOADS)
            act.sem_inc(keys_out, 1)
            with act.Fori(0, NB) as b:
                act.wait_ge(keys_done, b + 1)
                act.wait_ge(parts_free, b + 1)
                for layer in range(LAYERS):
                    act.activation(kf[:, layer, :], kps[:, layer, 0:BK], ACT.Identity,
                                   bias=bk_sb[:, layer:layer + 1])
                    last = act.activation(parts[:, layer, 0, :], kps[:, layer, 0:BK], ACT.Identity,
                                          bias=bk_sb[:, layer:layer + 1])
                last.then_inc(keys_out, 1)

        @block.gpsimd
        def _(pool):
            with pool.Fori(0, NB) as b:
                pool.wait_ge(rest_ready, b + 1)
                settle(pool, pool_settled)
                pool.tensor_copy(parts[:, :, 1, :], rest[:, :, :]).then_inc(mid_ready, 1)

        @block.vector
        def _(dve):
            link = chain(dve, setup)
            dve.wait_ge(loaded, LOADS)
            link(dve.tensor_scalar(keep3[:, :], m3[:, :], 0.0, None, ALU.is_equal))
            link(dve.tensor_tensor(valid3[:, :], keep3[:, :], valid_sb[:, :], ALU.mult))
            link(dve.memset(ones[:, :, :], 1.0))
            with dve.Fori(0, NB) as b:
                dve.tensor_copy(cur[:, :], c_all[:, ds(b * BK, BK)]).then_inc(cur_ready, 1)
                dve.wait_ge(keys_out, b + 2)
                dve.tensor_tensor(rest[:, :, :], kf[:, :, :], parts[:, :, 0, :], ALU.subtract).then_inc(rest_ready, 1)
                dve.tensor_copy(parts[:, :, 3, :], parts[:, :, 0, :])
                dve.tensor_copy(parts[:, :, 5, :], parts[:, :, 0, :])
                dve.wait_ge(mid_ready, b + 1)
                dve.tensor_copy(parts[:, :, 4, :], parts[:, :, 1, :])
                dve.tensor_tensor(parts[:, :, 2, :], rest[:, :, :], parts[:, :, 1, :],
                                  ALU.subtract).then_inc(low_ready, 1)
                dve.wait_ge(values_done, b + 1)
                dve.wait_ge(va_free, b + 1)
                for t in range(TB):
                    for layer in range(LAYERS):
                        dve.scalar_tensor_tensor(
                            out=va[:, layer, t, :, 0:HD],
                            in0=bv_sb[:, layer * D:(layer + 1) * D].rearrange("p (h d) -> p h d", h=H),
                            scalar=valid_sb[:, ds(b * TB + t, 1)],
                            in1=vps[:, t, layer * D:(layer + 1) * D].rearrange("p (h d) -> p h d", h=H),
                            op0=ALU.mult, op1=ALU.add)
                        last = dve.tensor_scalar(va[:, layer, t, :, HD:VW], ones[:, t, :].unsqueeze(2),
                                                 (valid3 if layer == 3 else valid_sb)[:, ds(b * TB + t, 1)],
                                                 None, ALU.mult)
                last.then_inc(va_ready, 1)


def norm_transpose(nc, xs, ident, xT, tag):
    with ExitStack() as ctx:
        m = Memory(nc, ctx, tag)
        stats, aggr = m.sb("stats", [P, NT, 6]), m.sb("aggr", [P, NT, 2])
        eps, std, rstd = m.sb("eps", [P, 1]), m.sb("std", [P, NT, 1]), m.sb("rstd", [P, NT, 1])
        xn = m.sb("xn", [P, NT, D])
        tp = m.ps("tp", [P, NT, P])
        step, var_ready, std_ready = m.sem("step"), m.sem("var_ready"), m.sem("std_ready")
        normed, turned = m.sem("normed"), m.sem("turned")
        block = ctx.enter_context(nc.Block())

        @block.vector
        def _(dve):
            link = chain(dve, step)
            dve.memset(eps[:, :], EPS)
            for t in range(NT):
                last = dve.bn_stats(stats[:, t, :], xs[:, t, :])
            link(last)
            for t in range(NT):
                last = dve.bn_aggr(aggr[:, t, :], stats[:, t, :])
            last.then_inc(var_ready, 1)
            dve.wait_ge(std_ready, 1)
            link(dve.reciprocal(rstd[:, :, :], std[:, :, :]))
            for t in range(NT):
                dve.tensor_scalar(xn[:, t, :], xs[:, t, :], aggr[:, t, 0:1], rstd[:, t, :],
                                  ALU.subtract, ALU.mult).then_inc(normed, 1)

        @block.scalar
        def _(act):
            act.wait_ge(var_ready, 1)
            act.activation(std[:, :, :], aggr[:, :, 1:2], ACT.Sqrt, bias=eps[:, 0:1]).then_inc(std_ready, 1)
            for half in range(2):
                act.wait_ge(turned, half + 1)
                act.copy(xT[:, half * 512:(half + 1) * 512],
                         tp[:, half * 4:half * 4 + 4, :].rearrange("p t c -> p (t c)"))

        @block.tensor
        def _(pe):
            for t in range(NT):
                pe.wait_ge(normed, t + 1)
                last = pe.transpose(tp[:, t, :], xn[:, t, :], ident[:, :])
                if t % 4 == 3:
                    last.then_inc(turned, 1)


def queries(nc, xT, wq, bq, scale, qst, tag):
    with ExitStack() as ctx:
        m = Memory(nc, ctx, tag)
        w, bias = m.sb("w", [P, D]), m.sb("bias", [P, 1])
        qf, rest = m.sb("qf", [P, N]), m.sb("rest", [P, N])
        parts = m.sb("parts", [P, NPROD, N], BF16)
        aux = m.sb("aux", [H, 3, 2, N], BF16)
        ps = m.ps("ps", [P, N])
        loaded, done, step, ready, stored = (m.sem("loaded"), m.sem("done"), m.sem("step"),
                                             m.sem("ready"), m.sem("stored"))
        aux_ready = m.sem("aux_ready")
        block = ctx.enter_context(nc.Block())

        @block.sync
        def _(sp):
            sp.dma_start(w[:, :], wq).then_inc(loaded, 16)
            sp.dma_start(bias[:, :], bq.unsqueeze(1)).then_inc(loaded, 16)
            sp.wait_ge(aux_ready, 2)
            sp.dma_start(qst[:, AUX:ROWS, :], aux[:, :, :, :].rearrange("h a b n -> h (a b) n")).then_inc(stored, 16)
            sp.wait_ge(ready, 1)
            sp.dma_start(qst[:, 0:AUX, :].rearrange("h (d s) n -> h d (s n)", s=NPROD),
                         parts[:, :, :].rearrange("p s n -> p (s n)")).then_inc(stored, 16)
            sp.wait_ge(stored, 32)

        @block.gpsimd
        def _(pool):
            pool.memset(aux[:, :, 0, :], 1.0).then_inc(aux_ready, 1)
            pool.memset(aux[:, :, 1, :], 0.0).then_inc(aux_ready, 1)

        @block.tensor
        def _(pe):
            pe.wait_ge(loaded, 32)
            for half in range(2):
                last = pe.matmul(ps[:, half * 512:(half + 1) * 512], w[:, :], xT[:, half * 512:(half + 1) * 512],
                                 start=True, stop=True)
            last.then_inc(done, 1)

        @block.vector
        def _(dve):
            link = chain(dve, step)
            dve.wait_ge(loaded, 32)
            dve.wait_ge(done, 1)
            link(dve.tensor_scalar(qf[:, :], ps[:, :], bias[:, 0:1], scale, ALU.add, ALU.mult))
            link(dve.tensor_copy(parts[:, 0, :], qf[:, :]))
            dve.tensor_copy(parts[:, 1, :], parts[:, 0, :])
            dve.tensor_copy(parts[:, 2, :], parts[:, 0, :])
            link(dve.tensor_tensor(rest[:, :], qf[:, :], parts[:, 0, :], ALU.subtract))
            link(dve.tensor_copy(parts[:, 3, :], rest[:, :]))
            dve.tensor_copy(parts[:, 4, :], parts[:, 3, :])
            dve.tensor_tensor(parts[:, 5, :], rest[:, :], parts[:, 3, :], ALU.subtract).then_inc(ready, 1)


def row_max(nc, kst_l, qst, top, tag):
    BANKS = 4
    CH = BANKS * 512
    NCH = -(-KPAD // CH)
    assert NCH % 2 == 0
    with ExitStack() as ctx:
        m = Memory(nc, ctx, tag)
        kb = [m.sb(f"kb{i}", [ROWS, NB, BK], BF16) for i in range(2)]
        qb = [m.sb(f"qb{i}", [ROWS, N], BF16) for i in range(2)]
        partial = m.sb("partial", [P, 2, NCH])
        score = [m.ps(f"score{i}", [P, CH]) for i in range(2)]
        k_loaded = [m.sem(f"k_loaded{i}") for i in range(2)]
        settled = m.sem("settled")
        scored, reduced, part_ready, top_ready = (m.sem("scored"), m.sem("reduced"), m.sem("part_ready"),
                                                  m.sem("top_ready"))
        block = ctx.enter_context(nc.Block())

        @block.sync
        def _(sp):
            def load(h, par):
                sp.dma_start(kb[par][:, :, :], kst_l[:, ds(h, 1), 0:ROWS, :].rearrange(
                    "b o r c -> (o r) b c")).then_inc(k_loaded[par], 16)
                sp.dma_start(qb[par][:, :], qst[ds(h, 1), 0:ROWS, :].rearrange(
                    "o r n -> (o r) n")).then_inc(k_loaded[par], 16)

            load(0, 0)
            load(1, 1)
            with sp.Fori(1, H // 2) as hp:
                for par in range(2):
                    sp.wait_ge(scored, hp * (2 * NT * NCH) + (par - 1) * NT * NCH)
                    load(hp * 2 + par, par)

        @block.tensor
        def _(pe):
            with pe.Fori(0, H // 2) as hp:
                for par in range(2):
                    keys = kb[par][:, :, :].rearrange("r b c -> r (b c)")
                    pe.wait_ge(k_loaded[par], hp * 32 + 32)
                    settle(pe, settled)
                    with pe.Fori(0, NT) as t:
                        for c in range(NCH):
                            pe.wait_ge(reduced, (hp * 2 + par) * (NT * NCH) + t * NCH + (c + 1))
                            settle(pe, settled)
                            for k in range(c * CH, min(c * CH + CH, KPAD), 512):
                                n = min(512, KPAD - k)
                                last = pe.matmul(score[c % 2][:, k - c * CH:k - c * CH + n],
                                                 qb[par][:, ds(t * P, P)], keys[:, k:k + n], start=True, stop=True)
                            last.then_inc(scored, 1)

        @block.vector
        def _(dve):
            dve.sem_inc(reduced, 2)
            with dve.Fori(0, H * NT // 2) as u:
                for half in range(2):
                    for c in range(NCH):
                        dve.wait_ge(scored, u * (2 * NCH) + half * NCH + (c + 1))
                        n = min(CH, KPAD - c * CH)
                        dve.tensor_reduce(partial[:, half, c:c + 1], score[c % 2][:, 0:n], AX,
                                          ALU.max).then_inc(reduced, 1)
                    dve.wait_ge(reduced, u * (2 * NCH) + (half * NCH + NCH + 2))
                    dve.tensor_reduce(top[:, ds(u * 2 + half, 1)], partial[:, half, :], AX,
                                      ALU.max).then_inc(top_ready, 1)


TOPK = 32
ROUNDS = TOPK // 8 + 1


def row_threshold(nc, kst_l, qst, top, ident, tag):
    BANKS = 3
    CH = BANKS * 512
    NCH = -(-KPAD // CH)
    CT = CH // P
    UNITS = H * NT
    LINKS = 2 * ROUNDS - 1
    SLACK = 5e-7
    FLOOR = 100.0
    with ExitStack() as ctx:
        m = Memory(nc, ctx, tag)
        kb = [m.sb(f"kb{i}", [ROWS, NB, BK], BF16) for i in range(2)]
        qb = [m.sb(f"qb{i}", [ROWS, N], BF16) for i in range(2)]
        rows = [m.sb(f"rows{i}", [P, KPAD]) for i in range(2)]
        cand = [m.sb(f"cand{i}", [P, KT, 8]) for i in range(2)]
        work = m.sb("work", [P, KT, 8])
        best = [m.sb(f"best{i}", [P, ROUNDS * 8]) for i in range(2)]
        edge = m.sb("edge", [P, 3, UNITS + 1])
        eighth, flag = m.sb("eighth", [P, 1]), [m.sb(f"flag{i}", [P, 1]) for i in range(2)]
        any_flag, taken = m.sb("any_flag", [1, 1]), m.sb("taken", [1, 1], I32)
        size, slack = m.sb("size", [P, 2, UNITS]), m.sb("slack", [P, UNITS])
        score = [m.ps(f"score{i}", [P, CH]) for i in range(2)]
        flags = m.ps("flags", [1, P])
        k_loaded = [m.sem(f"k_loaded{i}") for i in range(2)]
        settled, dve_settled = m.sem("settled"), m.sem("dve_settled")
        scored, copied, rows_free = m.sem("scored"), m.sem("copied"), m.sem("rows_free")
        cand_ready, merged, flagged, turned = m.sem("cand_ready"), m.sem("merged"), m.sem("flagged"), m.sem("turned")
        decided, searched, edge_ready, step = (m.sem("decided"), m.sem("searched"), m.sem("edge_ready"),
                                               m.sem("step"))
        eighth_ready = m.sem("eighth_ready")
        block = ctx.enter_context(nc.Block())

        @block.sync
        def _(sp):
            def load(h, par):
                sp.dma_start(kb[par][:, :, :], kst_l[:, ds(h, 1), 0:ROWS, :].rearrange(
                    "b o r c -> (o r) b c")).then_inc(k_loaded[par], 16)
                sp.dma_start(qb[par][:, :], qst[ds(h, 1), 0:ROWS, :].rearrange(
                    "o r n -> (o r) n")).then_inc(k_loaded[par], 16)

            load(0, 0)
            load(1, 1)
            with sp.Fori(1, H // 2) as hp:
                for par in range(2):
                    sp.wait_ge(scored, hp * (2 * NT * NCH) + (par - 1) * NT * NCH)
                    load(hp * 2 + par, par)

        @block.tensor
        def _(pe):
            with pe.Fori(0, H // 2) as hp:
                for par in range(2):
                    keys = kb[par][:, :, :].rearrange("r b c -> r (b c)")
                    pe.wait_ge(k_loaded[par], hp * 32 + 32)
                    settle(pe, settled)
                    with pe.Fori(0, NT // 2) as t2:
                        for half in range(2):
                            unit = hp * (2 * NT) + t2 * 2 + (par * NT + half)
                            for c in range(NCH):
                                pe.wait_ge(copied, unit * NCH + (c + 1))
                                settle(pe, settled)
                                for k in range(c * CH, min(c * CH + CH, KPAD), 512):
                                    n = min(512, KPAD - k)
                                    last = pe.matmul(score[(half * NCH + c) % 2][:, k - c * CH:k - c * CH + n],
                                                     qb[par][:, ds(t2 * (2 * P) + half * P, P)], keys[:, k:k + n],
                                                     start=True, stop=True)
                                last.then_inc(scored, 1)
                            pe.wait_ge(flagged, unit + 1)
                            settle(pe, settled)
                            pe.transpose(flags[0:1, :], flag[1 - half][:, :], ident[:, :]).then_inc(turned, 1)
            pe.wait_ge(flagged, UNITS + 1)
            pe.transpose(flags[0:1, :], flag[1][:, :], ident[:, :]).then_inc(turned, 1)

        @block.scalar
        def _(act):
            act.sem_inc(copied, 2)
            with act.Fori(0, UNITS // 2) as u2:
                for half in range(2):
                    unit = u2 * 2 + half
                    act.wait_ge(rows_free, unit + 1)
                    for c in range(NCH):
                        act.wait_ge(scored, unit * NCH + (c + 1))
                        n = min(CH, KPAD - c * CH)
                        act.copy(rows[half][:, c * CH:c * CH + n],
                                 score[(half * NCH + c) % 2][:, 0:n]).then_inc(copied, 1)

        @block.vector
        def _(dve):
            def search(values, scratch, half, sem, start):
                n = 0
                src = values
                for r in range(ROUNDS):
                    eight = best[half][:, r * 8:r * 8 + 8]
                    dve.max(eight, src).then_inc(sem, 1)
                    n += 1
                    dve.wait_ge(sem, start + n)
                    settle(dve, dve_settled)
                    if r < ROUNDS - 1:
                        dve.match_replace(scratch, eight, src, -3e38).then_inc(sem, 1)
                        n += 1
                        src = scratch
                        dve.wait_ge(sem, start + n)
                        settle(dve, dve_settled)

            def decide(v, half):
                dve.wait_ge(turned, v + 1)
                dve.tensor_reduce(any_flag[:, :], flags[0:1, :], AX, ALU.max).then_inc(decided, 1)
                dve.wait_ge(decided, v * 2 + 1)
                dve.tensor_copy(taken[:, :], any_flag[:, :]).then_inc(decided, 1)
                dve.wait_ge(decided, v * 2 + 2)
                settle(dve, dve_settled)
                value = dve.value_load(taken[0:1, 0:1], min_val=0, max_val=1)
                with dve.If(value > 0):
                    search(rows[half][:, :], rows[half][:, :], half, searched, v * LINKS)
                with dve.Else():
                    dve.sem_inc(searched, LINKS)
                for i, place in enumerate((0, TOPK - 1, TOPK)):
                    last = dve.tensor_copy(edge[:, i, ds(v, 1)], best[half][:, place:place + 1])
                last.then_inc(rows_free, 1)

            link = chain(dve, step)
            dve.sem_inc(rows_free, 1)
            dve.memset(best[1][:, :], 0.0)
            link(dve.memset(flag[1][:, :], 0.0))
            dve.sem_inc(flagged, 1)
            with dve.Fori(0, UNITS // 2) as u2:
                for half in range(2):
                    unit = u2 * 2 + half
                    for s in range(KT):
                        if s % CT == 0:
                            dve.wait_ge(copied, unit * NCH + (s // CT + 3))
                            settle(dve, dve_settled)
                        last = dve.max(cand[half][:, s, :], rows[half][:, s * P:(s + 1) * P])
                        if s == 2 * CT - 1:
                            decide(unit, 1 - half)
                    last.then_inc(cand_ready, 1)
                    dve.wait_ge(cand_ready, unit + 1)
                    dve.wait_ge(rows_free, unit + 1)
                    settle(dve, dve_settled)
                    dve.tensor_reduce(eighth[:, :], cand[half][:, :, 7], AX, ALU.max).then_inc(eighth_ready, 1)
                    search(cand[half][:, :, :].rearrange("p t e -> p (t e)"),
                           work[:, :, :].rearrange("p t e -> p (t e)"), half, merged, unit * LINKS)
                    dve.wait_ge(eighth_ready, unit + 1)
                    dve.tensor_tensor(flag[half][:, :], eighth[:, :], best[half][:, TOPK:TOPK + 1],
                                      ALU.is_ge).then_inc(flagged, 1)
            decide(UNITS, 1)
            dve.wait_ge(rows_free, UNITS + 2)
            largest, inside, outside = (edge[:, i, 1:UNITS + 1] for i in range(3))
            for i, value in enumerate((largest, inside)):
                link(dve.scalar_tensor_tensor(out=size[:, i, :], in0=value, scalar=-1.0, in1=value, op0=ALU.mult,
                                              op1=ALU.max))
            link(dve.tensor_tensor(slack[:, :], size[:, 0, :], size[:, 1, :], ALU.add))
            link(dve.scalar_tensor_tensor(out=slack[:, :], in0=slack[:, :], scalar=-SLACK, in1=inside, op0=ALU.mult,
                                          op1=ALU.add))
            link(dve.tensor_tensor(size[:, 0, :], inside, outside, ALU.add))
            link(dve.tensor_scalar(size[:, 0, :], size[:, 0, :], 0.5, None, ALU.mult))
            link(dve.tensor_tensor(size[:, 0, :], size[:, 0, :], slack[:, :], ALU.min))
            link(dve.tensor_scalar(size[:, 1, :], largest, -FLOOR, None, ALU.add))
            dve.tensor_tensor(top[:, :], size[:, 0, :], size[:, 1, :], ALU.max)


def set_shift(nc, top, qst, ident, tag):
    with ExitStack() as ctx:
        m = Memory(nc, ctx, tag)
        neg, rest = m.sb("neg", [P, P]), m.sb("rest", [P, P])
        parts = m.sb("parts", [P, 3, P], BF16)
        tp = m.ps("tp", [P, P])
        turned, step, ready, stored = m.sem("turned"), m.sem("step"), m.sem("ready"), m.sem("stored")
        block = ctx.enter_context(nc.Block())

        @block.tensor
        def _(pe):
            pe.transpose(tp[:, :], top[:, :], ident[:, :]).then_inc(turned, 1)

        @block.vector
        def _(dve):
            link = chain(dve, step)
            dve.wait_ge(turned, 1)
            link(dve.tensor_scalar(neg[:, :], tp[:, :], -1.0, None, ALU.mult))
            link(dve.tensor_copy(parts[:, 0, :], neg[:, :]))
            link(dve.tensor_tensor(rest[:, :], neg[:, :], parts[:, 0, :], ALU.subtract))
            link(dve.tensor_copy(parts[:, 1, :], rest[:, :]))
            dve.tensor_tensor(parts[:, 2, :], rest[:, :], parts[:, 1, :], ALU.subtract).then_inc(ready, 1)

        @block.sync
        def _(sp):
            sp.wait_ge(ready, 1)
            for i in range(3):
                sp.dma_start(qst[:, AUX + 2 * i + 1, :].rearrange("h (t c) -> h t c", c=P),
                             parts[:, i, :]).then_inc(stored, 16)
            sp.wait_ge(stored, 48)


def attend(nc, kst_l, vst_l, qst, ident, att, tag, topk=False):
    NU = NG * NQC
    with ExitStack() as ctx:
        m = Memory(nc, ctx, tag)
        kb = [m.sb(f"kb{i}", [P, G, BK], BF16) for i in range(2)]
        qb = [m.sb(f"qb{i}", [P, G, QC], BF16) for i in range(2)]
        v_all = m.sb("v_all", [P, KT, H, VW])
        vb = [m.sb(f"vb{i}", [P, TB, G, VW]) for i in range(2)]
        prob = [m.sb(f"prob{i}", [P, 2, QC]) for i in range(4)]
        kept = [m.sb(f"kept{i}", [P, 2, QC]) for i in range(4)] if topk else prob
        ob = m.sb("ob", [VW, G, QC])
        rden = m.sb("rden", [P, QC // P, G, 1])
        score = [m.ps(f"score{i}", [P, 2, QC]) for i in range(2)]
        acc = [m.ps(f"acc{i}", [P, QC]) for i in range(NQC)]
        tp = m.ps("tp", [P, QC // P, G, VW])
        q_loaded = [m.sem(f"q_loaded{i}") for i in range(2)]
        k_loaded = [m.sem(f"k_loaded{i}") for i in range(2)]
        cleared, v_loaded, vb_ready = m.sem("cleared"), m.sem("v_loaded"), m.sem("vb_ready")
        settled, pool_settled = m.sem("settled"), m.sem("pool_settled")
        scored, exped, kept_ready, summed = m.sem("scored"), m.sem("exped"), m.sem("kept_ready"), m.sem("summed")
        ob_ready, turned, tp_free, rden_ready = m.sem("ob_ready"), m.sem("turned"), m.sem("tp_free"), m.sem("rden_ready")
        if topk:
            lower, bias_ready = m.sb("lower", [P, 1]), m.sem("bias_ready")
        CREDIT = TB + 1
        block = ctx.enter_context(nc.Block())

        def blocks(eng, one_block):
            with eng.Fori(0, NG) as g:
                for qc in range(NQC):
                    for b in (0, 1):
                        one_block(g, qc, b, (qc + b) % 2)
                    with eng.Fori(1, NB // 2) as bp:
                        for b in range(2):
                            one_block(g, qc, bp * 2 + b, (qc + b) % 2)
                    one_block(g, qc, NB - 1, (qc + NB - 1) % 2)

        def number(g, qc, b):
            return g * (NQC * NB) + (b + qc * NB)

        def before_last_used(n):
            return n * TB + (CREDIT - TB)

        @block.sync
        def _(sp):
            sp.dma_start(v_all[:, :, :, :], vst_l).then_inc(v_loaded, 16)
            sp.wait_ge(cleared, 4)

            def one_block(g, qc, b, par):
                n = number(g, qc, b)
                sp.wait_ge(summed, before_last_used(n))
                if isinstance(b, int) and b == 0:
                    sp.dma_start(qb[qc][0:ROWS, :, :], qst[ds(g * G, G), 0:ROWS, qc * QC:(qc + 1) * QC].rearrange(
                        "j r c -> r j c")).then_inc(q_loaded[qc], 16)
                sp.dma_start(kb[par][0:ROWS, :, :], kst_l[ds(b, 1), ds(g * G, G), 0:ROWS, :].rearrange(
                    "o j r c -> (o r) j c")).then_inc(k_loaded[par], 16)

            blocks(sp, one_block)

        @block.gpsimd
        def _(pool):
            for i in range(2):
                pool.memset(kb[i][:, :, :], 0.0).then_inc(cleared, 1)
                pool.memset(qb[i][:, :, :], 0.0).then_inc(cleared, 1)
            pool.wait_ge(v_loaded, 16)

            def one_block(g, qc, b, par):
                n = number(g, qc, b)
                pool.wait_ge(summed, before_last_used(n))
                settle(pool, pool_settled)
                pool.tensor_copy(vb[par][:, :, :, :], v_all[:, ds(b * TB, TB), ds(g * G, G), :]).then_inc(vb_ready, 1)

            blocks(pool, one_block)

        @block.tensor
        def _(pe):
            def scores(k, qc, par, t, pair):
                pe.wait_ge(kept_ready if topk else exped, k * 2 + (pair + 1))
                for half in range(2):
                    j = 2 * pair + half
                    last = pe.matmul(score[pair][:, half, :], kb[par][:, j, t * P:(t + 1) * P],
                                     qb[qc][:, j, :], start=True, stop=True)
                last.then_inc(scored, 1)

            def sums(k, qc, par, t, first, final):
                pe.wait_ge(kept_ready if topk else exped, k * 2 + 4)
                for j in range(G):
                    last = pe.matmul(acc[qc][32 * j:32 * j + VW, :], vb[par][:, t, j, :],
                                     kept[2 * ((par + t) % 2) + j // 2][:, j % 2, :],
                                     start=first, stop=final, skip_group_check=True)
                last.then_inc(summed, 1)

            def one_block(g, qc, b, par):
                n = number(g, qc, b)
                known = isinstance(b, int)
                first, final = known and b == 0, known and b == NB - 1
                if first:
                    pe.wait_ge(q_loaded[qc], g * 16 + 16)
                    pe.wait_ge(ob_ready, g * NQC + (qc + 1))
                pe.wait_ge(k_loaded[par], fill_count(g, qc, b, par))
                pe.wait_ge(vb_ready, n + 1)
                for t in range(TB):
                    for pair in range(2):
                        scores(n * TB + t, qc, par, t, pair)
                    if t:
                        sums(n * TB + (t - 1), qc, par, t - 1, first and t == 1, False)
                sums(n * TB + (TB - 1), qc, par, TB - 1, False, final)
                if final:
                    pe.wait_ge(ob_ready, g * NQC + (qc + 3))
                    pe.wait_ge(tp_free, g * NQC + (qc + 1))
                    settle(pe, settled)
                    for c in range(QC // P):
                        for j in range(G):
                            last = pe.transpose(tp[:, c, j, :], ob[:, j, c * P:(c + 1) * P], ident[0:VW, 0:VW])
                    last.then_inc(turned, 1)

            def fill_count(g, qc, b, par):
                if isinstance(b, int):
                    return g * (NB * 16) + ((b + qc * NB) // 2 + 1) * 16
                odd = (par - qc) % 2
                return g * (NB * 16) + (b - odd) * 8 + ((odd + qc * NB) // 2 + 1) * 16

            pe.wait_ge(cleared, 4)
            pe.sem_inc(summed, CREDIT)
            blocks(pe, one_block)

        @block.scalar
        def _(act):
            act.sem_inc(exped, 2)
            if topk:
                act.wait_ge(bias_ready, 1)
            with act.Fori(0, NU * KT // 12) as i:
                for t in range(12):
                    for pair in range(2):
                        act.wait_ge(scored, i * 24 + (2 * t + pair + 1))
                        act.wait_ge(summed, i * 12 + (t + CREDIT - 1))
                        act.activation(prob[2 * (t % 2) + pair][:, :, :], score[pair][:, :, :],
                                       ACT.Exp, bias=lower[:, 0:1] if topk else 0.0).then_inc(exped, 1)

        @block.vector
        def _(dve):
            dve.sem_inc(tp_free, 1)
            dve.sem_inc(ob_ready, 2)
            if topk:
                dve.memset(lower[:, :], -LOWER).then_inc(bias_ready, 1)
                dve.sem_inc(kept_ready, 2)

            def keep(k, parity):
                for pair in range(2):
                    dve.wait_ge(exped, k * 2 + (pair + 3))
                    buf = 2 * parity + pair
                    for j in range(2):
                        last = dve.scalar_tensor_tensor(out=kept[buf][:, j, :], in0=score[pair][:, j, :], scalar=0.0,
                                                        in1=prob[buf][:, j, :], op0=ALU.is_ge, op1=ALU.mult)
                    last.then_inc(kept_ready, 1)

            with dve.Fori(0, NG) as g:
                for qc in range(NQC):
                    u = g * NQC + qc
                    if topk:
                        keep(u * KT, qc)
                        with dve.Fori(0, KT // 2) as i:
                            keep(u * KT + i * 2 + 1, 1 - qc)
                            keep(u * KT + i * 2 + 2, qc)
                    dve.wait_ge(summed, u * KT + (KT + CREDIT))
                    dve.wait_ge(tp_free, u + 1)
                    for j in range(G):
                        last = dve.tensor_copy(ob[:, j, :], acc[qc][32 * j:32 * j + VW, :])
                    last.then_inc(ob_ready, 1)
                    dve.wait_ge(turned, u + 1)
                    dve.reciprocal(rden[:, :, :, :], tp[:, :, :, HD:VW]).then_inc(rden_ready, 1)
                    dve.wait_ge(rden_ready, u + 1)
                    for c in range(QC // P):
                        last = dve.tensor_tensor(
                            att[:, qc * (QC // P) + c, ds(g * (G * HD), G * HD)].rearrange("p (j d) -> p j d", d=HD),
                            tp[:, c, :, 0:HD], rden[:, c, :, :].to_broadcast([P, G, HD]), ALU.mult)
                    last.then_inc(tp_free, 1)


def project(nc, att, wo, bo, gate, xs, ident, tag):
    with ExitStack() as ctx:
        m = Memory(nc, ctx, tag)
        w, bias, gt = m.sb("w", [P, D]), m.sb("bias", [P, D]), m.sb("gt", [P, 1])
        th = m.sb("th", [P, 1])
        bg = m.sb("bg", [P, D])
        aT = m.sb("aT", [P, NT, P])
        upd = m.sb("upd", [P, NT, D])
        tp, y = m.ps("tp", [P, NT, P]), m.ps("y", [P, NT, D])
        loaded, gate_ready, turned, aT_ready, done, step = (
            m.sem("loaded"), m.sem("gate_ready"), m.sem("turned"), m.sem("aT_ready"), m.sem("done"), m.sem("step"))
        block = ctx.enter_context(nc.Block())

        @block.sync
        def _(sp):
            sp.dma_start(w[:, :], wo).then_inc(loaded, 16)
            sp.dma_start(bias[:, :], bo.partition_broadcast(P)).then_inc(loaded, 16)
            sp.dma_start(gt[:, :], gate.partition_broadcast(P)).then_inc(loaded, 16)

        @block.tensor
        def _(pe):
            pe.wait_ge(loaded, 48)
            for t in range(NT):
                last = pe.transpose(tp[:, t, :], att[:, t, :], ident[:, :])
                if t % 4 == 3:
                    last.then_inc(turned, 1)
            for t in range(NT):
                if t % 4 == 0:
                    pe.wait_ge(aT_ready, t // 4 + 1)
                last = pe.matmul(y[:, t, :], aT[:, t, :], w[:, :], start=True, stop=True)
                if t % 4 == 3:
                    last.then_inc(done, 1)

        @block.scalar
        def _(act):
            act.wait_ge(loaded, 48)
            act.activation(th[:, :], gt[:, :], ACT.Tanh).then_inc(gate_ready, 1)
            for half in range(2):
                act.wait_ge(turned, half + 1)
                act.copy(aT[:, half * 4:half * 4 + 4, :], tp[:, half * 4:half * 4 + 4, :]).then_inc(aT_ready, 1)

        @block.vector
        def _(dve):
            link = chain(dve, step)
            dve.wait_ge(loaded, 48)
            dve.wait_ge(gate_ready, 1)
            for t in range(NT):
                if t % 4 == 0:
                    dve.wait_ge(done, t // 4 + 1)
                link(dve.tensor_tensor(upd[:, t, :], y[:, t, :], bias[:, :], ALU.add))
                dve.scalar_tensor_tensor(out=xs[:, t, :], in0=upd[:, t, :], scalar=th[:, 0:1], in1=xs[:, t, :],
                                         op0=ALU.mult, op1=ALU.add)


def route_sigmoid(nc, xT, gate_w, bias, ident, comb, tag):
    E, ROUTE_SCALE = L0_E, 2.826
    with ExitStack() as ctx:
        m = Memory(nc, ctx, tag)
        w, b = m.sb("w", [P, E]), m.sb("b", [P, E])
        score, sel, rep, picked = (m.sb("score", [P, NT, E]), m.sb("sel", [P, NT, E]),
                                   m.sb("rep", [P, NT, E]), m.sb("picked", [P, NT, E]))
        best = m.sb("best", [P, NT, 8])
        total, inv = m.sb("total", [P, NT, 1]), m.sb("inv", [P, NT, 1])
        combT = m.sb("combT", [E, N])
        one = m.sb("one", [1, N])
        logit, tp = m.ps("logit", [P, NT, E]), m.ps("tp", [E, N])
        loaded, logits_done, scores_ready, step, ready, turned, out_ready, stored = (
            m.sem("loaded"), m.sem("logits_done"), m.sem("scores_ready"), m.sem("step"), m.sem("ready"),
            m.sem("turned"), m.sem("out_ready"), m.sem("stored"))
        block = ctx.enter_context(nc.Block())

        @block.sync
        def _(sp):
            sp.dma_start(w[:, :], gate_w).then_inc(loaded, 16)
            sp.dma_start(b[:, :], bias.partition_broadcast(P)).then_inc(loaded, 16)
            sp.wait_ge(out_ready, 2)
            sp.dma_start(comb[0:E, :], combT[:, :]).then_inc(stored, 16)
            sp.dma_start(comb[E:E + 1, :], one[:, :]).then_inc(stored, 16)
            sp.wait_ge(stored, 32)

        @block.tensor
        def _(pe):
            pe.wait_ge(loaded, 32)
            for t in range(NT):
                last = pe.matmul(logit[:, t, :], xT[:, t * P:(t + 1) * P], w[:, :], start=True, stop=True)
            last.then_inc(logits_done, 1)
            pe.wait_ge(ready, 1)
            for t in range(NT):
                last = pe.transpose(tp[:, t * P:(t + 1) * P], picked[:, t, :], ident[:, :])
            last.then_inc(turned, 1)

        @block.scalar
        def _(act):
            act.wait_ge(logits_done, 1)
            act.activation(score[:, :, :], logit[:, :, :], ACT.Sigmoid).then_inc(scores_ready, 1)
            act.wait_ge(turned, 1)
            act.copy(combT[:, :], tp[:, :]).then_inc(out_ready, 1)

        @block.vector
        def _(dve):
            link = chain(dve, step)
            dve.memset(one[:, :], 1.0).then_inc(out_ready, 1)
            dve.wait_ge(loaded, 32)
            dve.wait_ge(scores_ready, 1)
            link(dve.tensor_tensor(sel[:, :, :], score[:, :, :], b[:, :].unsqueeze(1).to_broadcast([P, NT, E]), ALU.add))
            for t in range(NT):
                last = dve.max(best[:, t, :], sel[:, t, :])
            link(last)
            for t in range(NT):
                last = dve.match_replace(rep[:, t, :], best[:, t, :], sel[:, t, :], -3e38)
            link(last)
            link(dve.tensor_tensor(picked[:, :, :], rep[:, :, :], sel[:, :, :], ALU.not_equal))
            link(dve.tensor_tensor(picked[:, :, :], picked[:, :, :], score[:, :, :], ALU.mult))
            link(dve.tensor_reduce(total[:, :, 0], picked[:, :, :], AX, ALU.add))
            link(dve.reciprocal(inv[:, :, :], total[:, :, :]))
            link(dve.tensor_scalar(inv[:, :, :], inv[:, :, :], ROUTE_SCALE, None, ALU.mult))
            dve.tensor_tensor(picked[:, :, :], picked[:, :, :], inv[:, :, :].to_broadcast([P, NT, E]),
                              ALU.mult).then_inc(ready, 1)


def route_top2(nc, xT, router_w, ident, comb, tag):
    E, DUMMY = L3_E, -3e38
    with ExitStack() as ctx:
        m = Memory(nc, ctx, tag)
        w = m.sb("w", [P, E])
        logit, rep = m.sb("logit", [P, NT, 2 * E]), m.sb("rep", [P, NT, 2 * E])
        best, two = m.sb("best", [P, NT, 8]), m.sb("two", [P, NT, 8])
        diff, ex, picked = m.sb("diff", [P, NT, E]), m.sb("ex", [P, NT, E]), m.sb("picked", [P, NT, E])
        total, inv = m.sb("total", [P, NT, 1]), m.sb("inv", [P, NT, 1])
        combT = m.sb("combT", [E, N])
        ps, tp = m.ps("ps", [P, NT, E]), m.ps("tp", [E, N])
        loaded, logits_done, step, diff_ready, ex_ready, ready, turned, out_ready, stored = (
            m.sem("loaded"), m.sem("logits_done"), m.sem("step"), m.sem("diff_ready"), m.sem("ex_ready"),
            m.sem("ready"), m.sem("turned"), m.sem("out_ready"), m.sem("stored"))
        block = ctx.enter_context(nc.Block())

        @block.sync
        def _(sp):
            sp.dma_start(w[:, :], router_w).then_inc(loaded, 16)
            sp.wait_ge(out_ready, 1)
            sp.dma_start(comb[0:E, :], combT[:, :]).then_inc(stored, 16)
            sp.wait_ge(stored, 16)

        @block.tensor
        def _(pe):
            pe.wait_ge(loaded, 16)
            for t in range(NT):
                last = pe.matmul(ps[:, t, :], xT[:, t * P:(t + 1) * P], w[:, :], start=True, stop=True)
            last.then_inc(logits_done, 1)
            pe.wait_ge(ready, 1)
            for t in range(NT):
                last = pe.transpose(tp[:, t * P:(t + 1) * P], picked[:, t, :], ident[:, :])
            last.then_inc(turned, 1)

        @block.scalar
        def _(act):
            act.wait_ge(diff_ready, 1)
            act.activation(ex[:, :, :], diff[:, :, :], ACT.Exp).then_inc(ex_ready, 1)
            act.wait_ge(turned, 1)
            act.copy(combT[:, :], tp[:, :]).then_inc(out_ready, 1)

        @block.vector
        def _(dve):
            link = chain(dve, step)
            link(dve.memset(logit[:, :, :], DUMMY))
            link(dve.memset(two[:, :, :], DUMMY))
            dve.wait_ge(logits_done, 1)
            link(dve.tensor_copy(logit[:, :, 0:E], ps[:, :, :]))
            for t in range(NT):
                last = dve.max(best[:, t, :], logit[:, t, 0:E])
            link(last)
            link(dve.tensor_copy(two[:, :, 0:2], best[:, :, 0:2]))
            dve.tensor_tensor(diff[:, :, :], logit[:, :, 0:E], best[:, :, 0:1].to_broadcast([P, NT, E]),
                              ALU.subtract).then_inc(diff_ready, 1)
            for t in range(NT):
                last = dve.match_replace(rep[:, t, :], two[:, t, :], logit[:, t, :], -1e38)
            link(last)
            link(dve.tensor_tensor(picked[:, :, :], rep[:, :, 0:E], logit[:, :, 0:E], ALU.not_equal))
            dve.wait_ge(ex_ready, 1)
            link(dve.tensor_tensor(picked[:, :, :], picked[:, :, :], ex[:, :, :], ALU.mult))
            link(dve.tensor_reduce(total[:, :, 0], picked[:, :, :], AX, ALU.add))
            link(dve.reciprocal(inv[:, :, :], total[:, :, :]))
            dve.tensor_tensor(picked[:, :, :], picked[:, :, :], inv[:, :, :].to_broadcast([P, NT, E]),
                              ALU.mult).then_inc(ready, 1)


def experts(nc, xT, comb, w_gate, w_up, w_down, E, C, yT, tag):
    S = 2 * C
    HALF = N // 2
    with ExitStack() as ctx:
        m = Memory(nc, ctx, tag)
        wg = [m.sb(f"wg{i}", [P, C, P]) for i in range(2)]
        wu = [m.sb(f"wu{i}", [P, C, P]) for i in range(2)]
        wd = [m.sb(f"wd{i}", [P, C, D]) for i in range(2)]
        cb = [m.sb(f"cb{i}", [P, N]) for i in range(2)]
        sil = [m.sb(f"sil{i}", [P, HALF]) for i in range(2)]
        act_up = [m.sb(f"act_up{i}", [P, HALF]) for i in range(2)]
        hid = [m.sb(f"hid{i}", [P, HALF]) for i in range(2)]
        zero = m.sb("zero", [P, P])
        gp = [m.ps(f"gp{i}", [P, HALF]) for i in range(2)]
        up = [m.ps(f"up{i}", [P, HALF]) for i in range(2)]
        yp = m.ps("yp", [P, 2, HALF])
        loaded = [m.sem(f"loaded{i}") for i in range(2)]
        zeroed, projected, sil_ready, product_ready, hid_ready, summed, out_ready = (
            m.sem("zeroed"), m.sem("projected"), m.sem("sil_ready"), m.sem("product_ready"), m.sem("hid_ready"),
            m.sem("summed"), m.sem("out_ready"))
        CREDIT = S + 2
        block = ctx.enter_context(nc.Block())

        def each_expert(eng, one):
            with eng.Fori(0, E // 2) as ep:
                for par in range(2):
                    one(ep * 2 + par, par)
            if E % 2:
                one(E - 1, 0)

        @block.sync
        def _(sp):
            def one(e, par):
                sp.wait_ge(summed, e * S + (CREDIT - S))
                sp.dma_start(wg[par][:, :, :], w_gate[ds(e, 1)].rearrange("o p (c i) -> (o p) c i", c=C)).then_inc(loaded[par], 16)
                sp.dma_start(wu[par][:, :, :], w_up[ds(e, 1)].rearrange("o p (c i) -> (o p) c i", c=C)).then_inc(loaded[par], 16)
                sp.dma_start(wd[par][:, :, :], w_down[ds(e, 1)].rearrange("o (c p) d -> p (o c) d", p=P)).then_inc(loaded[par], 16)
                sp.dma_start(cb[par][:, :], comb[ds(e, 1), :].partition_broadcast(P).rearrange(
                    "p o n -> p (o n)")).then_inc(loaded[par], 16)

            each_expert(sp, one)

        def load_count(e, par):
            return 64 * (E // 2 + 1) if isinstance(e, int) else (e - par) * 32 + 64

        @block.tensor
        def _(pe):
            def one(e, par):
                pe.wait_ge(loaded[par], load_count(e, par))
                for i in range(S + 1):
                    if i < S:
                        c, half, buf = i // 2, i % 2, i % 2
                        pe.wait_ge(product_ready, e * S + (i + 1))
                        cols = slice(half * HALF, (half + 1) * HALF)
                        pe.matmul(gp[buf][:, :], wg[par][:, c, :], xT[:, cols], start=True, stop=True)
                        pe.matmul(up[buf][:, :], wu[par][:, c, :], xT[:, cols], start=True, stop=True).then_inc(projected, 1)
                    if i >= 1:
                        c, half, buf = (i - 1) // 2, (i - 1) % 2, (i - 1) % 2
                        pe.wait_ge(hid_ready, e * S + i)
                        pe.matmul(yp[:, half, :], wd[par][:, c, :], hid[buf][:, :], start=False, stop=False,
                                  skip_group_check=True).then_inc(summed, 1)

            pe.wait_ge(zeroed, 1)
            for half in range(2):
                pe.matmul(yp[:, half, :], zero[:, :], xT[:, half * HALF:(half + 1) * HALF], start=True, stop=False,
                          skip_group_check=True)
            pe.sem_inc(summed, CREDIT)
            each_expert(pe, one)
            for half in range(2):
                last = pe.matmul(yp[:, half, :], zero[:, :], xT[:, half * HALF:(half + 1) * HALF], start=False,
                                 stop=True, skip_group_check=True)
            last.then_inc(out_ready, 1)

        @block.scalar
        def _(act):
            def one(e, par):
                for i in range(S):
                    act.wait_ge(projected, e * S + (i + 1))
                    act.wait_ge(product_ready, e * S + (i + 1))
                    act.activation(sil[i % 2][:, :], gp[i % 2][:, :], ACT.Silu).then_inc(sil_ready, 1)

            each_expert(act, one)
            act.wait_ge(out_ready, 1)
            for half in range(2):
                act.copy(yT[:, half * HALF:(half + 1) * HALF], yp[:, half, :])

        @block.vector
        def _(dve):
            dve.memset(zero[:, :], 0.0).then_inc(zeroed, 1)
            dve.sem_inc(product_ready, 2)

            def one(e, par):
                for i in range(S):
                    half = i % 2
                    dve.wait_ge(sil_ready, e * S + (i + 1))
                    dve.tensor_tensor(act_up[i % 2][:, :], sil[i % 2][:, :], up[i % 2][:, :],
                                      ALU.mult).then_inc(product_ready, 1)
                    dve.wait_ge(product_ready, e * S + (i + 3))
                    dve.wait_ge(summed, e * S + (i - 1 + CREDIT))
                    if i == 0:
                        dve.wait_ge(loaded[par], load_count(e, par))
                    dve.tensor_tensor(hid[i % 2][:, :], act_up[i % 2][:, :],
                                      cb[par][:, half * HALF:(half + 1) * HALF], ALU.mult).then_inc(hid_ready, 1)

            each_expert(dve, one)


def add_gated(nc, yT, gate, xs, ident, tag):
    with ExitStack() as ctx:
        m = Memory(nc, ctx, tag)
        gt, th = m.sb("gt", [P, 1]), m.sb("th", [P, 1])
        tp = m.ps("tp", [P, NT, P])
        loaded, gate_ready, turned = m.sem("loaded"), m.sem("gate_ready"), m.sem("turned")
        block = ctx.enter_context(nc.Block())

        @block.sync
        def _(sp):
            sp.dma_start(gt[:, :], gate.partition_broadcast(P)).then_inc(loaded, 16)

        @block.scalar
        def _(act):
            act.wait_ge(loaded, 16)
            act.activation(th[:, :], gt[:, :], ACT.Tanh).then_inc(gate_ready, 1)

        @block.tensor
        def _(pe):
            for t in range(NT):
                last = pe.transpose(tp[:, t, :], yT[:, t * P:(t + 1) * P], ident[:, :])
                if t % 4 == 3:
                    last.then_inc(turned, 1)

        @block.vector
        def _(dve):
            dve.wait_ge(gate_ready, 1)
            for t in range(NT):
                if t % 4 == 0:
                    dve.wait_ge(turned, t // 4 + 1)
                dve.scalar_tensor_tensor(out=xs[:, t, :], in0=tp[:, t, :], scalar=th[:, 0:1], in1=xs[:, t, :],
                                         op0=ALU.mult, op1=ALU.add)


ROUND = 12582912.0


def quantized_ffn(nc, xT, w_inT, b_in, w_out, b_out, ident, yT, tag):
    F = 512
    C, HALF = F // P, N // 2
    with ExitStack() as ctx:
        m = Memory(nc, ctx, tag)
        wi, wo = m.sb("wi", [P, C, D]), m.sb("wo", [P, C, D])
        bi, bo = m.sb("bi", [P, C]), m.sb("bo", [P, 1])
        wq, wqT = m.sb("wq", [P, C, D]), m.sb("wqT", [P, C, P], BF16)
        ws = m.sb("ws", [P, C, D])
        wmax, wstep, wmul = m.sb("wmax", [P, 2, C]), m.sb("wstep", [P, 2, C]), m.sb("wmul", [P, 2, C])
        ones = m.sb("ones", [1, P])
        xmax, row, xstep, xmul, xall = (m.sb("xmax", [P, 1]), m.sb("row", [1, 1]), m.sb("xstep", [P, 2]),
                                        m.sb("xmul", [P, 2]), m.sb("xall", [P, 1]))
        hmax = m.sb("hmax", [P, 1])
        xq, xhi, xlo = m.sb("xq", [P, N]), m.sb("xhi", [P, N], BF16), m.sb("xlo", [P, N], BF16)
        fs = m.sb("fs", [P, C])
        hid = m.sb("hid", [P, C, N])
        small = m.ps("small", [P, P])
        bc = m.ps("bc", [P, 1])
        wt = m.ps("wt", [P, C, P])
        hp = m.ps("hp", [P, 2, HALF])
        yp = m.ps("yp", [P, 2, HALF])
        loaded, step, asked, given, hid_ready, hp_ready, y_ready, ready = (
            m.sem("loaded"), m.sem("step"), m.sem("asked"), m.sem("given"), m.sem("hid_ready"),
            m.sem("hp_ready"), m.sem("y_ready"), m.sem("ready"))
        block = ctx.enter_context(nc.Block())

        @block.sync
        def _(sp):
            sp.dma_start(wi[:, :, :], w_inT.rearrange("(c p) d -> p c d", p=P)).then_inc(loaded, 16)
            sp.dma_start(wo[:, :, :], w_out.rearrange("(c p) d -> p c d", p=P)).then_inc(loaded, 16)
            sp.dma_start(bi[:, :], b_in).then_inc(loaded, 16)
            sp.dma_start(bo[:, :], b_out.unsqueeze(1)).then_inc(loaded, 16)

        @block.vector
        def _(dve):
            link = chain(dve, step)
            link(dve.memset(ones[:, :], 1.0))

            def global_max(column, i, before):
                dve.sem_inc(asked, 1)
                dve.wait_ge(given, before + 1)
                link(dve.tensor_reduce(row[:, :], small[0:1, :], AX, ALU.max))
                dve.sem_inc(asked, 1)
                dve.wait_ge(given, before + 2)
                link(dve.tensor_scalar(xall[:, :], bc[:, :], 1e-8, None, ALU.max))
                link(dve.tensor_scalar(xmul[:, i:i + 1], xall[:, :], 1.0 / 32767.0, None, ALU.mult))
                link(dve.reciprocal(xstep[:, i:i + 1], xall[:, :]))
                link(dve.tensor_scalar(xstep[:, i:i + 1], xstep[:, i:i + 1], 32767.0, None, ALU.mult))

            link(dve.tensor_reduce(xmax[:, :], xT[:, :], AX, ALU.max, apply_absolute_value=True))
            global_max(xmax, 0, 0)
            link(dve.tensor_scalar(xq[:, :], xT[:, :], xstep[:, 0:1], ROUND, ALU.mult, ALU.add))
            link(dve.tensor_scalar(xq[:, :], xq[:, :], -ROUND, 32767.0, ALU.add, ALU.min))
            link(dve.tensor_scalar(xq[:, :], xq[:, :], -32768.0, None, ALU.max))
            link(dve.tensor_copy(xhi[:, :], xq[:, :]))
            link(dve.tensor_tensor(xlo[:, :], xq[:, :], xhi[:, :], ALU.subtract))
            dve.wait_ge(loaded, 64)
            for i, w in enumerate((wi, wo)):
                link(dve.tensor_reduce(wmax[:, i, :], w[:, :, :], AX, ALU.max, apply_absolute_value=True))
            link(dve.tensor_scalar(wmax[:, :, :], wmax[:, :, :], 1e-8, None, ALU.max))
            link(dve.tensor_scalar(wmul[:, :, :], wmax[:, :, :], 1.0 / 127.0, None, ALU.mult))
            link(dve.reciprocal(wstep[:, :, :], wmax[:, :, :]))
            link(dve.tensor_scalar(wstep[:, :, :], wstep[:, :, :], 127.0, None, ALU.mult))
            for i, (w, q) in enumerate(((wi, wq), (wo, ws))):
                for c in range(C):
                    link(dve.tensor_scalar(q[:, c, :], w[:, c, :], wstep[:, i, c:c + 1], ROUND, ALU.mult, ALU.add))
                link(dve.tensor_scalar(q[:, :, :], q[:, :, :], -ROUND, 127.0, ALU.add, ALU.min))
                link(dve.tensor_scalar(q[:, :, :], q[:, :, :], -128.0, None, ALU.max))
            for c in range(C):
                link(dve.tensor_scalar(ws[:, c, :], ws[:, c, :], wmul[:, 1, c:c + 1], None, ALU.mult))
            link(dve.tensor_scalar(fs[:, :], wmul[:, 0, :], xmul[:, 0:1], None, ALU.mult))
            dve.sem_inc(asked, 1)
            dve.wait_ge(given, 3)
            dve.tensor_copy(wqT[:, :, :], wt[:, :, :]).then_inc(ready, 1)
            dve.wait_ge(hid_ready, 2 * C)
            link(dve.tensor_reduce(hmax[:, :], hid[:, :, :].rearrange("p c n -> p (c n)"), AX, ALU.max,
                                   apply_absolute_value=True))
            global_max(hmax, 1, 3)
            for c in range(C):
                link(dve.tensor_scalar(hid[:, c, :], hid[:, c, :], xstep[:, 1:2], ROUND, ALU.mult, ALU.add))
                link(dve.tensor_scalar(hid[:, c, :], hid[:, c, :], -ROUND, 32767.0, ALU.add, ALU.min))
                dve.tensor_scalar(hid[:, c, :], hid[:, c, :], -32768.0, None, ALU.max).then_inc(ready, 1)
            dve.wait_ge(y_ready, 1)
            for half in range(2):
                dve.tensor_scalar(yT[:, half * HALF:(half + 1) * HALF], yp[:, half, :], xmul[:, 1:2], bo[:, 0:1],
                                  ALU.mult, ALU.add)

        @block.tensor
        def _(pe):
            pe.wait_ge(asked, 1)
            pe.transpose(small[0:1, :], xmax[:, :], ident[:, :]).then_inc(given, 1)
            pe.wait_ge(asked, 2)
            pe.matmul(bc[:, :], ones[:, :], row[:, :], start=True, stop=True).then_inc(given, 1)
            pe.wait_ge(asked, 3)
            for c in range(C):
                last = pe.transpose(wt[:, c, :], wq[:, c, :], ident[:, :])
            last.then_inc(given, 1)
            pe.wait_ge(ready, 1)
            for c in range(C):
                for half in range(2):
                    if c:
                        pe.wait_ge(hid_ready, 2 * (c - 1) + half + 1)
                    cols = slice(half * HALF, (half + 1) * HALF)
                    pe.matmul(hp[:, half, :], wqT[:, c, :], xhi[:, cols], start=True, stop=False)
                    pe.matmul(hp[:, half, :], wqT[:, c, :], xlo[:, cols], start=False, stop=True).then_inc(hp_ready, 1)
            pe.wait_ge(asked, 4)
            pe.transpose(small[0:1, :], hmax[:, :], ident[:, :]).then_inc(given, 1)
            pe.wait_ge(asked, 5)
            pe.matmul(bc[:, :], ones[:, :], row[:, :], start=True, stop=True).then_inc(given, 1)
            for c in range(C):
                pe.wait_ge(ready, c + 2)
                for half in range(2):
                    last = pe.matmul(yp[:, half, :], ws[:, c, :], hid[:, c, half * HALF:(half + 1) * HALF],
                                     start=(c == 0), stop=(c == C - 1))
            last.then_inc(y_ready, 1)

        @block.scalar
        def _(act):
            act.wait_ge(loaded, 64)
            for c in range(C):
                for half in range(2):
                    act.wait_ge(hp_ready, 2 * c + half + 1)
                    act.activation(hid[:, c, half * HALF:(half + 1) * HALF], hp[:, half, :], ACT.Gelu,
                                   bias=bi[:, c:c + 1], scale=fs[:, c:c + 1]).then_inc(hid_ready, 1)



DEPTH = 6
LH, LD = 16, 64
PAIRS = LH // 2
WIN = 32
TQ = P - WIN
LT = -(-N // TQ)
NPAD = WIN + LT * TQ
FC = 3
NORM_FLOOR = 1e-12


def local_transformer(nc, zT, a, ident):
    HALF = N // 2
    STEPS = 4 * PAIRS
    R0 = 6
    G4 = LH // 4
    with ExitStack() as ctx:
        m = Memory(nc, ctx, "lt")
        sT = m.sb("sT", [P, NPAD])
        cs = m.sb("cs", [P, 4, N])
        qsc = m.sb("qsc", [P, DEPTH, 4])
        gain, shift, bias2 = m.sb("gain", [P, DEPTH]), m.sb("shift", [P, DEPTH]), m.sb("bias2", [P, DEPTH])
        bias1 = m.sb("bias1", [P, DEPTH, 2, FC])
        eps = m.sb("eps", [P, 1])
        head_ones, mean_ones = m.sb("head_ones", [P, P]), m.sb("mean_ones", [P, P])
        band = m.sb("band", [P, 2, 4, P], BF16)
        identb = m.sb("identb", [P, TQ], BF16)
        w4 = [m.sb(f"w4{i}", [P, 4, P]) for i in range(2)]
        wv, wo = m.sb("wv", [P, LH * LD]), m.sb("wo", [P, PAIRS, D])
        w1, w2 = m.sb("w1", [P, 2, FC, P]), m.sb("w2", [P, FC, D])
        sq, nrm = [m.sb(f"sq{i}", [P, HALF]) for i in range(2)], [m.sb(f"nrm{i}", [P, HALF]) for i in range(2)]
        t1, t2 = [m.sb(f"t1{i}", [P, HALF]) for i in range(2)], [m.sb(f"t2{i}", [P, HALF]) for i in range(2)]
        t3, rn = [m.sb(f"t3{i}", [P, HALF]) for i in range(2)], [m.sb(f"rn{i}", [P, HALF]) for i in range(2)]
        qk = [m.sb("qT", [P, PAIRS, NPAD]), m.sb("kT", [P, PAIRS, NPAD])]
        oT = m.sb("oT", [P, PAIRS, LT * TQ])
        q_cur, k_cur, s_cur = m.sb("q_cur", [P, PAIRS, TQ]), m.sb("k_cur", [P, PAIRS, 2, P]), m.sb("s_cur", [P, P])
        v_cur = m.sb("v_cur", [P, LH * LD])
        nmax, rsum, rinv = ([m.sb(f"{n}{i}", [TQ, 4, 1]) for i in range(2)] for n in ("nmax", "rsum", "rinv"))
        ex = [m.sb(f"ex{i}", [TQ, 4, P]) for i in range(2)]
        pT = m.sb("pT", [P, 4, TQ])
        bank = [m.ps(f"bank{i}", [P, 512]) for i in range(8)]
        S = {n: m.sem(n) for n in (
            "loaded", "table_loaded", "setup", "w4_0", "w4_1", "wvo", "w12", "shifted", "tables", "proj", "sq_ready", "normed",
            "nrm_ready", "t2_ready", "t3_ready", "rn_ready", "roped", "staged", "v_done", "v_ready", "sc_done",
            "maxed", "subbed", "exped", "rs_ready", "rinv_ready", "norm_ready", "turned", "pt_ready", "pv_done",
            "o_ready", "y_done", "z_ready", "mean_done", "xc_ready", "xsq_ready", "var_done", "std_ready",
            "rstd_ready", "xn_half", "xn_mul", "xn_ready", "h_done", "gelu_ready", "hh_ready", "f_done", "settled", "psettled", "vsettled", "asettled",
            "cleared")}
        LOADS = 16 * 7
        block = ctx.enter_context(nc.Block())
        half_cols = [slice(WIN + h * HALF, WIN + (h + 1) * HALF) for h in range(2)]

        def pairs(eng, layer, one):
            with eng.Fori(0, PAIRS // 2) as jp:
                for par in range(2):
                    one(layer, jp * 2 + par, par)

        def tiles(eng, layer, one):
            one(layer, 0)
            with eng.Fori(1, LT) as t:
                one(layer, t)

        @block.sync
        def _(sp):
            for dst, src in ((qsc[:, :, :], a["lt_qsc"]), (gain[:, :], a["lt_g"]),
                             (shift[:, :], a["lt_b"]), (bias2[:, :], a["lt_b2"]), (bias1[:, :, :, :], a["lt_b1"]),
                             (head_ones[:, :], a["lt_head_ones"]), (mean_ones[:, :], a["lt_mean_ones"])):
                sp.dma_start(dst, src).then_inc(S["loaded"], 16)
            with sp.Fori(0, DEPTH) as layer:
                sp.wait_ge(S["roped"], layer * STEPS + R0)
                sp.dma_start(cs[:, :, :], a["lt_table"]).then_inc(S["table_loaded"], 16)
                sp.wait_ge(S["y_done"], layer + 1)
                sp.dma_start(wv[:, :], a["lt_wv"][ds(layer, 1)].rearrange("o p n -> p (o n)")).then_inc(S["wvo"], 16)
                sp.dma_start(wo[:, :, :], a["lt_wo"][ds(layer, 1)].rearrange("o (j p) d -> p (o j) d", p=P)).then_inc(S["wvo"], 16)
                sp.wait_ge(S["f_done"], layer + 1)
                sp.dma_start(w1[:, :, :, :], a["lt_w1"][ds(layer, 1)].rearrange(
                    "o p (s c i) -> p (o s) c i", s=2, c=FC)).then_inc(S["w12"], 16)
                sp.dma_start(w2[:, :, :], a["lt_w2"][ds(layer, 1)].rearrange("o (c p) d -> p (o c) d", p=P)).then_inc(S["w12"], 16)

                def one(layer, j, par):
                    sp.wait_ge(S["roped"], layer * STEPS + j * 4 + (R0 - 4))
                    sp.dma_start(w4[par][:, :, :], a["lt_w4"][ds(layer, 1), ds(j, 1)].rearrange(
                        "o q p (s n) -> p (o q s) n", s=4)).then_inc(S[f"w4_{par}"], 16)

                pairs(sp, layer, one)

        @block.tensor
        def _(pe):
            pe.wait_ge(S["loaded"], LOADS)
            pe.wait_ge(S["setup"], 7)
            pe.sem_inc(S["y_done"], 1)
            pe.sem_inc(S["f_done"], 1)
            with pe.Fori(0, DEPTH) as layer:
                pe.wait_ge(S["shifted"], layer * 2 + 1)
                settle(pe, S["settled"])

                def pair(layer, j, par):
                    pe.wait_ge(S[f"w4_{par}"], layer * (PAIRS // 2 * 16) + (j - par) * 8 + 16)
                    for i in range(5):
                        n = layer * STEPS + j * 4
                        if i < 4:
                            which, half, buf = i // 2, i % 2, i % 2
                            pe.wait_ge(S["roped"], n + (i + R0 - 1))
                            pe.matmul(bank[buf][:, :], w4[par][:, 2 * which, :], sT[:, half_cols[half]], start=True, stop=True)
                            pe.matmul(bank[2 + buf][:, :], w4[par][:, 2 * which + 1, :], sT[:, half_cols[half]],
                                      start=True, stop=True).then_inc(S["proj"], 1)
                        if i >= 1:
                            buf = (i - 1) % 2
                            pe.wait_ge(S["sq_ready"], n + i)
                            pe.matmul(bank[4 + buf][:, :], head_ones[:, :], sq[buf][:, :], start=True,
                                      stop=True).then_inc(S["normed"], 1)

                pairs(pe, layer, pair)
                pe.wait_ge(S["wvo"], layer * 32 + 32)

                def tile(layer, t):
                    n = layer * LT + t
                    pe.wait_ge(S["staged"], n + 1)
                    for h in range(2):
                        last = pe.matmul(bank[h][:, :], s_cur[:, :], wv[:, h * 512:(h + 1) * 512], start=True, stop=True)
                    last.then_inc(S["v_done"], 1)
                    for i in range(G4 + 1):
                        if i < G4:
                            pe.wait_ge(S["subbed"], n * G4 + (i + 1))
                            sc = bank[2 + i % 2]
                            pe.matmul(sc[0:TQ, :], identb[:, :], band[:, 0 if isinstance(t, int) else 1, :, :].rearrange(
                                "p h c -> p (h c)"), start=True, stop=False, skip_group_check=True)
                            for q in range(2):
                                last = pe.matmul(sc[0:TQ, q * 2 * P:(q + 1) * 2 * P], q_cur[:, 2 * i + q, :],
                                                 k_cur[:, 2 * i + q, :, :].rearrange("p s c -> p (s c)"), start=False,
                                                 stop=(q == 1), skip_group_check=True)
                            last.then_inc(S["sc_done"], 1)
                        if i >= 1:
                            g = i - 1
                            pe.wait_ge(S["norm_ready"], n * G4 + (g + 1))
                            pe.wait_ge(S["pt_ready"], n * G4 + (g + 1))
                            settle(pe, S["settled"])
                            for h in range(4):
                                last = pe.transpose(bank[4][:, h * TQ:(h + 1) * TQ], ex[g % 2][:, h, :], ident[0:TQ, 0:TQ])
                            last.then_inc(S["turned"], 1)
                            pe.wait_ge(S["pt_ready"], n * G4 + (g + 2))
                            pe.wait_ge(S["v_ready"], n + 1)
                            pe.wait_ge(S["o_ready"], n * G4 + (g + 1))
                            settle(pe, S["settled"])
                            for h in range(4):
                                last = pe.matmul(bank[5][64 * (h % 2):64 * (h % 2) + 64, (h // 2) * TQ:(h // 2 + 1) * TQ],
                                                 v_cur[:, (4 * g + h) * LD:(4 * g + h + 1) * LD], pT[:, h, :],
                                                 start=True, stop=True, skip_group_check=True)
                            last.then_inc(S["pv_done"], 1)

                tiles(pe, layer, tile)
                pe.wait_ge(S["o_ready"], layer * (LT * G4) + (LT * G4 + 1))
                for half in range(2):
                    for j in range(PAIRS):
                        last = pe.matmul(bank[6 + half][:, :], wo[:, j, :], oT[:, j, half * HALF:(half + 1) * HALF],
                                         start=(j == 0), stop=(j == PAIRS - 1))
                last.then_inc(S["y_done"], 1)

                pe.wait_ge(S["shifted"], layer * 2 + 2)
                for half in range(2):
                    pe.matmul(bank[half][:, :], mean_ones[:, :], sT[:, half_cols[half]], start=True,
                              stop=True).then_inc(S["mean_done"], 1)
                for half in range(2):
                    pe.wait_ge(S["xsq_ready"], layer * 2 + (half + 1))
                    pe.matmul(bank[2 + half][:, :], mean_ones[:, :], sq[half][:, :], start=True,
                              stop=True).then_inc(S["var_done"], 1)
                pe.wait_ge(S["w12"], layer * 32 + 32)
                for i in range(2 * FC + 1):
                    n = layer * (2 * FC)
                    if i < 2 * FC:
                        c, half = i // 2, i % 2
                        if c == 0:
                            pe.wait_ge(S["xn_ready"], layer * 2 + (half + 1))
                        else:
                            pe.wait_ge(S["hh_ready"], n + (i - 1))
                        for s in range(2):
                            last = pe.matmul(bank[4 * s + half][:, :], w1[:, s, c, :], nrm[half][:, :], start=True, stop=True)
                        last.then_inc(S["h_done"], 1)
                    if i >= 1:
                        c, half = (i - 1) // 2, (i - 1) % 2
                        pe.wait_ge(S["hh_ready"], n + i)
                        last = pe.matmul(bank[6 + half][:, :], w2[:, c, :], t1[half][:, :], start=(c == 0), stop=(c == FC - 1))
                last.then_inc(S["f_done"], 1)

        @block.scalar
        def _(act):
            act.sem_inc(S["pt_ready"], 1)
            with act.Fori(0, DEPTH) as layer:
                def pair(layer, j, par):
                    n = layer * STEPS + j * 4
                    for i in range(5):
                        if i < 4:
                            act.wait_ge(S["proj"], n + (i + 1))
                            act.activation(sq[i % 2][:, :], bank[i % 2][:, :], ACT.Square).then_inc(S["sq_ready"], 1)
                        if i >= 1:
                            act.wait_ge(S["normed"], n + i)
                            act.activation(nrm[(i - 1) % 2][:, :], bank[4 + (i - 1) % 2][:, :],
                                           ACT.Sqrt).then_inc(S["nrm_ready"], 1)

                pairs(act, layer, pair)

                def tile(layer, t):
                    n = layer * LT + t
                    act.wait_ge(S["v_done"], n + 1)
                    for h in range(2):
                        last = act.copy(v_cur[:, h * 512:(h + 1) * 512], bank[h][:, :])
                    last.then_inc(S["v_ready"], 1)
                    for i in range(G4 + 2):
                        if i < G4:
                            act.wait_ge(S["subbed"], n * G4 + (i + 3))
                            act.activation(ex[i % 2][:, :, :], ex[i % 2][:, :, :], ACT.Exp).then_inc(S["exped"], 1)
                        if 1 <= i <= G4:
                            act.wait_ge(S["turned"], n * G4 + (i + 2))
                            act.copy(pT[:, :, :].rearrange("p h q -> p (h q)"), bank[4][:, 0:4 * TQ]).then_inc(S["pt_ready"], 1)

                tiles(act, layer, tile)
                for half in range(2):
                    act.wait_ge(S["xc_ready"], layer * 2 + (half + 1))
                    act.activation(sq[half][:, :], t3[half][:, :], ACT.Square).then_inc(S["xsq_ready"], 1)
                for half in range(2):
                    act.wait_ge(S["var_done"], layer * 2 + (half + 1))
                    act.activation(t2[half][:, :], bank[2 + half][:, :], ACT.Sqrt, bias=eps[:, 0:1]).then_inc(S["std_ready"], 1)
                for i in range(2 * FC):
                    c, half = i // 2, i % 2
                    act.wait_ge(S["h_done"], layer * (2 * FC) + (i + 1))
                    if c:
                        act.wait_ge(S["hh_ready"], layer * (2 * FC) + (i - 1))
                    settle(act, S["asettled"])
                    act.activation(t2[half][:, :], bank[4 + half][:, :], ACT.Gelu,
                                   bias=bias1[:, ds(layer, 1), 1, c:c + 1].rearrange("p o i -> p (o i)")).then_inc(S["gelu_ready"], 1)

        @block.gpsimd
        def _(pool):
            for ap in (sT[:, :], qk[0][:, :, :], qk[1][:, :, :]):
                pool.memset(ap, 0.0).then_inc(S["cleared"], 1)
            pool.wait_ge(S["loaded"], LOADS)
            pool.wait_ge(S["cleared"], 3)
            pool.memset(identb[:, :], 0.0).then_inc(S["setup"], 1)
            pool.memset(band[:, :, :, :], 0.0).then_inc(S["setup"], 1)
            pool.memset(eps[:, :], EPS).then_inc(S["setup"], 1)
            pool.wait_ge(S["setup"], 3)
            pool.affine_select(out=identb[:, :], in_=identb[:, :], compare_op=ALU.not_equal, fill=1.0, base=0,
                               pattern=[[-1, TQ]], channel_multiplier=1).then_inc(S["setup"], 1)
            flat = band[:, :, :, :].rearrange("p a h c -> p (a h) c")
            pool.affine_select(out=flat, in_=flat, compare_op=ALU.is_ge, fill=NEG1, base=0,
                               pattern=[[0, 8], [1, P]], channel_multiplier=-1).then_inc(S["setup"], 1)
            pool.wait_ge(S["setup"], 5)
            pool.affine_select(out=flat, in_=flat, compare_op=ALU.is_ge, fill=NEG1, base=WIN,
                               pattern=[[0, 8], [-1, P]], channel_multiplier=1).then_inc(S["setup"], 1)
            pool.wait_ge(S["setup"], 6)
            pool.memset(band[:, 0, :, 0:WIN], NEG1).then_inc(S["setup"], 1)
            pool.wait_ge(S["setup"], 7)
            with pool.Fori(0, DEPTH) as layer:
                def pair(layer, j, par):
                    for i in range(4):
                        pool.wait_ge(S["t2_ready"], layer * STEPS + j * 4 + (i + 1))
                        settle(pool, S["psettled"])
                        pool.tensor_tensor(t3[i % 2][:, :], t1[i % 2][:, :], t2[i % 2][:, :], ALU.add).then_inc(S["t3_ready"], 1)

                pairs(pool, layer, pair)
                pool.wait_ge(S["roped"], layer * STEPS + (STEPS + R0))

                def tile(layer, t):
                    n = layer * LT + t
                    pool.wait_ge(S["pv_done"], n * G4 + 1)
                    settle(pool, S["psettled"])
                    keys, queries_ = (ds(t * TQ, P), ds(t * TQ + WIN, TQ))
                    pool.tensor_copy(s_cur[:, :], sT[:, keys])
                    pool.tensor_copy(q_cur[:, :, :], qk[0][:, :, queries_])
                    for s in range(2):
                        last = pool.tensor_tensor(k_cur[:, :, s, :], qk[1][:, :, keys], head_ones[:, 64 * s:64 * s + 1].unsqueeze(
                            2).to_broadcast([P, PAIRS, P]), ALU.mult)
                    last.then_inc(S["staged"], 1)
                    for g in range(G4):
                        pool.wait_ge(S["rinv_ready"], n * G4 + (g + 1))
                        settle(pool, S["psettled"])
                        pool.tensor_tensor(ex[g % 2][:, :, :], ex[g % 2][:, :, :],
                                           rinv[g % 2][:, :, :].to_broadcast([TQ, 4, P]), ALU.mult).then_inc(S["norm_ready"], 1)

                pool.sem_inc(S["psettled"], 1)
                tiles(pool, layer, tile)

        @block.vector
        def _(dve):
            dve.wait_ge(S["loaded"], LOADS)
            dve.wait_ge(S["cleared"], 3)
            dve.sem_inc(S["roped"], R0)
            dve.sem_inc(S["subbed"], 2)
            dve.sem_inc(S["turned"], 2)
            dve.sem_inc(S["pv_done"], 1)
            dve.sem_inc(S["o_ready"], 1)
            dve.sem_inc(S["z_ready"], 1)

            def shift_tokens():
                dve.tensor_copy(sT[0:64, WIN:WIN + N], zT[0:64, :])
                dve.tensor_copy(sT[64:P, WIN + 1:WIN + N], zT[64:P, 0:N - 1]).then_inc(S["shifted"], 1)

            with dve.Fori(0, DEPTH) as layer:
                dve.wait_ge(S["z_ready"], layer * 4 + 1)
                shift_tokens()
                dve.wait_ge(S["table_loaded"], layer * 16 + 16)
                for i in range(4):
                    last = dve.tensor_scalar(cs[:, i, :], cs[:, i, :], qsc[:, ds(layer, 1), i:i + 1].rearrange(
                        "p o i -> p (o i)"), None, ALU.mult)
                last.then_inc(S["tables"], 1)
                dve.wait_ge(S["tables"], layer + 1)
                settle(dve, S["vsettled"])

                def pair(layer, j, par):
                    n = layer * STEPS + j * 4
                    for i in range(5):
                        if i < 4:
                            which, half, buf = i // 2, i % 2, i % 2
                            cols = slice(half * HALF, (half + 1) * HALF)
                            dve.wait_ge(S["sq_ready"], n + (i + 1))
                            dve.wait_ge(S["roped"], n + (i + R0 - 1))
                            dve.tensor_tensor(t1[buf][:, :], bank[buf][:, :], cs[:, 2 * which, cols], ALU.mult)
                            dve.tensor_tensor(t2[buf][:, :], bank[2 + buf][:, :], cs[:, 2 * which + 1, cols],
                                              ALU.mult).then_inc(S["t2_ready"], 1)
                        if i >= 1:
                            which, half, buf = (i - 1) // 2, (i - 1) % 2, (i - 1) % 2
                            dve.wait_ge(S["nrm_ready"], n + i)
                            dve.reciprocal(rn[buf][:, :], nrm[buf][:, :]).then_inc(S["rn_ready"], 1)
                            dve.wait_ge(S["rn_ready"], n + i)
                            dve.wait_ge(S["t3_ready"], n + i)
                            dve.scalar_tensor_tensor(
                                out=qk[which][:, ds(j, 1), half_cols[half]].rearrange("p o n -> p (o n)"),
                                in0=rn[buf][:, :], scalar=1.0 / NORM_FLOOR, in1=t3[buf][:, :], op0=ALU.min,
                                op1=ALU.mult).then_inc(S["roped"], 1)

                pairs(dve, layer, pair)

                def tile(layer, t):
                    n = layer * LT + t

                    def lower_by_max(g):
                        k = n * G4
                        dve.wait_ge(S["sc_done"], k + (g + 1))
                        dve.wait_ge(S["subbed"], k + (g + 2))
                        sc = bank[2 + g % 2][0:TQ, :].rearrange("p (h c) -> p h c", h=4)
                        dve.tensor_reduce(nmax[g % 2][:, :, 0], sc, AX, ALU.max).then_inc(S["maxed"], 1)
                        dve.wait_ge(S["maxed"], k + (g + 1))
                        dve.wait_ge(S["turned"], k + (g + 1))
                        dve.tensor_tensor(ex[g % 2][:, :, :], sc, nmax[g % 2][:, :, :].to_broadcast([TQ, 4, P]),
                                          ALU.subtract).then_inc(S["subbed"], 1)

                    def denominators(g):
                        k = n * G4
                        dve.wait_ge(S["exped"], k + (g + 1))
                        dve.tensor_reduce(rsum[g % 2][:, :, 0], ex[g % 2][:, :, :], AX, ALU.add).then_inc(S["rs_ready"], 1)
                        dve.wait_ge(S["rs_ready"], k + (g + 1))
                        dve.reciprocal(rinv[g % 2][:, :, :], rsum[g % 2][:, :, :]).then_inc(S["rinv_ready"], 1)

                    def keep(g):
                        dve.wait_ge(S["pv_done"], n * G4 + (g + 2))
                        dve.tensor_copy(oT[:, 2 * g:2 * g + 2, ds(t * TQ, TQ)],
                                        bank[5][:, 0:2 * TQ].rearrange("p (j q) -> p j q", j=2)).then_inc(S["o_ready"], 1)

                    lower_by_max(0)
                    for g in range(1, G4):
                        lower_by_max(g)
                        denominators(g - 1)
                        if g >= 2:
                            keep(g - 2)
                    denominators(G4 - 1)
                    keep(G4 - 2)
                    keep(G4 - 1)

                tiles(dve, layer, tile)
                dve.wait_ge(S["y_done"], layer + 2)
                for half in range(2):
                    cols = slice(half * HALF, (half + 1) * HALF)
                    dve.tensor_tensor(zT[:, cols], zT[:, cols], bank[6 + half][:, :], ALU.add).then_inc(S["z_ready"], 1)
                dve.wait_ge(S["z_ready"], layer * 4 + 3)
                shift_tokens()
                dve.wait_ge(S["shifted"], layer * 2 + 2)
                for half in range(2):
                    dve.wait_ge(S["mean_done"], layer * 2 + (half + 1))
                    dve.tensor_tensor(t3[half][:, :], sT[:, half_cols[half]], bank[half][:, :],
                                      ALU.subtract).then_inc(S["xc_ready"], 1)
                for half in range(2):
                    dve.wait_ge(S["std_ready"], layer * 2 + (half + 1))
                    dve.reciprocal(rn[half][:, :], t2[half][:, :]).then_inc(S["rstd_ready"], 1)
                    dve.wait_ge(S["rstd_ready"], layer * 2 + (half + 1))
                    dve.tensor_tensor(t1[half][:, :], t3[half][:, :], rn[half][:, :], ALU.mult).then_inc(S["xn_mul"], 1)
                    dve.wait_ge(S["xn_mul"], layer * 2 + (half + 1))
                    dve.tensor_scalar(nrm[half][:, :], t1[half][:, :], gain[:, ds(layer, 1)], shift[:, ds(layer, 1)],
                                      ALU.mult, ALU.add).then_inc(S["xn_ready"], 1)
                for i in range(2 * FC):
                    c, half = i // 2, i % 2
                    n = layer * (2 * FC)
                    dve.wait_ge(S["gelu_ready"], n + (i + 1))
                    if c:
                        dve.wait_ge(S["h_done"], n + (i + 1))
                    dve.scalar_tensor_tensor(out=t1[half][:, :], in0=bank[half][:, :],
                                             scalar=bias1[:, ds(layer, 1), 0, c:c + 1].rearrange("p o i -> p (o i)"),
                                             in1=t2[half][:, :], op0=ALU.add, op1=ALU.mult).then_inc(S["hh_ready"], 1)
                dve.wait_ge(S["f_done"], layer + 2)
                for half in range(2):
                    cols = slice(half * HALF, (half + 1) * HALF)
                    dve.scalar_tensor_tensor(out=zT[:, cols], in0=bank[6 + half][:, :], scalar=bias2[:, ds(layer, 1)],
                                             in1=zT[:, cols], op0=ALU.add, op1=ALU.add).then_inc(S["z_ready"], 1)


def rotary_tables():
    f = np.float32
    half = np.arange(0, LD, 2, dtype=f)
    inv_freq = f(1.0) / f(10000.0) ** (half / f(LD))
    t = np.arange(N, dtype=f)
    freqs = t[:, None] * inv_freq[None, :]
    base = (half + f(0.4 * LD)) / f(1.4 * LD)
    power = (t - f(N // 2)) / f(WIN // 2)
    scale = base[None, :] ** power[:, None]
    freqs, scale = (np.concatenate([v, v], -1).T.astype(f) for v in (freqs, scale))
    sign = np.where(np.arange(LD) < LD // 2, -1.0, 1.0).astype(f)[:, None]
    cos, sin = np.cos(freqs), np.sin(freqs) * sign
    rows = np.stack([cos * scale * f(8.0), sin * scale * f(8.0), cos / scale, sin / scale])
    return np.concatenate([rows, rows], axis=1).astype(f)


def program(nc, a, out):
    kst = nc.dram_tensor("kst", (LAYERS, NB, H, HROWS, BK), BF16, kind="Internal").ap()
    kmask = nc.dram_tensor("kmask", (LAYERS, 6, KPAD), BF16, kind="Internal").ap()
    vst = nc.dram_tensor("vst", (LAYERS, P, KT, H, VW), F32, kind="Internal").ap()
    qst = nc.dram_tensor("qst", (H, HROWS, N), BF16, kind="Internal").ap()
    comb = nc.dram_tensor("comb", (L0_E + 1, N), F32, kind="Internal").ap()
    score_scale = [1.0 / np.sqrt(D)] + 3 * [1.0 / np.sqrt(HD)]

    with ExitStack() as ctx:
        m = Memory(nc, ctx, "g")
        ident, xs, xT = m.sb("ident", [P, P]), m.sb("xs", [P, NT, D]), m.sb("xT", [P, N])

        def attention(l):
            with ExitStack() as stage:
                s = Memory(nc, stage, f"x{l}")
                top, att = s.sb("top", [P, H * NT]), s.sb("att", [P, NT, D])
                norm_transpose(nc, xs, ident, xT, f"n{l}")
                queries(nc, xT, a[f"wq{l}"], a[f"bq{l}"], float(score_scale[l]), qst, f"q{l}")
                if l == 2:
                    row_threshold(nc, kst[l], qst, top, ident, f"m{l}")
                else:
                    row_max(nc, kst[l], qst, top, f"m{l}")
                set_shift(nc, top, qst, ident, f"s{l}")
                attend(nc, kst[l], vst[l], qst, ident, att, f"a{l}", topk=(l == 2))
                project(nc, att, a[f"wo{l}"], a[f"bo{l}"], a["g_xattn"][l:l + 1], xs, ident, f"p{l}")

        def feed_forward(l):
            with ExitStack() as stage:
                s = Memory(nc, stage, f"y{l}")
                norm_transpose(nc, xs, ident, xT, f"nf{l}")
                y = xT if l == 2 else s.sb("yT", [P, N])
                if l == 0:
                    route_sigmoid(nc, xT, a["f0_gate"], a["f0_bias"], ident, comb, "r0")
                    experts(nc, xT, comb, a["f0_wg"], a["f0_wu"], a["f0_wd"], L0_E + 1, 1, y, "e0")
                elif l == 1:
                    quantized_ffn(nc, xT, a["f1_wi"], a["f1_bi"], a["f1_wo"], a["f1_bo"], ident, y, "e1")
                elif l == 2:
                    local_transformer(nc, xT, a, ident)
                else:
                    route_top2(nc, xT, a["f3_router"], ident, comb, "r3")
                    experts(nc, xT, comb, a["f3_wg"], a["f3_wu"], a["f3_wd"], L3_E, L3_C, y, "e3")
                add_gated(nc, y, a["g_ffn"][l:l + 1], xs, ident, f"u{l}")

        make_identity(nc, ident)
        load_rows(nc, a["x"], xs)
        mask_rows(nc, a["mask0"], a["mask1"], a["mask3"], a["padneg"], kmask, kst)
        context_keys_values(nc, a["ctxT"], [a[f"wk{l}"] for l in range(4)], [a[f"bk{l}"] for l in range(4)],
                            [a[f"wv{l}"] for l in range(4)], [a[f"bv{l}"] for l in range(4)], a["valid"],
                            a["mask3t"], kst, vst)
        for l in range(LAYERS):
            attention(l)
            feed_forward(l)
        store_rows(nc, xs, out)


def host_layout(i):
    pad = KPAD - S2
    f = lambda v: np.ascontiguousarray(v)
    a = {"x": f(i["x"]), "ctxT": f(np.pad(np.asarray(i["ctx_1024"])[0].T, ((0, 0), (0, pad))))}
    a["mask0"] = np.pad(np.asarray(i["mask_Bx1x1xS2_if1"]).reshape(-1), (0, pad), constant_values=1)
    a["mask1"] = np.pad(np.asarray(i["mask_Bx1x1xS2_ik0"]).reshape(-1), (0, pad), constant_values=1)
    m3 = np.pad(np.asarray(i["mask_BxS2_bf0"]).reshape(-1), (0, pad), constant_values=True).astype(np.int32)
    a["mask3"] = m3
    a["mask3t"] = f(m3.reshape(KT, P).T)
    valid = (np.arange(KPAD) < S2).astype(np.float32)
    a["valid"] = f(valid.reshape(KT, P).T)
    a["padneg"] = np.where(valid > 0, 0.0, NEG1).astype(np.float32)
    a["g_xattn"], a["g_ffn"] = np.asarray(i["g_xattn"]), np.asarray(i["g_ffn"])
    for l, (q, k, v, o) in enumerate([("Wq", "Wk", "Wv", "Wo"), ("wq", "wk", "wv", "wo"), ("Wq", "Wk", "Wv", "Wo")]):
        for n, s in zip("qkvo", (q, k, v, o)):
            w = np.asarray(i[f"L{l}_xattn_{s}"])
            a[f"w{n}{l}"] = f(w if l == 1 else w.T)
            a[f"b{n}{l}"] = np.asarray(i[f"L{l}_xattn_b{n}"])
    a["wq3"], a["wo3"] = np.asarray(i["L3_xattn_Wq"]), np.asarray(i["L3_xattn_Wout"])
    a["bq3"], a["bo3"] = np.asarray(i["L3_xattn_bq"]), np.asarray(i["L3_xattn_bout"])
    wkv, bkv = np.asarray(i["L3_xattn_Wkv"]), np.asarray(i["L3_xattn_bkv"])
    a["wk3"], a["wv3"], a["bk3"], a["bv3"] = f(wkv[:, :D]), f(wkv[:, D:]), f(bkv[:D]), f(bkv[D:])
    g = lambda n: np.asarray(i[n])
    t = lambda w: f(np.swapaxes(w, -1, -2))
    a["f0_gate"], a["f0_bias"] = t(g("L0_ffn_gate_w")), g("L0_ffn_expert_bias")
    for n, w, shared in (("wg", "w_gate", "shared_gate_w"), ("wu", "w_up", "shared_up_w"), ("wd", "w_down", "shared_down_w")):
        a[f"f0_{n}"] = t(np.concatenate([g(f"L0_ffn_{w}"), g(f"L0_ffn_{shared}")[None]]))
    a["f1_wi"], a["f1_wo"] = t(g("L1_ffn_W_in")), g("L1_ffn_W_out")
    a["f1_bi"], a["f1_bo"] = f(g("L1_ffn_b_in").reshape(-1, P).T), g("L1_ffn_b_out")
    fill = L3_C * P - g("L3_ffn_w1").shape[2]
    a["f3_router"] = g("L3_ffn_router_w")
    a["f3_wg"] = np.pad(g("L3_ffn_w1"), ((0, 0), (0, 0), (0, fill)))
    a["f3_wu"] = np.pad(g("L3_ffn_w3"), ((0, 0), (0, 0), (0, fill)))
    a["f3_wd"] = np.pad(g("L3_ffn_w2"), ((0, 0), (0, fill), (0, 0)))
    wqkv = g("L2_ffn_Wqkv")
    a["lt_table"] = f(rotary_tables().transpose(1, 0, 2))
    swap = np.concatenate([np.arange(LD // 2, LD), np.arange(LD // 2)])
    q4, k4 = (wqkv[:, :, o:o + LH * LD].reshape(DEPTH, D, PAIRS, 2, LD) for o in (0, LH * LD))
    w4 = np.stack([q4, q4[..., swap], k4, k4[..., swap]], axis=3)
    a["lt_w4"] = f(w4.transpose(0, 2, 1, 3, 4, 5).reshape(DEPTH, PAIRS, D, 4 * P))
    a["lt_wv"] = f(wqkv[:, :, 2 * LH * LD:])
    a["lt_wo"] = g("L2_ffn_Wo")
    qs, ks = g("L2_ffn_q_scale"), g("L2_ffn_k_scale")
    gains = np.stack([qs, qs[:, swap], ks, ks[:, swap]], axis=-1)
    a["lt_qsc"] = f(np.concatenate([gains, gains], axis=1).transpose(1, 0, 2))
    a["lt_g"], a["lt_b"], a["lt_b2"] = t(g("L2_ffn_ln_g")), t(g("L2_ffn_ln_b")), t(g("L2_ffn_b2"))
    inner = g("L2_ffn_W2").shape[1]
    fill = FC * P - inner
    w1 = np.pad(g("L2_ffn_W1").reshape(DEPTH, D, 2, inner), ((0, 0), (0, 0), (0, 0), (0, fill)))
    a["lt_w1"] = f(w1.reshape(DEPTH, D, 2 * FC * P))
    b1 = np.pad(g("L2_ffn_b1").reshape(DEPTH, 2, inner), ((0, 0), (0, 0), (0, fill)))
    a["lt_b1"] = f(b1.reshape(DEPTH, 2, FC, P).transpose(3, 0, 1, 2))
    a["lt_w2"] = np.pad(g("L2_ffn_W2"), ((0, 0), (0, fill), (0, 0)))
    a["lt_head_ones"] = np.kron(np.eye(2), np.ones((LD, LD))).astype(np.float32)
    a["lt_mean_ones"] = np.full((P, P), 1.0 / D, np.float32)
    return a


def kernel(**inputs):
    import concourse.bacc as bacc
    from concourse.bass_utils import run_bass_kernel_spmd

    nc = bacc.Bacc("TRN2", target_bir_lowering=False, num_devices=1)
    arrays, args = {}, {}
    for name, array in host_layout(inputs).items():
        arrays[f"in_{name}"] = array
        args[name] = nc.dram_tensor(f"in_{name}", array.shape, mybir.dt.from_np(array.dtype), kind="ExternalInput").ap()
    out = nc.dram_tensor("out_dram", (1, N, D), F32, kind="ExternalOutput").ap()
    program(nc, args, out)
    result = run_bass_kernel_spmd(nc, [arrays], core_ids=[0])
    return result.results[0]["out_dram"]
```

```python
from contextlib import ExitStack

import numpy as np

import concourse.bass as bass
from concourse import mybir

ALU = mybir.AluOpType
ACT = mybir.ActivationFunctionType
AX = mybir.AxisListType.X
F32 = mybir.dt.float32
BF16 = mybir.dt.bfloat16
I32 = mybir.dt.int32
ds = bass.ds

P = 128
D = 128
N = 1024
NT = N // P
H = 16
HD = D // H
S2 = 6404
KT = -(-S2 // P)
KPAD = KT * P
TB = 3
NB = KT // TB
BK = TB * P
assert NB * TB == KT
LAYERS = 4
K_PARTS = (0, 1, 2, 0, 1, 0)
Q_PARTS = (0, 0, 0, 1, 1, 2)
NPROD = len(K_PARTS)
AUX = NPROD * HD
ROWS = AUX + 6
HROWS = 64
NEG0 = -1e20
NEG1 = -1e30
LOWEST = -3e38
EPS = 1e-5
QC = 512
NQC = N // QC
G = 4
NG = H // G
L0_E = 16
L3_E = 8
L3_C = 3
LOWER = 50.0
VW = HD + 1


class Memory:

    def __init__(self, nc, ctx, tag):
        self.nc, self.ctx, self.tag, self.sems = nc, ctx, tag, []
        ctx.callback(self.clear)

    def sb(self, name, shape, dt=F32):
        return self.ctx.enter_context(self.nc.sbuf_tensor(f"{self.tag}_{name}", shape, dt))

    def ps(self, name, shape, dt=F32):
        return self.ctx.enter_context(self.nc.psum_tensor(f"{self.tag}_{name}", shape, dt))

    def sem(self, name):
        self.sems.append(self.nc.alloc_semaphore(f"{self.tag}_{name}"))
        return self.sems[-1]

    def clear(self):
        if self.sems:
            self.nc.clear_and_free_semaphores(self.sems)
            self.nc.all_engine_barrier()


def chain(eng, sem):
    count = [0]

    def link(ins):
        count[0] += 1
        ins.then_inc(sem, 1)
        eng.wait_ge(sem, count[0])

    return link


def settle(eng, sem):
    eng.sem_inc(sem, 1)


def make_identity(nc, ident):
    with ExitStack() as ctx:
        m = Memory(nc, ctx, "ident")
        zeroed = m.sem("zeroed")
        block = ctx.enter_context(nc.Block())

        @block.gpsimd
        def _(pool):
            pool.memset(ident[:, :], 0.0).then_inc(zeroed, 1)
            pool.wait_ge(zeroed, 1)
            pool.affine_select(out=ident[:, :], in_=ident[:, :], compare_op=ALU.not_equal, fill=1.0,
                               base=0, pattern=[[-1, P]], channel_multiplier=1)


def load_rows(nc, x, xs):
    with ExitStack() as ctx:
        m = Memory(nc, ctx, "loadx")
        loaded = m.sem("loaded")
        block = ctx.enter_context(nc.Block())

        @block.sync
        def _(sp):
            sp.dma_start(xs[:, :, :], x[0].rearrange("(t p) d -> p t d", p=P)).then_inc(loaded, 16)
            sp.wait_ge(loaded, 16)


def store_rows(nc, xs, out):
    with ExitStack() as ctx:
        m = Memory(nc, ctx, "storex")
        stored = m.sem("stored")
        block = ctx.enter_context(nc.Block())

        @block.sync
        def _(sp):
            sp.dma_start(out[0].rearrange("(t p) d -> p t d", p=P), xs[:, :, :]).then_inc(stored, 16)
            sp.wait_ge(stored, 16)


def mask_rows(nc, mask0, mask1, mask3, padneg, kmask, kst):
    with ExitStack() as ctx:
        m = Memory(nc, ctx, "mask")
        m0, m1 = m.sb("m0", [KT, P], I32), m.sb("m1", [KT, P], I32)
        m3 = m.sb("m3", [KT, P], I32)
        add = m.sb("add", [KT, LAYERS, P])
        mid, low = m.sb("mid", [KT, LAYERS, P]), m.sb("low", [KT, LAYERS, P])
        rows = m.sb("rows", [KT, LAYERS, 6, P], BF16)
        loaded, step, rows_ready = m.sem("loaded"), m.sem("step"), m.sem("rows_ready")
        rows_stored, copied = m.sem("rows_stored"), m.sem("copied")
        block = ctx.enter_context(nc.Block())

        @block.sync
        def _(sp):
            sp.dma_start(m0[:, :], mask0.rearrange("(t p) -> t p", p=P)).then_inc(loaded, 16)
            sp.dma_start(m1[:, :], mask1.rearrange("(t p) -> t p", p=P)).then_inc(loaded, 16)
            sp.dma_start(m3[:, :], mask3.rearrange("(t p) -> t p", p=P)).then_inc(loaded, 16)
            sp.dma_start(add[:, 2, :], padneg.rearrange("(t p) -> t p", p=P)).then_inc(loaded, 16)
            sp.wait_ge(rows_ready, 1)
            for layer in range(LAYERS):
                sp.dma_start(kmask[layer].rearrange("r (t c) -> t r c", c=P),
                             rows[:, layer, :, :]).then_inc(rows_stored, 16)
            sp.wait_ge(rows_stored, 16 * LAYERS)
            for layer in range(LAYERS):
                for i in range(6):
                    sp.dma_start(kst[layer, :, :, AUX + i, :], kmask[layer, i].rearrange(
                        "(b c) -> b c", c=BK).unsqueeze(1).to_broadcast([NB, H, BK])).then_inc(copied, 16)
            sp.wait_ge(copied, 16 * 6 * LAYERS)

        @block.vector
        def _(dve):
            link = chain(dve, step)
            link(dve.memset(rows[:, :, :, :], 1.0))
            dve.wait_ge(loaded, 64)
            link(dve.tensor_scalar(add[:, 0, :], m0[:, :], 0.0, NEG0, ALU.is_equal, ALU.mult))
            link(dve.tensor_scalar(add[:, 1, :], m1[:, :], NEG1, None, ALU.mult))
            link(dve.tensor_scalar(add[:, 3, :], m3[:, :], NEG1, None, ALU.mult))
            link(dve.tensor_copy(rows[:, :, 0, :], add[:, :, :]))
            link(dve.tensor_tensor(mid[:, :, :], add[:, :, :], rows[:, :, 0, :], ALU.subtract))
            link(dve.tensor_copy(rows[:, :, 2, :], mid[:, :, :]))
            link(dve.tensor_tensor(low[:, :, :], mid[:, :, :], rows[:, :, 2, :], ALU.subtract))
            dve.tensor_copy(rows[:, :, 4, :], low[:, :, :]).then_inc(rows_ready, 1)


def context_keys_values(nc, ctxT, wk, bk, wv, bv, valid, mask3t, kst, vst):
    with ExitStack() as ctx:
        m = Memory(nc, ctx, "kv")
        c_all = m.sb("c_all", [P, KPAD])
        cur = [m.sb(f"cur{i}", [P, BK]) for i in range(2)]
        wk_sb, wv_sb = m.sb("wk", [P, LAYERS, D]), m.sb("wv", [P, LAYERS * D])
        bk_sb, bv_sb = m.sb("bk", [P, LAYERS]), m.sb("bv", [P, LAYERS * D])
        valid_sb, valid3, m3, keep3 = (m.sb("valid", [P, KT]), m.sb("valid3", [P, KT]),
                                       m.sb("m3", [P, KT], I32), m.sb("keep3", [P, KT]))
        ones = m.sb("ones", [P, TB, H])
        kf, rest = [m.sb(f"kf{i}", [P, LAYERS, BK]) for i in range(2)], m.sb("rest", [P, LAYERS, BK])
        parts = [m.sb(f"parts{i}", [P, LAYERS, NPROD, BK], BF16) for i in range(2)]
        va = [m.sb(f"va{i}", [P, LAYERS, TB, H, VW]) for i in range(2)]
        kps, vps = m.ps("kps", [P, LAYERS, 512]), m.ps("vps", [P, TB, 512])
        loaded, setup, pool_settled = m.sem("loaded"), m.sem("setup"), m.sem("pool_settled")
        cur_ready, keys_done, values_done = m.sem("cur_ready"), m.sem("keys_done"), m.sem("values_done")
        keys_out, rest_ready, mid_ready, low_ready = (m.sem("keys_out"), m.sem("rest_ready"),
                                                      m.sem("mid_ready"), m.sem("low_ready"))
        va_ready = m.sem("va_ready")
        keys_stored, values_stored = ([m.sem(f"{n}_stored{i}") for i in range(2)] for n in ("keys", "values"))
        parts_free, va_free = m.sem("parts_free"), m.sem("va_free")
        KEY_STORES = 16 * LAYERS
        VALUE_STORES = 16 * LAYERS
        LOADS = 16 * (4 * LAYERS + 3)
        block = ctx.enter_context(nc.Block())

        def blocks(eng, one_block):
            with eng.Fori(0, NB // 2) as i:
                for par in range(2):
                    one_block(i * 2 + par, i, par)
            one_block(NB - 1, NB // 2, 0)

        @block.sync
        def _(sp):
            sp.dma_start(c_all[:, :], ctxT).then_inc(loaded, 16)
            for layer in range(LAYERS):
                sp.dma_start(wk_sb[:, layer, :], wk[layer]).then_inc(loaded, 16)
                sp.dma_start(wv_sb[:, layer * D:(layer + 1) * D], wv[layer]).then_inc(loaded, 16)
                sp.dma_start(bk_sb[:, layer:layer + 1], bk[layer].unsqueeze(1)).then_inc(loaded, 16)
                sp.dma_start(bv_sb[:, layer * D:(layer + 1) * D],
                             bv[layer].partition_broadcast(P)).then_inc(loaded, 16)
            sp.dma_start(valid_sb[:, :], valid).then_inc(loaded, 16)
            sp.dma_start(m3[:, :], mask3t).then_inc(loaded, 16)
            sp.sem_inc(parts_free, 1)
            sp.sem_inc(va_free, 1)
            sp.sem_inc(keys_stored[1], KEY_STORES)
            sp.sem_inc(values_stored[1], VALUE_STORES)

            def one_block(b, i, par):
                sp.wait_ge(low_ready, b + 1)
                for layer in range(LAYERS):
                    dst = kst[layer, ds(b, 1), :, 0:AUX, :].rearrange("o h (d s) c -> (o h) d (s c)", s=NPROD)
                    sp.dma_start(dst, parts[par][:, layer, :, :].rearrange("p s c -> p (s c)")).then_inc(
                        keys_stored[par], 16)
                sp.wait_ge(va_ready, b + 2)
                for layer in range(LAYERS):
                    dst = vst[layer, :, ds(b * TB, TB), :, :].rearrange("p t h w -> p (t h w)")
                    sp.dma_start(dst, va[par][:, layer, :, :, :].rearrange("p t h w -> p (t h w)")).then_inc(
                        values_stored[par], 16)
                sp.wait_ge(keys_stored[1 - par], KEY_STORES * (i + 1))
                sp.sem_inc(parts_free, 1)
                sp.wait_ge(values_stored[1 - par], VALUE_STORES * (i + 1))
                sp.sem_inc(va_free, 1)

            blocks(sp, one_block)
            sp.wait_ge(keys_stored[0], KEY_STORES * (NB // 2 + 1))
            sp.wait_ge(values_stored[0], VALUE_STORES * (NB // 2 + 1))

        @block.tensor
        def _(pe):
            pe.wait_ge(loaded, LOADS)
            pe.sem_inc(va_ready, 1)

            def one_block(b, i, par):
                pe.wait_ge(cur_ready, b + 1)
                pe.wait_ge(keys_out, b + 1)
                for layer in range(LAYERS):
                    last = pe.matmul(kps[:, layer, 0:BK], wk_sb[:, layer, :], cur[par][:, :], start=True, stop=True)
                last.then_inc(keys_done, 1)
                pe.wait_ge(va_ready, b + 1)
                for t in range(TB):
                    last = pe.matmul(vps[:, t, :], cur[par][:, t * P:(t + 1) * P], wv_sb[:, :], start=True, stop=True)
                last.then_inc(values_done, 1)

            blocks(pe, one_block)

        @block.scalar
        def _(act):
            act.wait_ge(loaded, LOADS)
            act.sem_inc(keys_out, 1)

            def one_block(b, i, par):
                act.wait_ge(keys_done, b + 1)
                act.wait_ge(parts_free, b + 1)
                for layer in range(LAYERS):
                    act.activation(kf[par][:, layer, :], kps[:, layer, 0:BK], ACT.Identity,
                                   bias=bk_sb[:, layer:layer + 1])
                    last = act.activation(parts[par][:, layer, 0, :], kps[:, layer, 0:BK], ACT.Identity,
                                          bias=bk_sb[:, layer:layer + 1])
                last.then_inc(keys_out, 1)

            blocks(act, one_block)

        @block.gpsimd
        def _(pool):
            def one_block(b, i, par):
                pool.wait_ge(rest_ready, b + 1)
                settle(pool, pool_settled)
                pool.tensor_copy(parts[par][:, :, 1, :], rest[:, :, :]).then_inc(mid_ready, 1)

            blocks(pool, one_block)

        @block.vector
        def _(dve):
            link = chain(dve, setup)
            dve.wait_ge(loaded, LOADS)
            link(dve.tensor_scalar(keep3[:, :], m3[:, :], 0.0, None, ALU.is_equal))
            link(dve.tensor_tensor(valid3[:, :], keep3[:, :], valid_sb[:, :], ALU.mult))
            link(dve.memset(ones[:, :, :], 1.0))
            dve.tensor_copy(cur[0][:, :], c_all[:, 0:BK]).then_inc(cur_ready, 1)

            def one_block(b, i, par):
                if not isinstance(b, int):
                    dve.tensor_copy(cur[1 - par][:, :], c_all[:, ds(b * BK + BK, BK)]).then_inc(cur_ready, 1)
                dve.wait_ge(keys_out, b + 2)
                dve.tensor_tensor(rest[:, :, :], kf[par][:, :, :], parts[par][:, :, 0, :],
                                  ALU.subtract).then_inc(rest_ready, 1)
                dve.tensor_copy(parts[par][:, :, 3, :], parts[par][:, :, 0, :])
                dve.tensor_copy(parts[par][:, :, 5, :], parts[par][:, :, 0, :])
                dve.wait_ge(mid_ready, b + 1)
                dve.tensor_copy(parts[par][:, :, 4, :], parts[par][:, :, 1, :])
                dve.tensor_tensor(parts[par][:, :, 2, :], rest[:, :, :], parts[par][:, :, 1, :],
                                  ALU.subtract).then_inc(low_ready, 1)
                dve.wait_ge(values_done, b + 1)
                dve.wait_ge(va_free, b + 1)
                for t in range(TB):
                    for layer in range(LAYERS):
                        dve.scalar_tensor_tensor(
                            out=va[par][:, layer, t, :, 0:HD],
                            in0=bv_sb[:, layer * D:(layer + 1) * D].rearrange("p (h d) -> p h d", h=H),
                            scalar=valid_sb[:, ds(b * TB + t, 1)],
                            in1=vps[:, t, layer * D:(layer + 1) * D].rearrange("p (h d) -> p h d", h=H),
                            op0=ALU.mult, op1=ALU.add)
                        last = dve.tensor_scalar(va[par][:, layer, t, :, HD:VW], ones[:, t, :].unsqueeze(2),
                                                 (valid3 if layer == 3 else valid_sb)[:, ds(b * TB + t, 1)],
                                                 None, ALU.mult)
                last.then_inc(va_ready, 1)

            blocks(dve, one_block)


def norm_transpose(nc, xs, ident, xT, tag):
    with ExitStack() as ctx:
        m = Memory(nc, ctx, tag)
        stats, aggr = m.sb("stats", [P, NT, 6]), m.sb("aggr", [P, NT, 2])
        eps, std, rstd = m.sb("eps", [P, 1]), m.sb("std", [P, NT, 1]), m.sb("rstd", [P, NT, 1])
        xn = m.sb("xn", [P, NT, D])
        tp = m.ps("tp", [P, NT, P])
        step, var_ready, std_ready = m.sem("step"), m.sem("var_ready"), m.sem("std_ready")
        normed, turned = m.sem("normed"), m.sem("turned")
        block = ctx.enter_context(nc.Block())

        @block.vector
        def _(dve):
            link = chain(dve, step)
            dve.memset(eps[:, :], EPS)
            for t in range(NT):
                last = dve.bn_stats(stats[:, t, :], xs[:, t, :])
            link(last)
            for t in range(NT):
                last = dve.bn_aggr(aggr[:, t, :], stats[:, t, :])
            last.then_inc(var_ready, 1)
            dve.wait_ge(std_ready, 1)
            link(dve.reciprocal(rstd[:, :, :], std[:, :, :]))
            for t in range(NT):
                dve.tensor_scalar(xn[:, t, :], xs[:, t, :], aggr[:, t, 0:1], rstd[:, t, :],
                                  ALU.subtract, ALU.mult).then_inc(normed, 1)

        @block.scalar
        def _(act):
            act.wait_ge(var_ready, 1)
            act.activation(std[:, :, :], aggr[:, :, 1:2], ACT.Sqrt, bias=eps[:, 0:1]).then_inc(std_ready, 1)
            for half in range(2):
                act.wait_ge(turned, half + 1)
                act.copy(xT[:, half * 512:(half + 1) * 512],
                         tp[:, half * 4:half * 4 + 4, :].rearrange("p t c -> p (t c)"))

        @block.tensor
        def _(pe):
            for t in range(NT):
                pe.wait_ge(normed, t + 1)
                last = pe.transpose(tp[:, t, :], xn[:, t, :], ident[:, :])
                if t % 4 == 3:
                    last.then_inc(turned, 1)


def queries(nc, xT, wq, bq, scale, qst, tag):
    with ExitStack() as ctx:
        m = Memory(nc, ctx, tag)
        w, bias = m.sb("w", [P, D]), m.sb("bias", [P, 1])
        qf, rest = m.sb("qf", [P, N]), m.sb("rest", [P, N])
        parts = m.sb("parts", [P, NPROD, N], BF16)
        aux = m.sb("aux", [H, 3, 2, N], BF16)
        ps = m.ps("ps", [P, N])
        loaded, done, step, ready, stored = (m.sem("loaded"), m.sem("done"), m.sem("step"),
                                             m.sem("ready"), m.sem("stored"))
        aux_ready = m.sem("aux_ready")
        block = ctx.enter_context(nc.Block())

        @block.sync
        def _(sp):
            sp.dma_start(w[:, :], wq).then_inc(loaded, 16)
            sp.dma_start(bias[:, :], bq.unsqueeze(1)).then_inc(loaded, 16)
            sp.wait_ge(aux_ready, 2)
            sp.dma_start(qst[:, AUX:ROWS, :], aux[:, :, :, :].rearrange("h a b n -> h (a b) n")).then_inc(stored, 16)
            sp.wait_ge(ready, 1)
            sp.dma_start(qst[:, 0:AUX, :].rearrange("h (d s) n -> h d (s n)", s=NPROD),
                         parts[:, :, :].rearrange("p s n -> p (s n)")).then_inc(stored, 16)
            sp.wait_ge(stored, 32)

        @block.gpsimd
        def _(pool):
            pool.memset(aux[:, :, 0, :], 1.0).then_inc(aux_ready, 1)
            pool.memset(aux[:, :, 1, :], 0.0).then_inc(aux_ready, 1)

        @block.tensor
        def _(pe):
            pe.wait_ge(loaded, 32)
            for half in range(2):
                last = pe.matmul(ps[:, half * 512:(half + 1) * 512], w[:, :], xT[:, half * 512:(half + 1) * 512],
                                 start=True, stop=True)
            last.then_inc(done, 1)

        @block.vector
        def _(dve):
            link = chain(dve, step)
            dve.wait_ge(loaded, 32)
            dve.wait_ge(done, 1)
            link(dve.tensor_scalar(qf[:, :], ps[:, :], bias[:, 0:1], scale, ALU.add, ALU.mult))
            link(dve.tensor_copy(parts[:, 0, :], qf[:, :]))
            dve.tensor_copy(parts[:, 1, :], parts[:, 0, :])
            dve.tensor_copy(parts[:, 2, :], parts[:, 0, :])
            link(dve.tensor_tensor(rest[:, :], qf[:, :], parts[:, 0, :], ALU.subtract))
            link(dve.tensor_copy(parts[:, 3, :], rest[:, :]))
            dve.tensor_copy(parts[:, 4, :], parts[:, 3, :])
            dve.tensor_tensor(parts[:, 5, :], rest[:, :], parts[:, 3, :], ALU.subtract).then_inc(ready, 1)


TOPK = 32
ROUNDS = TOPK // 8 + 1


def row_threshold(nc, kst_l, qst, top, ident, tag):
    BANKS = 3
    CH = BANKS * 512
    NCH = -(-KPAD // CH)
    CT = CH // P
    UNITS = H * NT
    LINKS = 2 * ROUNDS - 1
    SLACK = 5e-7
    FLOOR = 100.0
    with ExitStack() as ctx:
        m = Memory(nc, ctx, tag)
        kb = [m.sb(f"kb{i}", [ROWS, NB, BK], BF16) for i in range(2)]
        qb = [m.sb(f"qb{i}", [ROWS, N], BF16) for i in range(2)]
        rows = [m.sb(f"rows{i}", [P, KPAD]) for i in range(4)]
        cand = [m.sb(f"cand{i}", [P, KT, 8]) for i in range(2)]
        work = m.sb("work", [P, KT, 8])
        best = [m.sb(f"best{i}", [P, ROUNDS * 8]) for i in range(2)]
        edge = m.sb("edge", [P, 3, UNITS])
        eighth, flag = m.sb("eighth", [P, 1]), [m.sb(f"flag{i}", [P, 1]) for i in range(2)]
        any_flag, taken = m.sb("any_flag", [1, 1]), m.sb("taken", [1, 1], I32)
        size, slack = m.sb("size", [P, 2, UNITS]), m.sb("slack", [P, UNITS])
        score = [m.ps(f"score{i}", [P, CH]) for i in range(2)]
        flags = m.ps("flags", [1, P])
        k_loaded = [m.sem(f"k_loaded{i}") for i in range(2)]
        settled, dve_settled = m.sem("settled"), m.sem("dve_settled")
        scored, copied, rows_free = m.sem("scored"), m.sem("copied"), m.sem("rows_free")
        cand_ready, merged, flagged, turned = m.sem("cand_ready"), m.sem("merged"), m.sem("flagged"), m.sem("turned")
        decided, searched, edge_ready, step = (m.sem("decided"), m.sem("searched"), m.sem("edge_ready"),
                                               m.sem("step"))
        eighth_ready = m.sem("eighth_ready")
        block = ctx.enter_context(nc.Block())

        @block.sync
        def _(sp):
            def load(h, par):
                sp.dma_start(kb[par][:, :, :], kst_l[:, ds(h, 1), 0:ROWS, :].rearrange(
                    "b o r c -> (o r) b c")).then_inc(k_loaded[par], 16)
                sp.dma_start(qb[par][:, :], qst[ds(h, 1), 0:ROWS, :].rearrange(
                    "o r n -> (o r) n")).then_inc(k_loaded[par], 16)

            load(0, 0)
            load(1, 1)
            with sp.Fori(1, H // 2) as hp:
                for par in range(2):
                    sp.wait_ge(scored, hp * (2 * NT * NCH) + (par - 1) * NT * NCH)
                    load(hp * 2 + par, par)

        @block.tensor
        def _(pe):
            with pe.Fori(0, H // 2) as hp:
                for par in range(2):
                    keys = kb[par][:, :, :].rearrange("r b c -> r (b c)")
                    pe.wait_ge(k_loaded[par], hp * 32 + 32)
                    settle(pe, settled)
                    with pe.Fori(0, NT // 2) as t2:
                        for half in range(2):
                            unit = hp * (2 * NT) + t2 * 2 + (par * NT + half)
                            for c in range(NCH):
                                pe.wait_ge(copied, unit * NCH + (c + 1))
                                settle(pe, settled)
                                for k in range(c * CH, min(c * CH + CH, KPAD), 512):
                                    n = min(512, KPAD - k)
                                    last = pe.matmul(score[(half * NCH + c) % 2][:, k - c * CH:k - c * CH + n],
                                                     qb[par][:, ds(t2 * (2 * P) + half * P, P)], keys[:, k:k + n],
                                                     start=True, stop=True)
                                last.then_inc(scored, 1)
                            pe.wait_ge(flagged, unit + 1)
                            settle(pe, settled)
                            pe.transpose(flags[0:1, :], flag[half][:, :], ident[:, :]).then_inc(turned, 1)
            for last in range(2):
                pe.wait_ge(flagged, UNITS + 1 + last)
                pe.transpose(flags[0:1, :], flag[last][:, :], ident[:, :]).then_inc(turned, 1)

        @block.scalar
        def _(act):
            act.sem_inc(copied, 2)
            with act.Fori(0, UNITS // 4) as u4:
                for i in range(4):
                    unit = u4 * 4 + i
                    act.wait_ge(rows_free, unit + 1)
                    for c in range(NCH):
                        act.wait_ge(scored, unit * NCH + (c + 1))
                        n = min(CH, KPAD - c * CH)
                        act.copy(rows[i][:, c * CH:c * CH + n],
                                 score[(i * NCH + c) % 2][:, 0:n]).then_inc(copied, 1)

        @block.vector
        def _(dve):
            def search_step(i, values, scratch, half, sem, start):
                if i:
                    dve.wait_ge(sem, start + i)
                    settle(dve, dve_settled)
                eight = best[half][:, i // 2 * 8:i // 2 * 8 + 8]
                src = values if i < 2 else scratch
                if i % 2 == 0:
                    dve.max(eight, src).then_inc(sem, 1)
                else:
                    dve.match_replace(scratch, eight, src, LOWEST).then_inc(sem, 1)

            def merge_step(w, half, i):
                if i == 0:
                    dve.wait_ge(cand_ready, w + 1)
                    dve.wait_ge(rows_free, w + 3)
                    settle(dve, dve_settled)
                    dve.tensor_reduce(eighth[:, :], cand[half][:, :, 7], AX, ALU.max).then_inc(eighth_ready, 1)
                search_step(i, cand[half][:, :, :].rearrange("p t e -> p (t e)"),
                            work[:, :, :].rearrange("p t e -> p (t e)"), half, merged, w * LINKS)

            def raise_flag(w, half):
                dve.wait_ge(merged, w * LINKS + LINKS)
                dve.wait_ge(eighth_ready, w + 1)
                dve.wait_ge(turned, w + 1)
                dve.tensor_tensor(flag[half][:, :], eighth[:, :], best[half][:, TOPK:TOPK + 1],
                                  ALU.is_ge).then_inc(flagged, 1)

            def decide(w, half, buf):
                dve.wait_ge(turned, w + 3)
                dve.tensor_reduce(any_flag[:, :], flags[0:1, :], AX, ALU.max).then_inc(decided, 1)
                dve.wait_ge(decided, w * 2 + 1)
                dve.tensor_copy(taken[:, :], any_flag[:, :]).then_inc(decided, 1)
                dve.wait_ge(decided, w * 2 + 2)
                settle(dve, dve_settled)
                value = dve.value_load(taken[0:1, 0:1], min_val=0, max_val=1)
                with dve.If(value > 0):
                    for i in range(LINKS):
                        search_step(i, rows[buf][:, :], rows[buf][:, :], half, searched, w * LINKS)
                    dve.wait_ge(searched, w * LINKS + LINKS)
                    settle(dve, dve_settled)
                with dve.Else():
                    dve.sem_inc(searched, LINKS)
                for i, place in enumerate((0, TOPK - 1, TOPK)):
                    last = dve.tensor_copy(edge[:, i, ds(w, 1)], best[half][:, place:place + 1])
                last.then_inc(rows_free, 1)

            def tile_maxima(unit, i, merge=True):
                for s in range(KT):
                    if s % CT == 0:
                        dve.wait_ge(copied, unit * NCH + (s // CT + 3))
                        settle(dve, dve_settled)
                    last = dve.max(cand[i % 2][:, s, :], rows[i][:, s * P:(s + 1) * P])
                    if merge and s % 4 == 3 and s // 4 < LINKS:
                        merge_step(unit - 1, 1 - i % 2, s // 4)
                    if merge and s == 4 * LINKS + 2:
                        raise_flag(unit - 1, 1 - i % 2)
                last.then_inc(cand_ready, 1)
                if merge:
                    decide(unit - 1, 1 - i % 2, (i - 1) % 4)

            link = chain(dve, step)
            dve.sem_inc(rows_free, 4)
            dve.memset(flag[0][:, :], 0.0)
            link(dve.memset(flag[1][:, :], 0.0))
            dve.sem_inc(flagged, 2)
            tile_maxima(0, 0, merge=False)
            with dve.Fori(0, UNITS // 4 - 1) as u4:
                for i in range(1, 5):
                    tile_maxima(u4 * 4 + i, i % 4)
            for unit in range(UNITS - 3, UNITS):
                tile_maxima(unit, unit % 4)
            for i in range(LINKS):
                merge_step(UNITS - 1, 1, i)
            raise_flag(UNITS - 1, 1)
            decide(UNITS - 1, 1, 3)
            dve.wait_ge(rows_free, UNITS + 4)
            largest, inside, outside = (edge[:, i, :] for i in range(3))
            for i, value in enumerate((largest, inside)):
                link(dve.scalar_tensor_tensor(out=size[:, i, :], in0=value, scalar=-1.0, in1=value, op0=ALU.mult,
                                              op1=ALU.max))
            link(dve.tensor_tensor(slack[:, :], size[:, 0, :], size[:, 1, :], ALU.add))
            link(dve.scalar_tensor_tensor(out=slack[:, :], in0=slack[:, :], scalar=-SLACK, in1=inside, op0=ALU.mult,
                                          op1=ALU.add))
            link(dve.tensor_tensor(size[:, 0, :], inside, outside, ALU.add))
            link(dve.tensor_scalar(size[:, 0, :], size[:, 0, :], 0.5, None, ALU.mult))
            link(dve.tensor_tensor(size[:, 0, :], size[:, 0, :], slack[:, :], ALU.min))
            link(dve.tensor_scalar(size[:, 1, :], largest, -FLOOR, None, ALU.add))
            dve.tensor_tensor(top[:, :], size[:, 0, :], size[:, 1, :], ALU.max)


def set_shift(nc, top, qst, ident, tag):
    with ExitStack() as ctx:
        m = Memory(nc, ctx, tag)
        neg, rest = m.sb("neg", [P, P]), m.sb("rest", [P, P])
        parts = m.sb("parts", [P, 3, P], BF16)
        tp = m.ps("tp", [P, P])
        turned, step, ready, stored = m.sem("turned"), m.sem("step"), m.sem("ready"), m.sem("stored")
        block = ctx.enter_context(nc.Block())

        @block.tensor
        def _(pe):
            pe.transpose(tp[:, :], top[:, :], ident[:, :]).then_inc(turned, 1)

        @block.vector
        def _(dve):
            link = chain(dve, step)
            dve.wait_ge(turned, 1)
            link(dve.tensor_scalar(neg[:, :], tp[:, :], -1.0, None, ALU.mult))
            link(dve.tensor_copy(parts[:, 0, :], neg[:, :]))
            link(dve.tensor_tensor(rest[:, :], neg[:, :], parts[:, 0, :], ALU.subtract))
            link(dve.tensor_copy(parts[:, 1, :], rest[:, :]))
            dve.tensor_tensor(parts[:, 2, :], rest[:, :], parts[:, 1, :], ALU.subtract).then_inc(ready, 1)

        @block.sync
        def _(sp):
            sp.wait_ge(ready, 1)
            for i in range(3):
                sp.dma_start(qst[:, AUX + 2 * i + 1, :].rearrange("h (t c) -> h t c", c=P),
                             parts[:, i, :]).then_inc(stored, 16)
            sp.wait_ge(stored, 48)


def attend_to_top(nc, kst_l, vst_l, qst, ident, att, tag):
    with ExitStack() as ctx:
        m = Memory(nc, ctx, tag)
        kb = [m.sb(f"kb{i}", [P, G, BK], BF16) for i in range(2)]
        qb = [m.sb(f"qb{i}", [P, G, QC], BF16) for i in range(2)]
        v_all = m.sb("v_all", [P, KT, H, VW])
        vb = [m.sb(f"vb{i}", [P, TB, G, VW]) for i in range(2)]
        prob = [m.sb(f"prob{i}", [P, G, QC]) for i in range(2)]
        kept = [m.sb(f"kept{i}", [P, G, QC]) for i in range(2)]
        ob = m.sb("ob", [VW, G, QC])
        rden = m.sb("rden", [P, QC // P, G, 1])
        score = [m.ps(f"score{i}", [P, QC]) for i in range(G)]
        acc = [m.ps(f"acc{i}", [P, QC]) for i in range(NQC)]
        tp = m.ps("tp", [P, QC // P, G, VW])
        q_loaded = [m.sem(f"q_loaded{i}") for i in range(2)]
        k_loaded = [m.sem(f"k_loaded{i}") for i in range(2)]
        cleared, v_loaded, vb_ready = m.sem("cleared"), m.sem("v_loaded"), m.sem("vb_ready")
        settled, pool_settled = m.sem("settled"), m.sem("pool_settled")
        scored, exped, kept_ready, summed = m.sem("scored"), m.sem("exped"), m.sem("kept_ready"), m.sem("summed")
        ob_ready, turned, tp_free, rden_ready = m.sem("ob_ready"), m.sem("turned"), m.sem("tp_free"), m.sem("rden_ready")
        lower, bias_ready = m.sb("lower", [P, 1]), m.sem("bias_ready")
        CREDIT = TB + 1
        block = ctx.enter_context(nc.Block())

        def blocks(eng, one_block):
            with eng.Fori(0, NG) as g:
                for qc in range(NQC):
                    for b in (0, 1):
                        one_block(g, qc, b, (qc + b) % 2)
                    with eng.Fori(1, NB // 2) as bp:
                        for b in range(2):
                            one_block(g, qc, bp * 2 + b, (qc + b) % 2)
                    one_block(g, qc, NB - 1, (qc + NB - 1) % 2)

        def number(g, qc, b):
            return g * (NQC * NB) + (b + qc * NB)

        def before_last_used(n):
            return n * TB + (CREDIT - TB)

        @block.sync
        def _(sp):
            sp.dma_start(v_all[:, :, :, :], vst_l).then_inc(v_loaded, 16)
            sp.wait_ge(cleared, 4)

            def one_block(g, qc, b, par):
                n = number(g, qc, b)
                sp.wait_ge(summed, before_last_used(n))
                if isinstance(b, int) and b == 0:
                    sp.dma_start(qb[qc][0:ROWS, :, :], qst[ds(g * G, G), 0:ROWS, qc * QC:(qc + 1) * QC].rearrange(
                        "j r c -> r j c")).then_inc(q_loaded[qc], 16)
                sp.dma_start(kb[par][0:ROWS, :, :], kst_l[ds(b, 1), ds(g * G, G), 0:ROWS, :].rearrange(
                    "o j r c -> (o r) j c")).then_inc(k_loaded[par], 16)

            blocks(sp, one_block)

        @block.gpsimd
        def _(pool):
            for i in range(2):
                pool.memset(kb[i][:, :, :], 0.0).then_inc(cleared, 1)
                pool.memset(qb[i][:, :, :], 0.0).then_inc(cleared, 1)
            pool.wait_ge(v_loaded, 16)

            def one_block(g, qc, b, par):
                n = number(g, qc, b)
                pool.wait_ge(summed, before_last_used(n))
                settle(pool, pool_settled)
                pool.tensor_copy(vb[par][:, :, :, :], v_all[:, ds(b * TB, TB), ds(g * G, G), :]).then_inc(vb_ready, 1)

            blocks(pool, one_block)

        @block.tensor
        def _(pe):
            def scores(k, qc, par, t, j):
                pe.wait_ge(kept_ready, k * G + (j + 1))
                pe.matmul(score[j][:, :], kb[par][:, j, t * P:(t + 1) * P], qb[qc][:, j, :], start=True,
                          stop=True).then_inc(scored, 1)

            def sums(k, qc, par, t, j, first, final):
                pe.wait_ge(kept_ready, k * G + (j + 1 + G))
                last = pe.matmul(acc[qc][32 * j:32 * j + VW, :], vb[par][:, t, j, :], kept[(par + t) % 2][:, j, :],
                                 start=first, stop=final, skip_group_check=True)
                if j == G - 1:
                    last.then_inc(summed, 1)

            def one_block(g, qc, b, par):
                n = number(g, qc, b)
                known = isinstance(b, int)
                first, final = known and b == 0, known and b == NB - 1
                if first:
                    pe.wait_ge(q_loaded[qc], g * 16 + 16)
                    pe.wait_ge(ob_ready, g * NQC + (qc + 1))
                pe.wait_ge(k_loaded[par], fill_count(g, qc, b, par))
                pe.wait_ge(vb_ready, n + 1)
                for t in range(TB):
                    for j in range(G):
                        scores(n * TB + t, qc, par, t, j)
                        if t:
                            sums(n * TB + (t - 1), qc, par, t - 1, j, first and t == 1, False)
                        elif not first:
                            sums(n * TB - 1, qc, 1 - par, TB - 1, j, False, False)
                if final:
                    for j in range(G):
                        sums(n * TB + (TB - 1), qc, par, TB - 1, j, False, True)
                if final:
                    pe.wait_ge(ob_ready, g * NQC + (qc + 3))
                    pe.wait_ge(tp_free, g * NQC + (qc + 1))
                    settle(pe, settled)
                    for c in range(QC // P):
                        for j in range(G):
                            last = pe.transpose(tp[:, c, j, :], ob[:, j, c * P:(c + 1) * P], ident[0:VW, 0:VW])
                    last.then_inc(turned, 1)

            def fill_count(g, qc, b, par):
                if isinstance(b, int):
                    return g * (NB * 16) + ((b + qc * NB) // 2 + 1) * 16
                odd = (par - qc) % 2
                return g * (NB * 16) + (b - odd) * 8 + ((odd + qc * NB) // 2 + 1) * 16

            pe.wait_ge(cleared, 4)
            pe.sem_inc(summed, CREDIT)
            blocks(pe, one_block)

        @block.scalar
        def _(act):
            act.wait_ge(bias_ready, 1)
            with act.Fori(0, NG * NQC * KT // 12) as i:
                for t in range(12):
                    for j in range(G):
                        act.wait_ge(scored, i * (12 * G) + (G * t + j + 1))
                        act.activation(prob[t % 2][:, j, :], score[j][:, :], ACT.Exp,
                                       bias=lower[:, 0:1]).then_inc(exped, 1)

        @block.vector
        def _(dve):
            dve.sem_inc(tp_free, 1)
            dve.sem_inc(ob_ready, 2)
            dve.memset(lower[:, :], -LOWER).then_inc(bias_ready, 1)
            dve.sem_inc(kept_ready, G)

            def keep(k, parity):
                dve.wait_ge(summed, k + (CREDIT - 1))
                for j in range(G):
                    dve.wait_ge(exped, k * G + (j + 1))
                    dve.scalar_tensor_tensor(out=kept[parity][:, j, :], in0=score[j][:, :], scalar=0.0,
                                             in1=prob[parity][:, j, :], op0=ALU.is_ge,
                                             op1=ALU.mult).then_inc(kept_ready, 1)

            with dve.Fori(0, NG) as g:
                for qc in range(NQC):
                    u = g * NQC + qc
                    keep(u * KT, qc)
                    with dve.Fori(0, KT // 2) as i:
                        keep(u * KT + i * 2 + 1, 1 - qc)
                        keep(u * KT + i * 2 + 2, qc)
                    dve.wait_ge(summed, u * KT + (KT + CREDIT))
                    dve.wait_ge(tp_free, u + 1)
                    for j in range(G):
                        last = dve.tensor_copy(ob[:, j, :], acc[qc][32 * j:32 * j + VW, :])
                    last.then_inc(ob_ready, 1)
                    dve.wait_ge(turned, u + 1)
                    dve.reciprocal(rden[:, :, :, :], tp[:, :, :, HD:VW]).then_inc(rden_ready, 1)
                    dve.wait_ge(rden_ready, u + 1)
                    for c in range(QC // P):
                        last = dve.tensor_tensor(
                            att[:, qc * (QC // P) + c, ds(g * (G * HD), G * HD)].rearrange("p (j d) -> p j d", d=HD),
                            tp[:, c, :, 0:HD], rden[:, c, :, :].to_broadcast([P, G, HD]), ALU.mult)
                    last.then_inc(tp_free, 1)


def attend_with_max(nc, kst_l, vst_l, qst, ident, att, tag):
    UNITS = NG * NQC
    QT = QC // P
    ITEMS = G * QT
    CW = 512
    NC = -(-KPAD // CW)
    assert ITEMS == NB - 1
    SPREAD = [range(t * NC // TB, (t + 1) * NC // TB) for t in range(TB)]
    CREDIT = TB + 1
    with ExitStack() as ctx:
        m = Memory(nc, ctx, tag)
        kg = [m.sb(f"kg{i}", [P, G, NB, BK], BF16) for i in range(2)]
        qn = [m.sb(f"qn{i}", [P, G, QC], BF16) for i in range(2)]
        qb = [m.sb(f"qb{i}", [P, G, QC], BF16) for i in range(2)]
        v_all = m.sb("v_all", [P, KT, H, VW])
        vb = [m.sb(f"vb{i}", [P, TB, G, VW]) for i in range(2)]
        prob = [m.sb(f"prob{i}", [P, 2, QC]) for i in range(4)]
        zeros = m.sb("zeros", [P, QC], BF16)
        partial, tops = m.sb("partial", [P, 2, NC]), m.sb("tops", [P, ITEMS])
        neg, rest = m.sb("neg", [ITEMS, P]), m.sb("rest", [ITEMS, P])
        parts = m.sb("parts", [ITEMS, 3, P], BF16)
        ob = m.sb("ob", [VW, G, QC])
        rden = m.sb("rden", [P, QT, G, 1])
        score = [m.ps(f"score{i}", [P, 2, QC]) for i in range(2)]
        acc = m.ps("acc", [P, QC])
        row = [m.ps(f"row{i}", [P, CW]) for i in range(2)]
        turn = m.ps("turn", [P, 512])
        tops_turned = turn[0:ITEMS, 0:P]
        tp = turn[:, P:P + QT * G * VW].rearrange("p (c j w) -> p c j w", c=QT, j=G)
        kg_loaded, qn_loaded, qb_loaded = ([m.sem(f"{n}_loaded{i}") for i in range(2)] for n in ("kg", "qn", "qb"))
        cleared_late = m.sem("cleared_late")
        cleared, v_loaded, vb_ready, pool_settled = (m.sem("cleared"), m.sem("v_loaded"), m.sem("vb_ready"),
                                                     m.sem("pool_settled"))
        scored, exped, summed, ob_ready, turned = (m.sem("scored"), m.sem("exped"), m.sem("summed"),
                                                   m.sem("ob_ready"), m.sem("turned"))
        turned_tops = m.sem("turned_tops")
        chunk_scored, reduced, tops_ready = m.sem("chunk_scored"), m.sem("reduced"), m.sem("tops_ready")
        tops_out, split, shift_ready, shift_stored = (m.sem("tops_out"), m.sem("split"), m.sem("shift_ready"),
                                                      m.sem("shift_stored"))
        rden_ready, att_ready, settled = m.sem("rden_ready"), m.sem("att_ready"), m.sem("settled")
        block = ctx.enter_context(nc.Block())

        def units(eng, one_unit):
            def groups(gp, end):
                for gi in range(2):
                    for qc in range(NQC):
                        one_unit(gp * (2 * NQC) + (gi * NQC + qc), gp * 2 + gi, gi, qc,
                                 end and (gi, qc) == (1, NQC - 1))

            with eng.Fori(0, NG // 2 - 1) as gp:
                groups(gp, False)
            groups(NG // 2 - 1, True)

        @block.sync
        def _(sp):
            def load_keys(g):
                for j in range(G):
                    sp.dma_start(kg[g % 2][0:ROWS, j, :, :],
                                 kst_l[:, g * G + j, 0:ROWS, :].rearrange("b r c -> r b c")).then_inc(
                                     kg_loaded[g % 2], 16)

            def load_queries(buf, sem, u):
                g, qc = u // NQC, u % NQC
                sp.dma_start(buf[u % 2][0:ROWS, :, :], qst[g * G:(g + 1) * G, 0:ROWS, qc * QC:(qc + 1) * QC].rearrange(
                    "j r c -> r j c")).then_inc(sem[u % 2], 16)

            sp.wait_ge(cleared, 6)
            load_queries(qn, qn_loaded, 0)
            load_keys(0)
            sp.dma_start(v_all[:, :, :, :], vst_l).then_inc(v_loaded, 16)
            load_queries(qn, qn_loaded, 1)
            sp.wait_ge(cleared_late, 1)
            load_keys(1)
            for u in range(UNITS):
                g, qc = u // NQC, u % NQC
                sp.wait_ge(shift_ready, u + 1)
                for i in range(3):
                    sp.dma_start(qst[g * G:(g + 1) * G, AUX + 2 * i + 1, qc * QC:(qc + 1) * QC].rearrange(
                        "j (t c) -> j t c", c=P), parts[:, i, :]).then_inc(shift_stored, 16)
                sp.wait_ge(shift_stored, 48 * (u + 1) + 1)
                if u >= 2:
                    sp.wait_ge(summed, (u - 1) * KT + CREDIT)
                load_queries(qb, qb_loaded, u)
                if u + 2 < UNITS:
                    sp.wait_ge(chunk_scored, (u + 1) * ITEMS * NC)
                    load_queries(qn, qn_loaded, u + 2)
                if qc == 0 and 2 <= g + 1 < NG:
                    sp.wait_ge(summed, u * KT + CREDIT)
                    load_keys(g + 1)

        @block.gpsimd
        def _(pool):
            pool.memset(kg[1][:, :, :, :], 0.0).then_inc(cleared_late, 1)
            pool.wait_ge(v_loaded, 16)

            def stage(n, b, g, par):
                pool.wait_ge(summed, n * TB + (CREDIT - TB))
                settle(pool, pool_settled)
                pool.tensor_copy(vb[par][:, :, :, :], v_all[:, ds(b * TB, TB), ds(g * G, G), :]).then_inc(vb_ready, 1)

            with pool.Fori(0, NG) as g:
                for qc in range(NQC):
                    n0 = g * (NQC * NB) + qc * NB
                    for b in (0, 1):
                        stage(n0 + b, b, g, (qc + b) % 2)
                    with pool.Fori(1, NB // 2) as bp:
                        for b in range(2):
                            stage(n0 + bp * 2 + b, bp * 2 + b, g, (qc + b) % 2)
                    stage(n0 + NB - 1, NB - 1, g, (qc + NB - 1) % 2)

        @block.tensor
        def _(pe):
            def row_chunks(u, gi, par, j, i, chunks):
                item = u * ITEMS + j * QT + i
                keys = kg[gi][:, :, :, :].rearrange("r j b c -> r (j b c)")
                for c in chunks:
                    n = min(CW, KPAD - c * CW)
                    pe.wait_ge(reduced, item * NC + (c + 1))
                    pe.matmul(row[(i * NC + c) % 2][:, 0:n],
                              qn[par][:, ds(j, 1), i * P:(i + 1) * P].rearrange("r o c -> r (o c)"),
                              keys[:, ds(j * KPAD + c * CW, n)], start=True, stop=True).then_inc(chunk_scored, 1)

            def scores(u, gi, qc, k, pair):
                pe.wait_ge(exped, (u * KT + k) * 2 + (pair + 1))
                keys = kg[gi][:, :, :, :].rearrange("r j b c -> r j (b c)")
                for half in range(2):
                    j = 2 * pair + half
                    last = pe.matmul(score[pair][:, half, :], keys[:, j, ds(k * P, P)], qb[qc][:, j, :],
                                     start=True, stop=True)
                last.then_inc(scored, 1)

            def sums(u, qc, j, c, pair, final=False):
                if c % TB == 0 and pair == 0:
                    pe.wait_ge(vb_ready, u * NB + j * QT + (c // TB + 1))
                pe.wait_ge(exped, (u * KT + j * (QT * TB) + c) * 2 + (pair + 3))
                for h in (2 * pair, 2 * pair + 1):
                    last = pe.matmul(acc[32 * h:32 * h + VW, :], vb[(qc + c // TB) % 2][:, c % TB, h, :],
                                     prob[2 * ((qc + c) % 2) + pair][:, h % 2, :], start=False, stop=final,
                                     skip_group_check=True)
                if pair == 1:
                    last.then_inc(summed, 1)

            def turn_tops(u):
                pe.wait_ge(tops_ready, (u + 1) * ITEMS)
                settle(pe, settled)
                pe.transpose(tops_turned, tops[:, :], ident[:, :]).then_inc(turned_tops, 1)

            def one_unit(u, g, gi, qc, last_unit):
                next_gi = (gi + qc) % 2
                pe.wait_ge(qb_loaded[qc], g * 16 + 16)
                for pair in range(2):
                    scores(u, gi, qc, 0, pair)
                pe.wait_ge(ob_ready, u + 1)
                pe.matmul(acc[:, :], zeros[:, 0:P], zeros[:, :], start=True, stop=False, skip_group_check=True)
                if not last_unit:
                    if qc == 1:
                        pe.wait_ge(kg_loaded[next_gi], (g - gi) * (G * 8) + G * 16 * (1 + gi))
                    pe.wait_ge(qn_loaded[1 - qc], g * 16 + (16 + 16 * qc))
                settle(pe, settled)
                with pe.Fori(0, G) as j:
                    for i in range(QT):
                        for t in range(TB):
                            c = i * TB + t
                            chunks = SPREAD[t]
                            for slot in range(4):
                                if slot < 2:
                                    scores(u, gi, qc, j * (QT * TB) + (c + 1), slot)
                                else:
                                    sums(u, qc, j, c, slot - 2)
                                if not last_unit:
                                    row_chunks(u + 1, next_gi, 1 - qc, j, i,
                                               chunks[slot * len(chunks) // 4:(slot + 1) * len(chunks) // 4])
                for c in range(G * QT * TB, KT):
                    for pair in range(2):
                        if c < KT - 1:
                            scores(u, gi, qc, c + 1, pair)
                    if c == KT - 1 and not last_unit:
                        turn_tops(u + 1)
                    for pair in range(2):
                        sums(u, qc, 0, c, pair, c == KT - 1)
                pe.wait_ge(ob_ready, u + 2)
                if last_unit:
                    pe.wait_ge(att_ready, u + 1)
                else:
                    pe.wait_ge(tops_out, u + 2)
                settle(pe, settled)
                for c in range(QT):
                    for j in range(G):
                        last = pe.transpose(tp[:, c, j, :], ob[:, j, c * P:(c + 1) * P], ident[0:VW, 0:VW])
                last.then_inc(turned, 1)

            pe.wait_ge(cleared, 6)
            pe.sem_inc(summed, CREDIT)
            pe.sem_inc(turned, 1)
            pe.wait_ge(kg_loaded[0], G * 16)
            pe.wait_ge(qn_loaded[0], 16)
            with pe.Fori(0, G) as j:
                for i in range(QT):
                    row_chunks(0, 0, 0, j, i, range(NC))
            turn_tops(0)
            units(pe, one_unit)

        @block.scalar
        def _(act):
            def exponentials(u, qc, k, c):
                for pair in range(2):
                    act.wait_ge(scored, (u * KT + k) * 2 + (pair + 1))
                    act.wait_ge(summed, u * KT + k + (CREDIT - 1))
                    act.activation(prob[2 * ((qc + c) % 2) + pair][:, :, :], score[pair][:, :, :],
                                   ACT.Exp).then_inc(exped, 1)

            def one_unit(u, g, gi, qc, last_unit):
                with act.Fori(0, G) as j:
                    for c in range(QT * TB):
                        exponentials(u, qc, j * (QT * TB) + c, c)
                for c in range(G * QT * TB, KT):
                    exponentials(u, qc, c, c)
                act.wait_ge(summed, u * KT + (KT + CREDIT))
                act.wait_ge(turned, u + 1)
                for j in range(G):
                    last = act.copy(ob[:, j, :], acc[32 * j:32 * j + VW, :])
                last.then_inc(ob_ready, 1)

            act.sem_inc(exped, 2)
            act.sem_inc(ob_ready, 1)
            units(act, one_unit)

        @block.vector
        def _(dve):
            def search_rows(u):
                with dve.Fori(0, G) as j:
                    for i in range(QT):
                        item = u * ITEMS + j * QT + i
                        for c in range(NC):
                            dve.wait_ge(chunk_scored, item * NC + (c + 1))
                            n = min(CW, KPAD - c * CW)
                            dve.tensor_reduce(partial[:, i % 2, c:c + 1], row[(i * NC + c) % 2][:, 0:n], AX,
                                              ALU.max).then_inc(reduced, 1)
                        dve.wait_ge(reduced, item * NC + (NC + 2))
                        dve.tensor_reduce(tops[:, ds(j * QT + i, 1)], partial[:, i % 2, :], AX,
                                          ALU.max).then_inc(tops_ready, 1)

            def shift_rows(u):
                dve.wait_ge(turned_tops, u + 1)
                dve.tensor_scalar(neg[:, :], tops_turned, -1.0, None, ALU.mult).then_inc(tops_out, 1)
                dve.wait_ge(tops_out, u + 1)
                dve.wait_ge(shift_stored, u * 48 + 1)
                dve.tensor_copy(parts[:, 0, :], neg[:, :]).then_inc(split, 1)
                dve.wait_ge(split, u * 3 + 1)
                dve.tensor_tensor(rest[:, :], neg[:, :], parts[:, 0, :], ALU.subtract).then_inc(split, 1)
                dve.wait_ge(split, u * 3 + 2)
                dve.tensor_copy(parts[:, 1, :], rest[:, :]).then_inc(split, 1)
                dve.wait_ge(split, u * 3 + 3)
                dve.tensor_tensor(parts[:, 2, :], rest[:, :], parts[:, 1, :], ALU.subtract).then_inc(shift_ready, 1)

            def one_unit(u, g, gi, qc, last_unit):
                if not last_unit:
                    search_rows(u + 1)
                    shift_rows(u + 1)
                dve.wait_ge(turned, u + 2)
                dve.wait_ge(att_ready, u + 1)
                dve.reciprocal(rden[:, :, :, :], tp[:, :, :, HD:VW]).then_inc(rden_ready, 1)
                dve.wait_ge(rden_ready, u + 1)
                for c in range(QT):
                    last = dve.tensor_tensor(
                        att[:, qc * QT + c, ds(g * (G * HD), G * HD)].rearrange("p (j d) -> p j d", d=HD),
                        tp[:, c, :, 0:HD], rden[:, c, :, :].to_broadcast([P, G, HD]), ALU.mult)
                last.then_inc(att_ready, 1)

            for tile in (zeros[:, :], qn[0][:, :, :], qn[1][:, :, :], kg[0][:, :, :, :], qb[0][:, :, :], qb[1][:, :, :]):
                dve.memset(tile, 0.0).then_inc(cleared, 1)
            dve.sem_inc(reduced, 2)
            dve.sem_inc(att_ready, 1)
            dve.sem_inc(shift_stored, 1)
            search_rows(0)
            shift_rows(0)
            units(dve, one_unit)


def project(nc, att, wo, bo, gate, xs, ident, tag):
    with ExitStack() as ctx:
        m = Memory(nc, ctx, tag)
        w, bias, gt = m.sb("w", [P, D]), m.sb("bias", [P, D]), m.sb("gt", [P, 1])
        th = m.sb("th", [P, 1])
        bg = m.sb("bg", [P, D])
        aT = m.sb("aT", [P, NT, P])
        upd = m.sb("upd", [P, NT, D])
        tp, y = m.ps("tp", [P, NT, P]), m.ps("y", [P, NT, D])
        loaded, gate_ready, turned, aT_ready, done, step = (
            m.sem("loaded"), m.sem("gate_ready"), m.sem("turned"), m.sem("aT_ready"), m.sem("done"), m.sem("step"))
        block = ctx.enter_context(nc.Block())

        @block.sync
        def _(sp):
            sp.dma_start(w[:, :], wo).then_inc(loaded, 16)
            sp.dma_start(bias[:, :], bo.partition_broadcast(P)).then_inc(loaded, 16)
            sp.dma_start(gt[:, :], gate.partition_broadcast(P)).then_inc(loaded, 16)

        @block.tensor
        def _(pe):
            pe.wait_ge(loaded, 48)
            for t in range(NT):
                last = pe.transpose(tp[:, t, :], att[:, t, :], ident[:, :])
                if t % 4 == 3:
                    last.then_inc(turned, 1)
            for t in range(NT):
                if t % 4 == 0:
                    pe.wait_ge(aT_ready, t // 4 + 1)
                last = pe.matmul(y[:, t, :], aT[:, t, :], w[:, :], start=True, stop=True)
                if t % 4 == 3:
                    last.then_inc(done, 1)

        @block.scalar
        def _(act):
            act.wait_ge(loaded, 48)
            act.activation(th[:, :], gt[:, :], ACT.Tanh).then_inc(gate_ready, 1)
            for half in range(2):
                act.wait_ge(turned, half + 1)
                act.copy(aT[:, half * 4:half * 4 + 4, :], tp[:, half * 4:half * 4 + 4, :]).then_inc(aT_ready, 1)

        @block.vector
        def _(dve):
            link = chain(dve, step)
            dve.wait_ge(loaded, 48)
            dve.wait_ge(gate_ready, 1)
            for t in range(NT):
                if t % 4 == 0:
                    dve.wait_ge(done, t // 4 + 1)
                link(dve.tensor_tensor(upd[:, t, :], y[:, t, :], bias[:, :], ALU.add))
                dve.scalar_tensor_tensor(out=xs[:, t, :], in0=upd[:, t, :], scalar=th[:, 0:1], in1=xs[:, t, :],
                                         op0=ALU.mult, op1=ALU.add)


def route_sigmoid(nc, xT, gate_w, bias, ident, comb, tag):
    E, ROUTE_SCALE = L0_E, 2.826
    with ExitStack() as ctx:
        m = Memory(nc, ctx, tag)
        w, b = m.sb("w", [P, E]), m.sb("b", [P, E])
        score, sel, rep, picked = (m.sb("score", [P, NT, E]), m.sb("sel", [P, NT, E]),
                                   m.sb("rep", [P, NT, E]), m.sb("picked", [P, NT, E]))
        best = m.sb("best", [P, NT, 8])
        total, inv = m.sb("total", [P, NT, 1]), m.sb("inv", [P, NT, 1])
        combT = m.sb("combT", [E, N])
        one = m.sb("one", [1, N])
        logit, tp = m.ps("logit", [P, NT, E]), m.ps("tp", [E, N])
        loaded, logits_done, scores_ready, step, ready, turned, out_ready, stored = (
            m.sem("loaded"), m.sem("logits_done"), m.sem("scores_ready"), m.sem("step"), m.sem("ready"),
            m.sem("turned"), m.sem("out_ready"), m.sem("stored"))
        block = ctx.enter_context(nc.Block())

        @block.sync
        def _(sp):
            sp.dma_start(w[:, :], gate_w).then_inc(loaded, 16)
            sp.dma_start(b[:, :], bias.partition_broadcast(P)).then_inc(loaded, 16)
            sp.wait_ge(out_ready, 2)
            sp.dma_start(comb[0:E, :], combT[:, :]).then_inc(stored, 16)
            sp.dma_start(comb[E:E + 1, :], one[:, :]).then_inc(stored, 16)
            sp.wait_ge(stored, 32)

        @block.tensor
        def _(pe):
            pe.wait_ge(loaded, 32)
            for t in range(NT):
                last = pe.matmul(logit[:, t, :], xT[:, t * P:(t + 1) * P], w[:, :], start=True, stop=True)
            last.then_inc(logits_done, 1)
            pe.wait_ge(ready, 1)
            for t in range(NT):
                last = pe.transpose(tp[:, t * P:(t + 1) * P], picked[:, t, :], ident[:, :])
            last.then_inc(turned, 1)

        @block.scalar
        def _(act):
            act.wait_ge(logits_done, 1)
            act.activation(score[:, :, :], logit[:, :, :], ACT.Sigmoid).then_inc(scores_ready, 1)
            act.wait_ge(turned, 1)
            act.copy(combT[:, :], tp[:, :]).then_inc(out_ready, 1)

        @block.vector
        def _(dve):
            link = chain(dve, step)
            dve.memset(one[:, :], 1.0).then_inc(out_ready, 1)
            dve.wait_ge(loaded, 32)
            dve.wait_ge(scores_ready, 1)
            link(dve.tensor_tensor(sel[:, :, :], score[:, :, :], b[:, :].unsqueeze(1).to_broadcast([P, NT, E]), ALU.add))
            for t in range(NT):
                last = dve.max(best[:, t, :], sel[:, t, :])
            link(last)
            for t in range(NT):
                last = dve.match_replace(rep[:, t, :], best[:, t, :], sel[:, t, :], -3e38)
            link(last)
            link(dve.tensor_tensor(picked[:, :, :], rep[:, :, :], sel[:, :, :], ALU.not_equal))
            link(dve.tensor_tensor(picked[:, :, :], picked[:, :, :], score[:, :, :], ALU.mult))
            link(dve.tensor_reduce(total[:, :, 0], picked[:, :, :], AX, ALU.add))
            link(dve.reciprocal(inv[:, :, :], total[:, :, :]))
            link(dve.tensor_scalar(inv[:, :, :], inv[:, :, :], ROUTE_SCALE, None, ALU.mult))
            dve.tensor_tensor(picked[:, :, :], picked[:, :, :], inv[:, :, :].to_broadcast([P, NT, E]),
                              ALU.mult).then_inc(ready, 1)


def route_top2(nc, xT, router_w, ident, comb, tag):
    E, DUMMY = L3_E, -3e38
    with ExitStack() as ctx:
        m = Memory(nc, ctx, tag)
        w = m.sb("w", [P, E])
        logit, rep = m.sb("logit", [P, NT, 2 * E]), m.sb("rep", [P, NT, 2 * E])
        best, two = m.sb("best", [P, NT, 8]), m.sb("two", [P, NT, 8])
        diff, ex, picked = m.sb("diff", [P, NT, E]), m.sb("ex", [P, NT, E]), m.sb("picked", [P, NT, E])
        total, inv = m.sb("total", [P, NT, 1]), m.sb("inv", [P, NT, 1])
        combT = m.sb("combT", [E, N])
        ps, tp = m.ps("ps", [P, NT, E]), m.ps("tp", [E, N])
        loaded, logits_done, step, diff_ready, ex_ready, ready, turned, out_ready, stored = (
            m.sem("loaded"), m.sem("logits_done"), m.sem("step"), m.sem("diff_ready"), m.sem("ex_ready"),
            m.sem("ready"), m.sem("turned"), m.sem("out_ready"), m.sem("stored"))
        block = ctx.enter_context(nc.Block())

        @block.sync
        def _(sp):
            sp.dma_start(w[:, :], router_w).then_inc(loaded, 16)
            sp.wait_ge(out_ready, 1)
            sp.dma_start(comb[0:E, :], combT[:, :]).then_inc(stored, 16)
            sp.wait_ge(stored, 16)

        @block.tensor
        def _(pe):
            pe.wait_ge(loaded, 16)
            for t in range(NT):
                last = pe.matmul(ps[:, t, :], xT[:, t * P:(t + 1) * P], w[:, :], start=True, stop=True)
            last.then_inc(logits_done, 1)
            pe.wait_ge(ready, 1)
            for t in range(NT):
                last = pe.transpose(tp[:, t * P:(t + 1) * P], picked[:, t, :], ident[:, :])
            last.then_inc(turned, 1)

        @block.scalar
        def _(act):
            act.wait_ge(diff_ready, 1)
            act.activation(ex[:, :, :], diff[:, :, :], ACT.Exp).then_inc(ex_ready, 1)
            act.wait_ge(turned, 1)
            act.copy(combT[:, :], tp[:, :]).then_inc(out_ready, 1)

        @block.vector
        def _(dve):
            link = chain(dve, step)
            link(dve.memset(logit[:, :, :], DUMMY))
            link(dve.memset(two[:, :, :], DUMMY))
            dve.wait_ge(logits_done, 1)
            link(dve.tensor_copy(logit[:, :, 0:E], ps[:, :, :]))
            for t in range(NT):
                last = dve.max(best[:, t, :], logit[:, t, 0:E])
            link(last)
            link(dve.tensor_copy(two[:, :, 0:2], best[:, :, 0:2]))
            dve.tensor_tensor(diff[:, :, :], logit[:, :, 0:E], best[:, :, 0:1].to_broadcast([P, NT, E]),
                              ALU.subtract).then_inc(diff_ready, 1)
            for t in range(NT):
                last = dve.match_replace(rep[:, t, :], two[:, t, :], logit[:, t, :], -1e38)
            link(last)
            link(dve.tensor_tensor(picked[:, :, :], rep[:, :, 0:E], logit[:, :, 0:E], ALU.not_equal))
            dve.wait_ge(ex_ready, 1)
            link(dve.tensor_tensor(picked[:, :, :], picked[:, :, :], ex[:, :, :], ALU.mult))
            link(dve.tensor_reduce(total[:, :, 0], picked[:, :, :], AX, ALU.add))
            link(dve.reciprocal(inv[:, :, :], total[:, :, :]))
            dve.tensor_tensor(picked[:, :, :], picked[:, :, :], inv[:, :, :].to_broadcast([P, NT, E]),
                              ALU.mult).then_inc(ready, 1)


def experts(nc, xT, comb, w_gate, w_up, w_down, E, C, yT, tag):
    S = 2 * C
    HALF = N // 2
    with ExitStack() as ctx:
        m = Memory(nc, ctx, tag)
        wg = [m.sb(f"wg{i}", [P, C, P]) for i in range(2)]
        wu = [m.sb(f"wu{i}", [P, C, P]) for i in range(2)]
        wd = [m.sb(f"wd{i}", [P, C, D]) for i in range(2)]
        cb = [m.sb(f"cb{i}", [P, N]) for i in range(2)]
        sil = [m.sb(f"sil{i}", [P, HALF]) for i in range(2)]
        act_up = [m.sb(f"act_up{i}", [P, HALF]) for i in range(2)]
        hid = [m.sb(f"hid{i}", [P, HALF]) for i in range(2)]
        zero = m.sb("zero", [P, P])
        gp = [m.ps(f"gp{i}", [P, HALF]) for i in range(2)]
        up = [m.ps(f"up{i}", [P, HALF]) for i in range(2)]
        yp = m.ps("yp", [P, 2, HALF])
        loaded = [m.sem(f"loaded{i}") for i in range(2)]
        zeroed, projected, sil_ready, product_ready, hid_ready, summed, out_ready = (
            m.sem("zeroed"), m.sem("projected"), m.sem("sil_ready"), m.sem("product_ready"), m.sem("hid_ready"),
            m.sem("summed"), m.sem("out_ready"))
        CREDIT = S + 2
        block = ctx.enter_context(nc.Block())

        def each_expert(eng, one):
            with eng.Fori(0, E // 2) as ep:
                for par in range(2):
                    one(ep * 2 + par, par)
            if E % 2:
                one(E - 1, 0)

        @block.sync
        def _(sp):
            def one(e, par):
                sp.wait_ge(summed, e * S + (CREDIT - S))
                sp.dma_start(wg[par][:, :, :], w_gate[ds(e, 1)].rearrange("o p (c i) -> (o p) c i", c=C)).then_inc(loaded[par], 16)
                sp.dma_start(wu[par][:, :, :], w_up[ds(e, 1)].rearrange("o p (c i) -> (o p) c i", c=C)).then_inc(loaded[par], 16)
                sp.dma_start(wd[par][:, :, :], w_down[ds(e, 1)].rearrange("o (c p) d -> p (o c) d", p=P)).then_inc(loaded[par], 16)
                sp.dma_start(cb[par][:, :], comb[ds(e, 1), :].partition_broadcast(P).rearrange(
                    "p o n -> p (o n)")).then_inc(loaded[par], 16)

            each_expert(sp, one)

        def load_count(e, par):
            return 64 * (E // 2 + 1) if isinstance(e, int) else (e - par) * 32 + 64

        @block.tensor
        def _(pe):
            def one(e, par):
                pe.wait_ge(loaded[par], load_count(e, par))
                for i in range(S + 1):
                    if i < S:
                        c, half, buf = i // 2, i % 2, i % 2
                        pe.wait_ge(product_ready, e * S + (i + 1))
                        cols = slice(half * HALF, (half + 1) * HALF)
                        pe.matmul(gp[buf][:, :], wg[par][:, c, :], xT[:, cols], start=True, stop=True)
                        pe.matmul(up[buf][:, :], wu[par][:, c, :], xT[:, cols], start=True, stop=True).then_inc(projected, 1)
                    if i >= 1:
                        c, half, buf = (i - 1) // 2, (i - 1) % 2, (i - 1) % 2
                        pe.wait_ge(hid_ready, e * S + i)
                        pe.matmul(yp[:, half, :], wd[par][:, c, :], hid[buf][:, :], start=False, stop=False,
                                  skip_group_check=True).then_inc(summed, 1)

            pe.wait_ge(zeroed, 1)
            for half in range(2):
                pe.matmul(yp[:, half, :], zero[:, :], xT[:, half * HALF:(half + 1) * HALF], start=True, stop=False,
                          skip_group_check=True)
            pe.sem_inc(summed, CREDIT)
            each_expert(pe, one)
            for half in range(2):
                last = pe.matmul(yp[:, half, :], zero[:, :], xT[:, half * HALF:(half + 1) * HALF], start=False,
                                 stop=True, skip_group_check=True)
            last.then_inc(out_ready, 1)

        @block.scalar
        def _(act):
            def one(e, par):
                for i in range(S):
                    act.wait_ge(projected, e * S + (i + 1))
                    act.wait_ge(product_ready, e * S + (i + 1))
                    act.activation(sil[i % 2][:, :], gp[i % 2][:, :], ACT.Silu).then_inc(sil_ready, 1)

            each_expert(act, one)
            act.wait_ge(out_ready, 1)
            for half in range(2):
                act.copy(yT[:, half * HALF:(half + 1) * HALF], yp[:, half, :])

        @block.vector
        def _(dve):
            dve.memset(zero[:, :], 0.0).then_inc(zeroed, 1)
            dve.sem_inc(product_ready, 2)

            def one(e, par):
                for i in range(S):
                    half = i % 2
                    dve.wait_ge(sil_ready, e * S + (i + 1))
                    dve.tensor_tensor(act_up[i % 2][:, :], sil[i % 2][:, :], up[i % 2][:, :],
                                      ALU.mult).then_inc(product_ready, 1)
                    dve.wait_ge(product_ready, e * S + (i + 3))
                    dve.wait_ge(summed, e * S + (i - 1 + CREDIT))
                    if i == 0:
                        dve.wait_ge(loaded[par], load_count(e, par))
                    dve.tensor_tensor(hid[i % 2][:, :], act_up[i % 2][:, :],
                                      cb[par][:, half * HALF:(half + 1) * HALF], ALU.mult).then_inc(hid_ready, 1)

            each_expert(dve, one)


def add_gated(nc, yT, gate, xs, ident, tag):
    with ExitStack() as ctx:
        m = Memory(nc, ctx, tag)
        gt, th = m.sb("gt", [P, 1]), m.sb("th", [P, 1])
        tp = m.ps("tp", [P, NT, P])
        loaded, gate_ready, turned = m.sem("loaded"), m.sem("gate_ready"), m.sem("turned")
        block = ctx.enter_context(nc.Block())

        @block.sync
        def _(sp):
            sp.dma_start(gt[:, :], gate.partition_broadcast(P)).then_inc(loaded, 16)

        @block.scalar
        def _(act):
            act.wait_ge(loaded, 16)
            act.activation(th[:, :], gt[:, :], ACT.Tanh).then_inc(gate_ready, 1)

        @block.tensor
        def _(pe):
            for t in range(NT):
                last = pe.transpose(tp[:, t, :], yT[:, t * P:(t + 1) * P], ident[:, :])
                if t % 4 == 3:
                    last.then_inc(turned, 1)

        @block.vector
        def _(dve):
            dve.wait_ge(gate_ready, 1)
            for t in range(NT):
                if t % 4 == 0:
                    dve.wait_ge(turned, t // 4 + 1)
                dve.scalar_tensor_tensor(out=xs[:, t, :], in0=tp[:, t, :], scalar=th[:, 0:1], in1=xs[:, t, :],
                                         op0=ALU.mult, op1=ALU.add)


ROUND = 12582912.0


def quantized_ffn(nc, xT, w_inT, b_in, w_out, b_out, ident, yT, tag):
    F = 512
    C, HALF = F // P, N // 2
    with ExitStack() as ctx:
        m = Memory(nc, ctx, tag)
        wi, wo = m.sb("wi", [P, C, D]), m.sb("wo", [P, C, D])
        bi, bo = m.sb("bi", [P, C]), m.sb("bo", [P, 1])
        wq, wqT = m.sb("wq", [P, C, D]), m.sb("wqT", [P, C, P], BF16)
        ws = m.sb("ws", [P, C, D])
        wmax, wstep, wmul = m.sb("wmax", [P, 2, C]), m.sb("wstep", [P, 2, C]), m.sb("wmul", [P, 2, C])
        ones = m.sb("ones", [1, P])
        xmax, row, xstep, xmul, xall = (m.sb("xmax", [P, 1]), m.sb("row", [1, 1]), m.sb("xstep", [P, 2]),
                                        m.sb("xmul", [P, 2]), m.sb("xall", [P, 1]))
        hmax = m.sb("hmax", [P, 1])
        xq, xhi, xlo = m.sb("xq", [P, N]), m.sb("xhi", [P, N], BF16), m.sb("xlo", [P, N], BF16)
        fs = m.sb("fs", [P, C])
        hid = m.sb("hid", [P, C, N])
        small = m.ps("small", [P, P])
        bc = m.ps("bc", [P, 1])
        wt = m.ps("wt", [P, C, P])
        hp = m.ps("hp", [P, 2, HALF])
        yp = m.ps("yp", [P, 2, HALF])
        loaded, step, asked, given, hid_ready, hp_ready, y_ready, ready = (
            m.sem("loaded"), m.sem("step"), m.sem("asked"), m.sem("given"), m.sem("hid_ready"),
            m.sem("hp_ready"), m.sem("y_ready"), m.sem("ready"))
        block = ctx.enter_context(nc.Block())

        @block.sync
        def _(sp):
            sp.dma_start(wi[:, :, :], w_inT.rearrange("(c p) d -> p c d", p=P)).then_inc(loaded, 16)
            sp.dma_start(wo[:, :, :], w_out.rearrange("(c p) d -> p c d", p=P)).then_inc(loaded, 16)
            sp.dma_start(bi[:, :], b_in).then_inc(loaded, 16)
            sp.dma_start(bo[:, :], b_out.unsqueeze(1)).then_inc(loaded, 16)

        @block.vector
        def _(dve):
            link = chain(dve, step)
            link(dve.memset(ones[:, :], 1.0))

            def global_max(column, i, before):
                dve.sem_inc(asked, 1)
                dve.wait_ge(given, before + 1)
                link(dve.tensor_reduce(row[:, :], small[0:1, :], AX, ALU.max))
                dve.sem_inc(asked, 1)
                dve.wait_ge(given, before + 2)
                link(dve.tensor_scalar(xall[:, :], bc[:, :], 1e-8, None, ALU.max))
                link(dve.tensor_scalar(xmul[:, i:i + 1], xall[:, :], 1.0 / 32767.0, None, ALU.mult))
                link(dve.reciprocal(xstep[:, i:i + 1], xall[:, :]))
                link(dve.tensor_scalar(xstep[:, i:i + 1], xstep[:, i:i + 1], 32767.0, None, ALU.mult))

            link(dve.tensor_reduce(xmax[:, :], xT[:, :], AX, ALU.max, apply_absolute_value=True))
            global_max(xmax, 0, 0)
            link(dve.tensor_scalar(xq[:, :], xT[:, :], xstep[:, 0:1], ROUND, ALU.mult, ALU.add))
            link(dve.tensor_scalar(xq[:, :], xq[:, :], -ROUND, 32767.0, ALU.add, ALU.min))
            link(dve.tensor_scalar(xq[:, :], xq[:, :], -32768.0, None, ALU.max))
            link(dve.tensor_copy(xhi[:, :], xq[:, :]))
            link(dve.tensor_tensor(xlo[:, :], xq[:, :], xhi[:, :], ALU.subtract))
            dve.wait_ge(loaded, 64)
            for i, w in enumerate((wi, wo)):
                link(dve.tensor_reduce(wmax[:, i, :], w[:, :, :], AX, ALU.max, apply_absolute_value=True))
            link(dve.tensor_scalar(wmax[:, :, :], wmax[:, :, :], 1e-8, None, ALU.max))
            link(dve.tensor_scalar(wmul[:, :, :], wmax[:, :, :], 1.0 / 127.0, None, ALU.mult))
            link(dve.reciprocal(wstep[:, :, :], wmax[:, :, :]))
            link(dve.tensor_scalar(wstep[:, :, :], wstep[:, :, :], 127.0, None, ALU.mult))
            for i, (w, q) in enumerate(((wi, wq), (wo, ws))):
                for c in range(C):
                    link(dve.tensor_scalar(q[:, c, :], w[:, c, :], wstep[:, i, c:c + 1], ROUND, ALU.mult, ALU.add))
                link(dve.tensor_scalar(q[:, :, :], q[:, :, :], -ROUND, 127.0, ALU.add, ALU.min))
                link(dve.tensor_scalar(q[:, :, :], q[:, :, :], -128.0, None, ALU.max))
            for c in range(C):
                link(dve.tensor_scalar(ws[:, c, :], ws[:, c, :], wmul[:, 1, c:c + 1], None, ALU.mult))
            link(dve.tensor_scalar(fs[:, :], wmul[:, 0, :], xmul[:, 0:1], None, ALU.mult))
            dve.sem_inc(asked, 1)
            dve.wait_ge(given, 3)
            dve.tensor_copy(wqT[:, :, :], wt[:, :, :]).then_inc(ready, 1)
            dve.wait_ge(hid_ready, 2 * C)
            link(dve.tensor_reduce(hmax[:, :], hid[:, :, :].rearrange("p c n -> p (c n)"), AX, ALU.max,
                                   apply_absolute_value=True))
            global_max(hmax, 1, 3)
            for c in range(C):
                link(dve.tensor_scalar(hid[:, c, :], hid[:, c, :], xstep[:, 1:2], ROUND, ALU.mult, ALU.add))
                link(dve.tensor_scalar(hid[:, c, :], hid[:, c, :], -ROUND, 32767.0, ALU.add, ALU.min))
                dve.tensor_scalar(hid[:, c, :], hid[:, c, :], -32768.0, None, ALU.max).then_inc(ready, 1)
            dve.wait_ge(y_ready, 1)
            for half in range(2):
                dve.tensor_scalar(yT[:, half * HALF:(half + 1) * HALF], yp[:, half, :], xmul[:, 1:2], bo[:, 0:1],
                                  ALU.mult, ALU.add)

        @block.tensor
        def _(pe):
            pe.wait_ge(asked, 1)
            pe.transpose(small[0:1, :], xmax[:, :], ident[:, :]).then_inc(given, 1)
            pe.wait_ge(asked, 2)
            pe.matmul(bc[:, :], ones[:, :], row[:, :], start=True, stop=True).then_inc(given, 1)
            pe.wait_ge(asked, 3)
            for c in range(C):
                last = pe.transpose(wt[:, c, :], wq[:, c, :], ident[:, :])
            last.then_inc(given, 1)
            pe.wait_ge(ready, 1)
            for c in range(C):
                for half in range(2):
                    if c:
                        pe.wait_ge(hid_ready, 2 * (c - 1) + half + 1)
                    cols = slice(half * HALF, (half + 1) * HALF)
                    pe.matmul(hp[:, half, :], wqT[:, c, :], xhi[:, cols], start=True, stop=False)
                    pe.matmul(hp[:, half, :], wqT[:, c, :], xlo[:, cols], start=False, stop=True).then_inc(hp_ready, 1)
            pe.wait_ge(asked, 4)
            pe.transpose(small[0:1, :], hmax[:, :], ident[:, :]).then_inc(given, 1)
            pe.wait_ge(asked, 5)
            pe.matmul(bc[:, :], ones[:, :], row[:, :], start=True, stop=True).then_inc(given, 1)
            for c in range(C):
                pe.wait_ge(ready, c + 2)
                for half in range(2):
                    last = pe.matmul(yp[:, half, :], ws[:, c, :], hid[:, c, half * HALF:(half + 1) * HALF],
                                     start=(c == 0), stop=(c == C - 1))
            last.then_inc(y_ready, 1)

        @block.scalar
        def _(act):
            act.wait_ge(loaded, 64)
            for c in range(C):
                for half in range(2):
                    act.wait_ge(hp_ready, 2 * c + half + 1)
                    act.activation(hid[:, c, half * HALF:(half + 1) * HALF], hp[:, half, :], ACT.Gelu,
                                   bias=bi[:, c:c + 1], scale=fs[:, c:c + 1]).then_inc(hid_ready, 1)



DEPTH = 6
LH, LD = 16, 64
PAIRS = LH // 2
WIN = 32
TQ = P - WIN
LT = -(-N // TQ)
NPAD = WIN + LT * TQ
FC = 3
NORM_FLOOR = 1e-12


def local_transformer(nc, zT, a, ident):
    HALF = N // 2
    STEPS = 4 * PAIRS
    R0 = 6
    G4 = LH // 4
    with ExitStack() as ctx:
        m = Memory(nc, ctx, "lt")
        sT = m.sb("sT", [P, NPAD])
        cs = m.sb("cs", [P, 4, N])
        qsc = m.sb("qsc", [P, DEPTH, 4])
        gain, shift, bias2 = m.sb("gain", [P, DEPTH]), m.sb("shift", [P, DEPTH]), m.sb("bias2", [P, DEPTH])
        bias1 = m.sb("bias1", [P, DEPTH, 2, FC])
        eps = m.sb("eps", [P, 1])
        head_ones, mean_ones = m.sb("head_ones", [P, P]), m.sb("mean_ones", [P, P])
        band = m.sb("band", [P, 2, 4, P], BF16)
        identb = m.sb("identb", [P, TQ], BF16)
        w4 = [m.sb(f"w4{i}", [P, 4, P]) for i in range(2)]
        wv, wo = m.sb("wv", [P, LH * LD]), m.sb("wo", [P, PAIRS, D])
        w1, w2 = m.sb("w1", [P, 2, FC, P]), m.sb("w2", [P, FC, D])
        wide = m.sb("wide", [P, 12, HALF])
        sq, nrm, t1, t2, t3, rn = ([wide[:, 2 * n + i, :] for i in range(2)] for n in range(6))
        ex = [[wide[0:TQ, 4 * par + g, :].rearrange("p (h c) -> p h c", h=4) for g in range(4)] for par in range(2)]
        qk = [m.sb("qT", [P, PAIRS, NPAD]), m.sb("kT", [P, PAIRS, NPAD])]
        oT = m.sb("oT", [P, PAIRS, LT * TQ])
        q_cur, s_cur = [m.sb(f"q_cur{i}", [P, PAIRS, TQ]) for i in range(2)], [m.sb(f"s_cur{i}", [P, P]) for i in range(2)]
        k_cur = [m.sb("k_cur", [P, PAIRS, 2, P])[:, :, :, :],
                 wide[:, 8:12, :].rearrange("p a (j s c) -> p (a j) s c", j=2, s=2)]
        v_cur = [m.sb(f"v_cur{i}", [P, LH * LD]) for i in range(2)]
        nmax, rsum, rinv = ([m.sb(f"{n}{i}", [TQ, 4, 1]) for i in range(4)] for n in ("nmax", "rsum", "rinv"))
        pT = [m.sb(f"pT{i}", [P, 4, TQ]) for i in range(2)]
        bank = [m.ps(f"bank{i}", [P, 512]) for i in range(8)]
        S = {n: m.sem(n) for n in (
            "loaded", "table_loaded", "setup", "w4_0", "w4_1", "wvo", "w12", "shifted", "tables", "proj", "sq_ready", "normed",
            "nrm_ready", "t2_ready", "t3_ready", "rn_ready", "roped", "staged", "v_done", "v_ready", "sc_done",
            "maxed", "subbed", "exped", "rs_ready", "rinv_ready", "norm_ready", "turned", "pt_ready", "pv_done",
            "o_ready", "y_done", "z_ready", "mean_done", "xc_ready", "xsq_ready", "var_done", "std_ready",
            "rstd_ready", "xn_half", "xn_mul", "xn_ready", "h_done", "gelu_ready", "hh_ready", "f_done", "settled", "psettled", "vsettled", "asettled",
            "cleared")}
        LOADS = 16 * 7
        block = ctx.enter_context(nc.Block())
        half_cols = [slice(WIN + h * HALF, WIN + (h + 1) * HALF) for h in range(2)]

        def pairs(eng, layer, one):
            with eng.Fori(0, PAIRS // 2) as jp:
                for par in range(2):
                    one(layer, jp * 2 + par, par)

        score_bank = [bank[2], bank[3], bank[6], bank[7]]
        turn_bank, value_bank, out_bank = [bank[4], bank[5]], bank[0], bank[1]

        def tiles(eng, layer, one):
            n = layer * LT
            one(n, 0, None, 1, None)
            with eng.Fori(0, LT // 2) as i:
                one(n + i * 2 + 1, 1, n + i * 2, 0, i * 2)
                one(n + i * 2 + 2, 0, n + i * 2 + 1, 1, i * 2 + 1)
            one(None, 1, n + (LT - 1), 0, LT - 1)

        @block.sync
        def _(sp):
            for dst, src in ((qsc[:, :, :], a["lt_qsc"]), (gain[:, :], a["lt_g"]),
                             (shift[:, :], a["lt_b"]), (bias2[:, :], a["lt_b2"]), (bias1[:, :, :, :], a["lt_b1"]),
                             (head_ones[:, :], a["lt_head_ones"]), (mean_ones[:, :], a["lt_mean_ones"])):
                sp.dma_start(dst, src).then_inc(S["loaded"], 16)
            with sp.Fori(0, DEPTH) as layer:
                sp.wait_ge(S["roped"], layer * STEPS + R0)
                sp.dma_start(cs[:, :, :], a["lt_table"]).then_inc(S["table_loaded"], 16)
                sp.wait_ge(S["y_done"], layer + 1)
                sp.dma_start(wv[:, :], a["lt_wv"][ds(layer, 1)].rearrange("o p n -> p (o n)")).then_inc(S["wvo"], 16)
                sp.dma_start(wo[:, :, :], a["lt_wo"][ds(layer, 1)].rearrange("o (j p) d -> p (o j) d", p=P)).then_inc(S["wvo"], 16)

                def one(layer, j, par):
                    sp.wait_ge(S["roped"], layer * STEPS + j * 4 + (R0 - 4))
                    sp.dma_start(w4[par][:, :, :], a["lt_w4"][ds(layer, 1), ds(j, 1)].rearrange(
                        "o q p (s n) -> p (o q s) n", s=4)).then_inc(S[f"w4_{par}"], 16)

                pairs(sp, layer, one)
                sp.wait_ge(S["f_done"], layer + 1)
                sp.dma_start(w1[:, :, :, :], a["lt_w1"][ds(layer, 1)].rearrange(
                    "o p (s c i) -> p (o s) c i", s=2, c=FC)).then_inc(S["w12"], 16)
                sp.dma_start(w2[:, :, :], a["lt_w2"][ds(layer, 1)].rearrange("o (c p) d -> p (o c) d", p=P)).then_inc(S["w12"], 16)

        @block.tensor
        def _(pe):
            pe.wait_ge(S["loaded"], LOADS)
            pe.wait_ge(S["setup"], 7)
            pe.sem_inc(S["y_done"], 1)
            pe.sem_inc(S["f_done"], 1)
            pe.sem_inc(S["sc_done"], 5)
            pe.sem_inc(S["turned"], 8)
            pe.sem_inc(S["pv_done"], 5)
            with pe.Fori(0, DEPTH) as layer:
                pe.wait_ge(S["shifted"], layer * 2 + 1)
                settle(pe, S["settled"])

                def pair(layer, j, par):
                    pe.wait_ge(S[f"w4_{par}"], layer * (PAIRS // 2 * 16) + (j - par) * 8 + 16)
                    for i in range(5):
                        n = layer * STEPS + j * 4
                        if i < 4:
                            which, half, buf = i // 2, i % 2, i % 2
                            pe.wait_ge(S["roped"], n + (i + R0 - 1))
                            pe.matmul(bank[buf][:, :], w4[par][:, 2 * which, :], sT[:, half_cols[half]], start=True, stop=True)
                            pe.matmul(bank[2 + buf][:, :], w4[par][:, 2 * which + 1, :], sT[:, half_cols[half]],
                                      start=True, stop=True).then_inc(S["proj"], 1)
                        if i >= 1:
                            buf = (i - 1) % 2
                            pe.wait_ge(S["sq_ready"], n + i)
                            pe.matmul(bank[4 + buf][:, :], head_ones[:, :], sq[buf], start=True,
                                      stop=True).then_inc(S["normed"], 1)

                pairs(pe, layer, pair)
                pe.wait_ge(S["wvo"], layer * 32 + 32)

                def values(n, par, half):
                    pe.wait_ge(S["v_ready"], n * 2 + (half + 1))
                    settle(pe, S["settled"])
                    pe.matmul(value_bank[:, :], s_cur[par][:, :], wv[:, half * 512:(half + 1) * 512], start=True,
                              stop=True).then_inc(S["v_done"], 1)

                def scores(n, par, g, mask):
                    pe.wait_ge(S["subbed"], n * G4 + (g + 1))
                    sc = score_bank[g]
                    pe.matmul(sc[0:TQ, :], identb[:, :], band[:, mask, :, :].rearrange("p h c -> p (h c)"),
                              start=True, stop=False, skip_group_check=True)
                    for q in range(2):
                        last = pe.matmul(sc[0:TQ, q * 2 * P:(q + 1) * 2 * P], q_cur[par][:, 2 * g + q, :],
                                         k_cur[par][:, 2 * g + q, :, :].rearrange("p s c -> p (s c)"), start=False,
                                         stop=(q == 1), skip_group_check=True)
                    last.then_inc(S["sc_done"], 1)

                def turn(n, par, g):
                    pe.wait_ge(S["norm_ready"], n * G4 + (g + 5))
                    pe.wait_ge(S["pt_ready"], n * G4 + (g + 1))
                    settle(pe, S["settled"])
                    for h in range(4):
                        last = pe.transpose(turn_bank[g % 2][:, h * TQ:(h + 1) * TQ], ex[par][g][:, h, :],
                                            ident[0:TQ, 0:TQ])
                    last.then_inc(S["turned"], 1)

                def outputs(n, par, g):
                    pe.wait_ge(S["pt_ready"], n * G4 + (g + 3))
                    pe.wait_ge(S["v_ready"], n * 2 + 3)
                    pe.wait_ge(S["o_ready"], n * G4 + (g + 1))
                    settle(pe, S["settled"])
                    for h in range(4):
                        last = pe.matmul(out_bank[64 * (h % 2):64 * (h % 2) + 64, (h // 2) * TQ:(h // 2 + 1) * TQ],
                                         v_cur[par][:, (4 * g + h) * LD:(4 * g + h + 1) * LD], pT[g % 2][:, h, :],
                                         start=True, stop=True, skip_group_check=True)
                    last.then_inc(S["pv_done"], 1)

                def one(n, par, b, bpar, t):
                    if n is not None:
                        pe.wait_ge(S["staged"], n + 1)
                    for g in range(G4 + 1):
                        if n is not None and g < G4:
                            if g % 2 == 0:
                                values(n, par, g // 2)
                            scores(n, par, g, 0 if b is None else 1)
                        if b is not None:
                            if g < G4:
                                turn(b, bpar, g)
                            if g >= 1:
                                outputs(b, bpar, g - 1)

                tiles(pe, layer, one)
                pe.wait_ge(S["o_ready"], layer * (LT * G4) + (LT * G4 + 1))
                for half in range(2):
                    for j in range(PAIRS):
                        last = pe.matmul(bank[6 + half][:, :], wo[:, j, :], oT[:, j, half * HALF:(half + 1) * HALF],
                                         start=(j == 0), stop=(j == PAIRS - 1))
                last.then_inc(S["y_done"], 1)

                pe.wait_ge(S["shifted"], layer * 2 + 2)
                for half in range(2):
                    pe.matmul(bank[half][:, :], mean_ones[:, :], sT[:, half_cols[half]], start=True,
                              stop=True).then_inc(S["mean_done"], 1)
                for half in range(2):
                    pe.wait_ge(S["xsq_ready"], layer * 2 + (half + 1))
                    pe.matmul(bank[2 + half][:, :], mean_ones[:, :], sq[half], start=True,
                              stop=True).then_inc(S["var_done"], 1)
                pe.wait_ge(S["w12"], layer * 32 + 32)
                for i in range(2 * FC + 1):
                    n = layer * (2 * FC)
                    if i < 2 * FC:
                        c, half = i // 2, i % 2
                        if c == 0:
                            pe.wait_ge(S["xn_ready"], layer * 2 + (half + 1))
                        else:
                            pe.wait_ge(S["hh_ready"], n + (i - 1))
                        for s in range(2):
                            last = pe.matmul(bank[4 * s + half][:, :], w1[:, s, c, :], nrm[half], start=True, stop=True)
                        last.then_inc(S["h_done"], 1)
                    if i >= 1:
                        c, half = (i - 1) // 2, (i - 1) % 2
                        pe.wait_ge(S["hh_ready"], n + i)
                        last = pe.matmul(bank[6 + half][:, :], w2[:, c, :], t1[half], start=(c == 0), stop=(c == FC - 1))
                last.then_inc(S["f_done"], 1)

        @block.scalar
        def _(act):
            act.sem_inc(S["pt_ready"], 2)
            act.sem_inc(S["v_ready"], 1)
            with act.Fori(0, DEPTH) as layer:
                def pair(layer, j, par):
                    n = layer * STEPS + j * 4
                    for i in range(5):
                        if i < 4:
                            act.wait_ge(S["proj"], n + (i + 1))
                            act.activation(sq[i % 2], bank[i % 2][:, :], ACT.Square).then_inc(S["sq_ready"], 1)
                        if i >= 1:
                            act.wait_ge(S["normed"], n + i)
                            act.activation(nrm[(i - 1) % 2], bank[4 + (i - 1) % 2][:, :],
                                           ACT.Sqrt).then_inc(S["nrm_ready"], 1)

                pairs(act, layer, pair)

                def copy_values(n, par, half):
                    act.wait_ge(S["v_done"], n * 2 + (half + 1))
                    act.wait_ge(S["pv_done"], n * G4 + 1)
                    act.copy(v_cur[par][:, half * 512:(half + 1) * 512], value_bank[:, :]).then_inc(S["v_ready"], 1)

                def one(n, par, b, bpar, t):
                    for g in range(G4):
                        if n is not None and g == 0:
                            copy_values(n, par, 0)
                        if b is not None:
                            act.wait_ge(S["turned"], b * G4 + (g + 9))
                            act.wait_ge(S["pv_done"], b * G4 + (g + 4))
                            act.copy(pT[g % 2][:, :, :].rearrange("p h q -> p (h q)"),
                                     turn_bank[g % 2][:, 0:4 * TQ]).then_inc(S["pt_ready"], 1)
                        if n is not None:
                            if g == 1:
                                copy_values(n, par, 1)
                            act.wait_ge(S["subbed"], n * G4 + (g + 5))
                            act.activation(ex[par][g], ex[par][g], ACT.Exp).then_inc(S["exped"], 1)

                tiles(act, layer, one)
                for half in range(2):
                    act.wait_ge(S["xc_ready"], layer * 2 + (half + 1))
                    act.activation(sq[half], t3[half], ACT.Square).then_inc(S["xsq_ready"], 1)
                for half in range(2):
                    act.wait_ge(S["var_done"], layer * 2 + (half + 1))
                    act.activation(t2[half], bank[2 + half][:, :], ACT.Sqrt, bias=eps[:, 0:1]).then_inc(S["std_ready"], 1)
                for i in range(2 * FC):
                    c, half = i // 2, i % 2
                    act.wait_ge(S["h_done"], layer * (2 * FC) + (i + 1))
                    if c:
                        act.wait_ge(S["hh_ready"], layer * (2 * FC) + (i - 1))
                    settle(act, S["asettled"])
                    act.activation(t2[half], bank[4 + half][:, :], ACT.Gelu,
                                   bias=bias1[:, ds(layer, 1), 1, c:c + 1].rearrange("p o i -> p (o i)")).then_inc(S["gelu_ready"], 1)

        @block.gpsimd
        def _(pool):
            for ap in (sT[:, :], qk[0][:, :, :], qk[1][:, :, :]):
                pool.memset(ap, 0.0).then_inc(S["cleared"], 1)
            pool.wait_ge(S["loaded"], LOADS)
            pool.wait_ge(S["cleared"], 3)
            pool.memset(identb[:, :], 0.0).then_inc(S["setup"], 1)
            pool.memset(band[:, :, :, :], 0.0).then_inc(S["setup"], 1)
            pool.memset(eps[:, :], EPS).then_inc(S["setup"], 1)
            pool.wait_ge(S["setup"], 3)
            pool.affine_select(out=identb[:, :], in_=identb[:, :], compare_op=ALU.not_equal, fill=1.0, base=0,
                               pattern=[[-1, TQ]], channel_multiplier=1).then_inc(S["setup"], 1)
            flat = band[:, :, :, :].rearrange("p a h c -> p (a h) c")
            pool.affine_select(out=flat, in_=flat, compare_op=ALU.is_ge, fill=NEG1, base=0,
                               pattern=[[0, 8], [1, P]], channel_multiplier=-1).then_inc(S["setup"], 1)
            pool.wait_ge(S["setup"], 5)
            pool.affine_select(out=flat, in_=flat, compare_op=ALU.is_ge, fill=NEG1, base=WIN,
                               pattern=[[0, 8], [-1, P]], channel_multiplier=1).then_inc(S["setup"], 1)
            pool.wait_ge(S["setup"], 6)
            pool.memset(band[:, 0, :, 0:WIN], NEG1).then_inc(S["setup"], 1)
            pool.wait_ge(S["setup"], 7)
            pool.sem_inc(S["norm_ready"], 4)
            with pool.Fori(0, DEPTH) as layer:
                def pair(layer, j, par):
                    for i in range(4):
                        pool.wait_ge(S["t2_ready"], layer * STEPS + j * 4 + (i + 1))
                        settle(pool, S["psettled"])
                        pool.tensor_tensor(t3[i % 2], t1[i % 2], t2[i % 2], ALU.add).then_inc(S["t3_ready"], 1)

                pairs(pool, layer, pair)
                pool.wait_ge(S["roped"], layer * STEPS + (STEPS + R0))

                def stage(n, t, par):
                    pool.wait_ge(S["sc_done"], n * G4 + 1)
                    settle(pool, S["psettled"])
                    keys, queries_ = (ds(t * TQ, P), ds(t * TQ + WIN, TQ))
                    pool.tensor_copy(s_cur[par][:, :], sT[:, keys])
                    pool.tensor_copy(q_cur[par][:, :, :], qk[0][:, :, queries_])
                    for s in range(2):
                        last = pool.tensor_tensor(k_cur[par][:, :, s, :], qk[1][:, :, keys],
                                                  head_ones[:, 64 * s:64 * s + 1].unsqueeze(2).to_broadcast(
                                                      [P, PAIRS, P]), ALU.mult)
                    last.then_inc(S["staged"], 1)

                def normalise(n, par):
                    for g in range(G4):
                        pool.wait_ge(S["rinv_ready"], n * G4 + (g + 1))
                        settle(pool, S["psettled"])
                        pool.tensor_tensor(ex[par][g], ex[par][g], rinv[g][:, :, :].to_broadcast([TQ, 4, P]),
                                           ALU.mult).then_inc(S["norm_ready"], 1)

                n = layer * LT
                stage(n, 0, 0)
                with pool.Fori(0, LT // 2) as i:
                    for par in range(2):
                        stage(n + i * 2 + (par + 1), i * 2 + (par + 1), 1 - par)
                        normalise(n + i * 2 + par, par)
                normalise(n + (LT - 1), 0)

        @block.vector
        def _(dve):
            dve.wait_ge(S["loaded"], LOADS)
            dve.wait_ge(S["cleared"], 3)
            dve.sem_inc(S["roped"], R0)
            dve.sem_inc(S["subbed"], 4)
            dve.sem_inc(S["o_ready"], 1)
            dve.sem_inc(S["z_ready"], 1)

            def shift_tokens():
                dve.tensor_copy(sT[0:64, WIN:WIN + N], zT[0:64, :])
                dve.tensor_copy(sT[64:P, WIN + 1:WIN + N], zT[64:P, 0:N - 1]).then_inc(S["shifted"], 1)

            with dve.Fori(0, DEPTH) as layer:
                dve.wait_ge(S["z_ready"], layer * 4 + 1)
                shift_tokens()
                dve.wait_ge(S["table_loaded"], layer * 16 + 16)
                for i in range(4):
                    last = dve.tensor_scalar(cs[:, i, :], cs[:, i, :], qsc[:, ds(layer, 1), i:i + 1].rearrange(
                        "p o i -> p (o i)"), None, ALU.mult)
                last.then_inc(S["tables"], 1)
                dve.wait_ge(S["tables"], layer + 1)
                settle(dve, S["vsettled"])

                def pair(layer, j, par):
                    n = layer * STEPS + j * 4
                    for i in range(5):
                        if i < 4:
                            which, half, buf = i // 2, i % 2, i % 2
                            cols = slice(half * HALF, (half + 1) * HALF)
                            dve.wait_ge(S["sq_ready"], n + (i + 1))
                            dve.wait_ge(S["roped"], n + (i + R0 - 1))
                            dve.tensor_tensor(t1[buf], bank[buf][:, :], cs[:, 2 * which, cols], ALU.mult)
                            dve.tensor_tensor(t2[buf], bank[2 + buf][:, :], cs[:, 2 * which + 1, cols],
                                              ALU.mult).then_inc(S["t2_ready"], 1)
                        if i >= 1:
                            which, half, buf = (i - 1) // 2, (i - 1) % 2, (i - 1) % 2
                            dve.wait_ge(S["nrm_ready"], n + i)
                            dve.reciprocal(rn[buf], nrm[buf]).then_inc(S["rn_ready"], 1)
                            dve.wait_ge(S["rn_ready"], n + i)
                            dve.wait_ge(S["t3_ready"], n + i)
                            dve.scalar_tensor_tensor(
                                out=qk[which][:, ds(j, 1), half_cols[half]].rearrange("p o n -> p (o n)"),
                                in0=rn[buf], scalar=1.0 / NORM_FLOOR, in1=t3[buf], op0=ALU.min,
                                op1=ALU.mult).then_inc(S["roped"], 1)

                pairs(dve, layer, pair)

                def lower_by_max(n, par, g):
                    k = n * G4 + g
                    dve.wait_ge(S["sc_done"], k + 6)
                    sc = score_bank[g][0:TQ, :].rearrange("p (h c) -> p h c", h=4)
                    dve.tensor_reduce(nmax[g][:, :, 0], sc, AX, ALU.max).then_inc(S["maxed"], 1)
                    dve.wait_ge(S["maxed"], k + 1)
                    dve.wait_ge(S["turned"], k + 1)
                    dve.tensor_tensor(ex[par][g], sc, nmax[g][:, :, :].to_broadcast([TQ, 4, P]),
                                      ALU.subtract).then_inc(S["subbed"], 1)

                def denominators(n, par, g):
                    k = n * G4 + g
                    dve.wait_ge(S["exped"], k + 1)
                    dve.tensor_reduce(rsum[g][:, :, 0], ex[par][g], AX, ALU.add).then_inc(S["rs_ready"], 1)
                    dve.wait_ge(S["rs_ready"], k + 1)
                    dve.wait_ge(S["norm_ready"], k + 1)
                    dve.reciprocal(rinv[g][:, :, :], rsum[g][:, :, :]).then_inc(S["rinv_ready"], 1)

                def keep(b, t, g):
                    dve.wait_ge(S["pv_done"], b * G4 + (g + 6))
                    dve.tensor_copy(oT[:, 2 * g:2 * g + 2, ds(t * TQ, TQ)],
                                    out_bank[:, 0:2 * TQ].rearrange("p (j q) -> p j q", j=2)).then_inc(S["o_ready"], 1)

                def one(n, par, b, bpar, t):
                    for g in range(G4 + 1):
                        if n is not None and g < G4:
                            lower_by_max(n, par, g)
                        if g >= 1:
                            if n is not None:
                                denominators(n, par, g - 1)
                            if b is not None:
                                keep(b, t, g - 1)

                tiles(dve, layer, one)
                dve.wait_ge(S["y_done"], layer + 2)
                for half in range(2):
                    cols = slice(half * HALF, (half + 1) * HALF)
                    dve.tensor_tensor(zT[:, cols], zT[:, cols], bank[6 + half][:, :], ALU.add).then_inc(S["z_ready"], 1)
                dve.wait_ge(S["z_ready"], layer * 4 + 3)
                shift_tokens()
                dve.wait_ge(S["shifted"], layer * 2 + 2)
                for half in range(2):
                    dve.wait_ge(S["mean_done"], layer * 2 + (half + 1))
                    dve.tensor_tensor(t3[half], sT[:, half_cols[half]], bank[half][:, :],
                                      ALU.subtract).then_inc(S["xc_ready"], 1)
                for half in range(2):
                    dve.wait_ge(S["std_ready"], layer * 2 + (half + 1))
                    dve.reciprocal(rn[half], t2[half]).then_inc(S["rstd_ready"], 1)
                    dve.wait_ge(S["rstd_ready"], layer * 2 + (half + 1))
                    dve.tensor_tensor(t1[half], t3[half], rn[half], ALU.mult).then_inc(S["xn_mul"], 1)
                    dve.wait_ge(S["xn_mul"], layer * 2 + (half + 1))
                    dve.tensor_scalar(nrm[half], t1[half], gain[:, ds(layer, 1)], shift[:, ds(layer, 1)],
                                      ALU.mult, ALU.add).then_inc(S["xn_ready"], 1)
                for i in range(2 * FC):
                    c, half = i // 2, i % 2
                    n = layer * (2 * FC)
                    dve.wait_ge(S["gelu_ready"], n + (i + 1))
                    if c:
                        dve.wait_ge(S["h_done"], n + (i + 1))
                    dve.scalar_tensor_tensor(out=t1[half], in0=bank[half][:, :],
                                             scalar=bias1[:, ds(layer, 1), 0, c:c + 1].rearrange("p o i -> p (o i)"),
                                             in1=t2[half], op0=ALU.add, op1=ALU.mult).then_inc(S["hh_ready"], 1)
                dve.wait_ge(S["f_done"], layer + 2)
                for half in range(2):
                    cols = slice(half * HALF, (half + 1) * HALF)
                    dve.scalar_tensor_tensor(out=zT[:, cols], in0=bank[6 + half][:, :], scalar=bias2[:, ds(layer, 1)],
                                             in1=zT[:, cols], op0=ALU.add, op1=ALU.add).then_inc(S["z_ready"], 1)


def rotary_tables():
    f = np.float32
    half = np.arange(0, LD, 2, dtype=f)
    inv_freq = f(1.0) / f(10000.0) ** (half / f(LD))
    t = np.arange(N, dtype=f)
    freqs = t[:, None] * inv_freq[None, :]
    base = (half + f(0.4 * LD)) / f(1.4 * LD)
    power = (t - f(N // 2)) / f(WIN // 2)
    scale = base[None, :] ** power[:, None]
    freqs, scale = (np.concatenate([v, v], -1).T.astype(f) for v in (freqs, scale))
    sign = np.where(np.arange(LD) < LD // 2, -1.0, 1.0).astype(f)[:, None]
    cos, sin = np.cos(freqs), np.sin(freqs) * sign
    rows = np.stack([cos * scale * f(8.0), sin * scale * f(8.0), cos / scale, sin / scale])
    return np.concatenate([rows, rows], axis=1).astype(f)


def program(nc, a, out):
    kst = nc.dram_tensor("kst", (LAYERS, NB, H, HROWS, BK), BF16, kind="Internal").ap()
    kmask = nc.dram_tensor("kmask", (LAYERS, 6, KPAD), BF16, kind="Internal").ap()
    vst = nc.dram_tensor("vst", (LAYERS, P, KT, H, VW), F32, kind="Internal").ap()
    qst = nc.dram_tensor("qst", (H, HROWS, N), BF16, kind="Internal").ap()
    comb = nc.dram_tensor("comb", (L0_E + 1, N), F32, kind="Internal").ap()
    score_scale = [1.0 / np.sqrt(D)] + 3 * [1.0 / np.sqrt(HD)]

    with ExitStack() as ctx:
        m = Memory(nc, ctx, "g")
        ident, xs, xT = m.sb("ident", [P, P]), m.sb("xs", [P, NT, D]), m.sb("xT", [P, N])

        def attention(l):
            with ExitStack() as stage:
                s = Memory(nc, stage, f"x{l}")
                top, att = s.sb("top", [P, H * NT]), s.sb("att", [P, NT, D])
                norm_transpose(nc, xs, ident, xT, f"n{l}")
                queries(nc, xT, a[f"wq{l}"], a[f"bq{l}"], float(score_scale[l]), qst, f"q{l}")
                if l == 2:
                    row_threshold(nc, kst[l], qst, top, ident, f"m{l}")
                    set_shift(nc, top, qst, ident, f"s{l}")
                    attend_to_top(nc, kst[l], vst[l], qst, ident, att, f"a{l}")
                else:
                    attend_with_max(nc, kst[l], vst[l], qst, ident, att, f"a{l}")
                project(nc, att, a[f"wo{l}"], a[f"bo{l}"], a["g_xattn"][l:l + 1], xs, ident, f"p{l}")

        def feed_forward(l):
            with ExitStack() as stage:
                s = Memory(nc, stage, f"y{l}")
                norm_transpose(nc, xs, ident, xT, f"nf{l}")
                y = xT if l == 2 else s.sb("yT", [P, N])
                if l == 0:
                    route_sigmoid(nc, xT, a["f0_gate"], a["f0_bias"], ident, comb, "r0")
                    experts(nc, xT, comb, a["f0_wg"], a["f0_wu"], a["f0_wd"], L0_E + 1, 1, y, "e0")
                elif l == 1:
                    quantized_ffn(nc, xT, a["f1_wi"], a["f1_bi"], a["f1_wo"], a["f1_bo"], ident, y, "e1")
                elif l == 2:
                    local_transformer(nc, xT, a, ident)
                else:
                    route_top2(nc, xT, a["f3_router"], ident, comb, "r3")
                    experts(nc, xT, comb, a["f3_wg"], a["f3_wu"], a["f3_wd"], L3_E, L3_C, y, "e3")
                add_gated(nc, y, a["g_ffn"][l:l + 1], xs, ident, f"u{l}")

        make_identity(nc, ident)
        load_rows(nc, a["x"], xs)
        mask_rows(nc, a["mask0"], a["mask1"], a["mask3"], a["padneg"], kmask, kst)
        context_keys_values(nc, a["ctxT"], [a[f"wk{l}"] for l in range(4)], [a[f"bk{l}"] for l in range(4)],
                            [a[f"wv{l}"] for l in range(4)], [a[f"bv{l}"] for l in range(4)], a["valid"],
                            a["mask3t"], kst, vst)
        for l in range(LAYERS):
            attention(l)
            feed_forward(l)
        store_rows(nc, xs, out)


def host_layout(i):
    pad = KPAD - S2
    f = lambda v: np.ascontiguousarray(v)
    a = {"x": f(i["x"]), "ctxT": f(np.pad(np.asarray(i["ctx_1024"])[0].T, ((0, 0), (0, pad))))}
    a["mask0"] = np.pad(np.asarray(i["mask_Bx1x1xS2_if1"]).reshape(-1), (0, pad), constant_values=1)
    a["mask1"] = np.pad(np.asarray(i["mask_Bx1x1xS2_ik0"]).reshape(-1), (0, pad), constant_values=1)
    m3 = np.pad(np.asarray(i["mask_BxS2_bf0"]).reshape(-1), (0, pad), constant_values=True).astype(np.int32)
    a["mask3"] = m3
    a["mask3t"] = f(m3.reshape(KT, P).T)
    valid = (np.arange(KPAD) < S2).astype(np.float32)
    a["valid"] = f(valid.reshape(KT, P).T)
    a["padneg"] = np.where(valid > 0, 0.0, NEG1).astype(np.float32)
    a["g_xattn"], a["g_ffn"] = np.asarray(i["g_xattn"]), np.asarray(i["g_ffn"])
    for l, (q, k, v, o) in enumerate([("Wq", "Wk", "Wv", "Wo"), ("wq", "wk", "wv", "wo"), ("Wq", "Wk", "Wv", "Wo")]):
        for n, s in zip("qkvo", (q, k, v, o)):
            w = np.asarray(i[f"L{l}_xattn_{s}"])
            a[f"w{n}{l}"] = f(w if l == 1 else w.T)
            a[f"b{n}{l}"] = np.asarray(i[f"L{l}_xattn_b{n}"])
    a["wq3"], a["wo3"] = np.asarray(i["L3_xattn_Wq"]), np.asarray(i["L3_xattn_Wout"])
    a["bq3"], a["bo3"] = np.asarray(i["L3_xattn_bq"]), np.asarray(i["L3_xattn_bout"])
    wkv, bkv = np.asarray(i["L3_xattn_Wkv"]), np.asarray(i["L3_xattn_bkv"])
    a["wk3"], a["wv3"], a["bk3"], a["bv3"] = f(wkv[:, :D]), f(wkv[:, D:]), f(bkv[:D]), f(bkv[D:])
    g = lambda n: np.asarray(i[n])
    t = lambda w: f(np.swapaxes(w, -1, -2))
    a["f0_gate"], a["f0_bias"] = t(g("L0_ffn_gate_w")), g("L0_ffn_expert_bias")
    for n, w, shared in (("wg", "w_gate", "shared_gate_w"), ("wu", "w_up", "shared_up_w"), ("wd", "w_down", "shared_down_w")):
        a[f"f0_{n}"] = t(np.concatenate([g(f"L0_ffn_{w}"), g(f"L0_ffn_{shared}")[None]]))
    a["f1_wi"], a["f1_wo"] = t(g("L1_ffn_W_in")), g("L1_ffn_W_out")
    a["f1_bi"], a["f1_bo"] = f(g("L1_ffn_b_in").reshape(-1, P).T), g("L1_ffn_b_out")
    fill = L3_C * P - g("L3_ffn_w1").shape[2]
    a["f3_router"] = g("L3_ffn_router_w")
    a["f3_wg"] = np.pad(g("L3_ffn_w1"), ((0, 0), (0, 0), (0, fill)))
    a["f3_wu"] = np.pad(g("L3_ffn_w3"), ((0, 0), (0, 0), (0, fill)))
    a["f3_wd"] = np.pad(g("L3_ffn_w2"), ((0, 0), (0, fill), (0, 0)))
    wqkv = g("L2_ffn_Wqkv")
    a["lt_table"] = f(rotary_tables().transpose(1, 0, 2))
    swap = np.concatenate([np.arange(LD // 2, LD), np.arange(LD // 2)])
    q4, k4 = (wqkv[:, :, o:o + LH * LD].reshape(DEPTH, D, PAIRS, 2, LD) for o in (0, LH * LD))
    w4 = np.stack([q4, q4[..., swap], k4, k4[..., swap]], axis=3)
    a["lt_w4"] = f(w4.transpose(0, 2, 1, 3, 4, 5).reshape(DEPTH, PAIRS, D, 4 * P))
    a["lt_wv"] = f(wqkv[:, :, 2 * LH * LD:])
    a["lt_wo"] = g("L2_ffn_Wo")
    qs, ks = g("L2_ffn_q_scale"), g("L2_ffn_k_scale")
    gains = np.stack([qs, qs[:, swap], ks, ks[:, swap]], axis=-1)
    a["lt_qsc"] = f(np.concatenate([gains, gains], axis=1).transpose(1, 0, 2))
    a["lt_g"], a["lt_b"], a["lt_b2"] = t(g("L2_ffn_ln_g")), t(g("L2_ffn_ln_b")), t(g("L2_ffn_b2"))
    inner = g("L2_ffn_W2").shape[1]
    fill = FC * P - inner
    w1 = np.pad(g("L2_ffn_W1").reshape(DEPTH, D, 2, inner), ((0, 0), (0, 0), (0, 0), (0, fill)))
    a["lt_w1"] = f(w1.reshape(DEPTH, D, 2 * FC * P))
    b1 = np.pad(g("L2_ffn_b1").reshape(DEPTH, 2, inner), ((0, 0), (0, 0), (0, fill)))
    a["lt_b1"] = f(b1.reshape(DEPTH, 2, FC, P).transpose(3, 0, 1, 2))
    a["lt_w2"] = np.pad(g("L2_ffn_W2"), ((0, 0), (0, fill), (0, 0)))
    a["lt_head_ones"] = np.kron(np.eye(2), np.ones((LD, LD))).astype(np.float32)
    a["lt_mean_ones"] = np.full((P, P), 1.0 / D, np.float32)
    return a


def kernel(**inputs):
    import concourse.bacc as bacc
    from concourse.bass_utils import run_bass_kernel_spmd

    nc = bacc.Bacc("TRN2", target_bir_lowering=False, num_devices=1)
    arrays, args = {}, {}
    for name, array in host_layout(inputs).items():
        arrays[f"in_{name}"] = array
        args[name] = nc.dram_tensor(f"in_{name}", array.shape, mybir.dt.from_np(array.dtype), kind="ExternalInput").ap()
    out = nc.dram_tensor("out_dram", (1, N, D), F32, kind="ExternalOutput").ap()
    program(nc, args, out)
    result = run_bass_kernel_spmd(nc, [arrays], core_ids=[0])
    return result.results[0]["out_dram"]
```
